# Optimizing a Trainium2 kernel written in Bass

```python
import numpy as np
import jax
import jax.numpy as jnp

def _softmax(x, axis=-1):
    return jax.nn.softmax(x, axis=axis)

def _gelu(x):
    return jax.nn.gelu(x, approximate=True)

def _silu(x):
    return jax.nn.silu(x)

def _sigmoid(x):
    return jax.nn.sigmoid(x)

def _layernorm(x, axis=-1, eps=1e-05):
    m = jnp.mean(x, axis=axis, keepdims=True)
    v = jnp.var(x, axis=axis, keepdims=True)
    return (x - m) / jnp.sqrt(v + eps)

def _scatter_add(tgt, idx, src, axis=0):
    return tgt.at[idx].add(src)

def _segment_sum(src, seg, n):
    return jax.ops.segment_sum(src, seg, n)
kernel_name = 'mk_prb_d1_jaxref_r4_564115'

def setup_inputs(seed: int=0):
    np.random.seed(seed)
    _w = jnp.asarray

    def _L0_attn_setup():
        import jax, jax.numpy as jnp
        import numpy as np
        B, S, D, H, W, FFN = (2, 1024, 256, 16, 64, 1024)
        HD = D // H

        def layer_norm(x, g, b):
            mu = x.mean(-1, keepdims=True)
            var = ((x - mu) ** 2).mean(-1, keepdims=True)
            return (x - mu) * jax.lax.rsqrt(var + 1e-05) * g + b

        def sliding_window_attn(x, Wq, bq, Wk, bk, Wv, bv, Wo, bo):
            b, s, d = x.shape
            nb = s // W
            q = (x @ Wq + bq).reshape(b, nb, W, H, HD)
            k = (x @ Wk + bk).reshape(b, nb, W, H, HD)
            v = (x @ Wv + bv).reshape(b, nb, W, H, HD)
            pad = [(0, 0), (1, 1), (0, 0), (0, 0), (0, 0)]
            kp, vp = (jnp.pad(k, pad), jnp.pad(v, pad))
            kc = jnp.concatenate([kp[:, :-2], kp[:, 1:-1], kp[:, 2:]], axis=2)
            vc = jnp.concatenate([vp[:, :-2], vp[:, 1:-1], vp[:, 2:]], axis=2)
            scale = jnp.asarray(1.0 / np.sqrt(HD), x.dtype)
            scores = jnp.einsum('bnqhd,bnkhd->bhnqk', q, kc) * scale
            i = jnp.arange(W)[:, None]
            j = jnp.arange(3 * W)[None, :]
            band = jnp.abs(i + W - j) <= W
            kidx = jnp.arange(nb)[:, None] * W - W + jnp.arange(3 * W)[None, :]
            valid = (kidx >= 0) & (kidx < s)
            mask = band[None, :, :] & valid[:, None, :]
            scores = jnp.where(mask[None, None], scores, jnp.asarray(-1000000000.0, x.dtype))
            attn = jax.nn.softmax(scores, axis=-1)
            out = jnp.einsum('bhnqk,bnkhd->bnqhd', attn, vc).reshape(b, s, d)
            return out @ Wo + bo
        key = jax.random.key(seed)
        ks = jax.random.split(key, 16)
        s = 1.0 / np.sqrt(D)
        inp = {'x': jax.random.normal(ks[0], (B, S, D), jnp.float32), 'Wq': jax.random.normal(ks[1], (D, D), jnp.float32) * s, 'bq': jnp.zeros((D,), jnp.float32), 'Wk': jax.random.normal(ks[2], (D, D), jnp.float32) * s, 'bk': jnp.zeros((D,), jnp.float32), 'Wv': jax.random.normal(ks[3], (D, D), jnp.float32) * s, 'bv': jnp.zeros((D,), jnp.float32), 'Wo': jax.random.normal(ks[4], (D, D), jnp.float32) * s, 'bo': jnp.zeros((D,), jnp.float32), 'g1': jnp.ones((D,), jnp.float32), 'b1': jnp.zeros((D,), jnp.float32), 'W1': jax.random.normal(ks[5], (D, FFN), jnp.float32) * s, 'c1': jnp.zeros((FFN,), jnp.float32), 'W2': jax.random.normal(ks[6], (FFN, D), jnp.float32) * (1.0 / np.sqrt(FFN)), 'c2': jnp.zeros((D,), jnp.float32), 'g2': jnp.ones((D,), jnp.float32), 'b2': jnp.zeros((D,), jnp.float32)}
        return inp
    _L0_attn_in = _L0_attn_setup()

    def _L0_ffn_setup():
        import jax, jax.numpy as jnp
        import numpy as np
        B, S, H, E = (2, 2048, 256, 8)
        SCALE = 0.5
        key = jax.random.key(seed)
        k1, k2 = jax.random.split(key)
        x = jax.random.normal(k1, (B, S, H), dtype=jnp.float32)
        gate_w = jax.random.normal(k2, (E, H), dtype=jnp.float32) * 0.02
        coeff = SCALE * (1.0 + 0.05 * jnp.arange(E, dtype=jnp.float32))
        expert_w = coeff[:, None, None] * jnp.eye(H, dtype=jnp.float32)
        return {'x': x, 'gate_w': gate_w, 'expert_w': expert_w}
    _L0_ffn_in = _L0_ffn_setup()
    _d = {'L0_attn_x': _L0_attn_in['x'], 'L0_attn_Wq': _L0_attn_in['Wq'], 'L0_attn_bq': _L0_attn_in['bq'], 'L0_attn_Wk': _L0_attn_in['Wk'], 'L0_attn_bk': _L0_attn_in['bk'], 'L0_attn_Wv': _L0_attn_in['Wv'], 'L0_attn_bv': _L0_attn_in['bv'], 'L0_attn_Wo': _L0_attn_in['Wo'], 'L0_attn_bo': _L0_attn_in['bo'], 'L0_attn_g1': _L0_attn_in['g1'], 'L0_attn_b1': _L0_attn_in['b1'], 'L0_attn_W1': _L0_attn_in['W1'], 'L0_attn_c1': _L0_attn_in['c1'], 'L0_attn_W2': _L0_attn_in['W2'], 'L0_attn_c2': _L0_attn_in['c2'], 'L0_attn_g2': _L0_attn_in['g2'], 'L0_attn_b2': _L0_attn_in['b2'], 'L0_ffn_gate_w': _L0_ffn_in['gate_w'], 'L0_ffn_expert_w': _L0_ffn_in['expert_w']}
    _x0 = _d['L0_attn_x']
    _d['L0_attn_x'] = jax.random.normal(jax.random.fold_in(jax.random.key(seed), 1), (8, 1024, 256), dtype=_x0.dtype)
    del _x0
    return _d

def reference(L0_attn_x, L0_attn_Wq, L0_attn_bq, L0_attn_Wk, L0_attn_bk, L0_attn_Wv, L0_attn_bv, L0_attn_Wo, L0_attn_bo, L0_attn_g1, L0_attn_b1, L0_attn_W1, L0_attn_c1, L0_attn_W2, L0_attn_c2, L0_attn_g2, L0_attn_b2, L0_ffn_gate_w, L0_ffn_expert_w):

    def _L0_attn_ref(x, Wq, bq, Wk, bk, Wv, bv, Wo, bo, g1, b1, W1, c1, W2, c2, g2, b2):
        import jax, jax.numpy as jnp
        import numpy as np
        B, S, D, H, W, FFN = (2, 1024, 256, 16, 64, 1024)
        HD = D // H

        def layer_norm(x, g, b):
            mu = x.mean(-1, keepdims=True)
            var = ((x - mu) ** 2).mean(-1, keepdims=True)
            return (x - mu) * jax.lax.rsqrt(var + 1e-05) * g + b

        def sliding_window_attn(x, Wq, bq, Wk, bk, Wv, bv, Wo, bo):
            b, s, d = x.shape
            nb = s // W
            q = (x @ Wq + bq).reshape(b, nb, W, H, HD)
            k = (x @ Wk + bk).reshape(b, nb, W, H, HD)
            v = (x @ Wv + bv).reshape(b, nb, W, H, HD)
            pad = [(0, 0), (1, 1), (0, 0), (0, 0), (0, 0)]
            kp, vp = (jnp.pad(k, pad), jnp.pad(v, pad))
            kc = jnp.concatenate([kp[:, :-2], kp[:, 1:-1], kp[:, 2:]], axis=2)
            vc = jnp.concatenate([vp[:, :-2], vp[:, 1:-1], vp[:, 2:]], axis=2)
            scale = jnp.asarray(1.0 / np.sqrt(HD), x.dtype)
            scores = jnp.einsum('bnqhd,bnkhd->bhnqk', q, kc) * scale
            i = jnp.arange(W)[:, None]
            j = jnp.arange(3 * W)[None, :]
            band = jnp.abs(i + W - j) <= W
            kidx = jnp.arange(nb)[:, None] * W - W + jnp.arange(3 * W)[None, :]
            valid = (kidx >= 0) & (kidx < s)
            mask = band[None, :, :] & valid[:, None, :]
            scores = jnp.where(mask[None, None], scores, jnp.asarray(-1000000000.0, x.dtype))
            attn = jax.nn.softmax(scores, axis=-1)
            out = jnp.einsum('bhnqk,bnkhd->bnqhd', attn, vc).reshape(b, s, d)
            return out @ Wo + bo
        a = sliding_window_attn(x, Wq, bq, Wk, bk, Wv, bv, Wo, bo)
        h = layer_norm(a + x, g1, b1)
        f = jax.nn.gelu(h @ W1 + c1) @ W2 + c2
        return layer_norm(f + h, g2, b2)

    def _L0_ffn_ref(x, gate_w, expert_w):
        import jax, jax.numpy as jnp
        import numpy as np
        B, S, H, E = (2, 2048, 256, 8)
        SCALE = 0.5
        scores = jnp.einsum('bsh,eh->bse', x, gate_w)
        chosen = jnp.argmax(scores, axis=-1)
        onehot = jax.nn.one_hot(chosen, gate_w.shape[0], dtype=x.dtype)
        expert_out = jnp.einsum('bsh,efh->bsef', x, expert_w)
        return x + jnp.einsum('bsef,bse->bsf', expert_out, onehot)
    x = L0_attn_x
    xn = _layernorm(x, axis=-1)
    x = x + _L0_attn_ref(xn, L0_attn_Wq, L0_attn_bq, L0_attn_Wk, L0_attn_bk, L0_attn_Wv, L0_attn_bv, L0_attn_Wo, L0_attn_bo, L0_attn_g1, L0_attn_b1, L0_attn_W1, L0_attn_c1, L0_attn_W2, L0_attn_c2, L0_attn_g2, L0_attn_b2) + _L0_ffn_ref(xn, L0_ffn_gate_w, L0_ffn_expert_w)
    return x

_drawn_inputs = setup_inputs


def setup_inputs(seed=0):
    import zlib

    import numpy as np

    out = dict(_drawn_inputs(seed))
    spreads = {'L0_attn_bq': (0.0, 0.8),
     'L0_attn_bk': (0.0, 2.0),
     'L0_attn_bv': (0.0, 0.294),
     'L0_attn_bo': (0.0, 0.284),
     'L0_attn_g1': (1.0, 0.2),
     'L0_attn_b1': (0.0, 0.294),
     'L0_attn_c1': (0.0, 0.524),
     'L0_attn_c2': (0.0, 0.369),
     'L0_attn_g2': (1.0, 0.2),
     'L0_attn_b2': (0.0, 0.1)}
    factors = {'L0_ffn_gate_w': 11.107}
    for name, (base, spread) in spreads.items():
        noise = np.random.default_rng([zlib.crc32(name.encode()), seed]).standard_normal(out[name].shape)
        drawn = base * np.exp(spread * noise) if base else spread * noise
        out[name] = jnp.asarray(drawn.astype(out[name].dtype))
    for name, factor in factors.items():
        out[name] = (out[name] * factor).astype(out[name].dtype)
    return out
```

```python
from contextlib import ExitStack

import concourse.bass as bass
from concourse import mybir
from concourse.alu_op_type import AluOpType as ALU

ACT = mybir.ActivationFunctionType
F32 = mybir.dt.float32
F16 = mybir.dt.float16
BF16 = mybir.dt.bfloat16
AX = mybir.AxisListType

P = 128
W = 64
HD = 16
WS = 16.0
KONE = 256.0
NEG = -1.0e30
EPS = 1e-5
LEAD = 16
MAX_AT = 1
LAG = 2


class Count:

    def __init__(self, sem, per, credit=0):
        self.sem, self.per, self.credit = sem, per, credit

    def at(self, b, k):
        return b * self.per + (k + self.credit)


def build(nc, x, Wq, bq_c, Wk, bk_c, Wv, bv, Wo, bo, g1_c, b1, W1, c1_c, W2, c2, g2, b2, gateT, expT, b1_c, out):
    NB, S, D = x.shape
    F = W1.shape[1]
    E = gateT.shape[1]
    H = D // HD
    T = S // P
    DC = D // P
    FC = F // P
    HALF = S // 2
    TH = T // 2
    G = H // 4
    STEPS = G * T
    WIN = 3 * W
    QW = 4 * W
    EXP_SCALE = HD ** -0.5 / (WS * WS)
    VW = 32

    x_v = x.rearrange("b (t p) d -> b p t d", p=P)
    out_v = out.rearrange("b (t p) d -> b p t d", p=P)
    res_dram = nc.dram_tensor("res_dram", (NB, P, T, D), F32, kind="Internal").ap()

    pair_dram = nc.dram_tensor("pair_dram", (2, 4, P, S), F16, kind="Internal").ap()
    max_dram = nc.dram_tensor("max_dram", (G, 4, S), F16, kind="Internal").ap()

    with ExitStack() as ctx:
        def sb(name, shape, dt):
            return ctx.enter_context(nc.sbuf_tensor(name, shape, dt))

        def count(name, per, credit=0):
            return Count(ctx.enter_context(nc.semaphore(name)), per, credit)

        ident = sb("ident", [P, P], F32)
        mask = sb("mask", [P, 3, WIN], BF16)
        ones16 = sb("ones16", [P, P], F16)
        wqk_h, wqk_l = sb("wqk_h", [P, DC, 2 * D], F16), sb("wqk_l", [P, DC, 2 * D], F16)
        wvg_h, wvg_l = sb("wvg_h", [P, DC, D + E], F16), sb("wvg_l", [P, DC, D + E], F16)
        wo = sb("wo", [P, DC, D], F32)
        w1_h, w1_l = sb("w1_h", [P, DC, F], F16), sb("w1_l", [P, DC, F], F16)
        w2_h, w2_l = sb("w2_h", [P, FC, D], F16), sb("w2_l", [P, FC, D], F16)
        ex_h, ex_l = sb("ex_h", [P, DC, E, D], F16), sb("ex_l", [P, DC, E, D], F16)
        dg_h, dg_l = sb("dg_h", [P, DC, P], F16), sb("dg_l", [P, DC, P], F16)
        rowb = sb("rowb", [P, D], F16)
        bqk = sb("bqk", [P, 4], F32)
        cols = sb("cols", [P, 2, DC], F32)
        c1c = sb("c1c", [P, FC], F32)
        bc = sb("bc", [P, 4, D], F32)
        iota8 = sb("iota8", [P, E], F32)
        neghalf = sb("neghalf", [P, T], F32)
        x_sb = sb("x_sb", [P, T, D], F32)
        xn = sb("xn", [P, T, D], F32)
        xnbo = sb("xnbo", [P, T, D], F32)
        res_r = sb("res_r", [P, T, D], F32)
        tr_h, tr_l = sb("tr_h", [P, DC, S], F16), sb("tr_l", [P, DC, S], F16)
        pool1 = sb("pool1", [P, 2, 4, S], F16)
        pool0 = sb("pool0", [P, 2, 8, HALF], F16)
        pool2 = sb("pool2", [P, 3 * 4 * QW], F32)
        q_s = sb("q_s", [P, H, S + 2 * W], F16)
        k_s = sb("k_s", [P, H // 2, S + 2 * W], F16)
        v_a = sb("v_a", [P, T, H, VW], F32)
        m_sb = sb("m_sb", [P, H, T], F32)
        mT = sb("mT", [4 * T, G, P], F16)
        sc = sb("sc", [P, T, E], F32)
        oh = sb("oh", [P, T, E], F32)
        oh2 = sb("oh2", [P, T, E], F32)
        mx8 = sb("mx8", [P, 2, T], F32)
        rec = sb("rec", [P, T, H], F32)
        st = sb("st", [P, 3, T, 6], F32)
        mv = sb("mv", [P, 3, T, 2], F32)
        ve = sb("ve", [P, 3, T], F32)
        rs = sb("rs", [P, 3, T], F32)
        nm = sb("nm", [P, 2, T], F32)
        ftmp = sb("ftmp", [P, 2, D], F32)

        qk_h, qk_l = pool1[:, 0], pool1[:, 1]
        gH = [pool0[:, 0], pool1[:, 0].rearrange("p a (c t) -> p (a c) t", c=2)]
        gL = [pool0[:, 1], pool1[:, 1].rearrange("p a (c t) -> p (a c) t", c=2)]
        oT = pool0[:, :, :, :].rearrange("p a c t -> p (a c t)").bitcast(F32).rearrange("p (g t) -> p g t", g=G)
        prob = pool2[:, :].rearrange("p (s h q) -> p s h q", s=3, h=4)
        n1 = pool2[:, 0:T * D].rearrange("p (t d) -> p t d", t=T)
        g32 = pool2[:, T * D:T * D + 2 * HALF].rearrange("p (s t) -> p s t", s=2)
        stage = pool2[:, :]
        rows = stage[:, 1560:1560 + 2 * D].rearrange("p (a d) -> p a d", a=2)
        attn = g32[:, 0, :].rearrange("p (s d) -> p s d", s=2)
        aT = g32[:, 1, :].rearrange("p (s c q) -> p s c q", s=2, c=DC)

        bank = [ctx.enter_context(nc.psum_tensor(f"bank{i}", [P, 512], F32)) for i in range(8)]
        SB, TB, OB, MB = bank[0:2], bank[2:4], bank[4:6], bank[6:8]

        QB = TB + MB

        wa_in, wb_in = count("wa_in", 0), count("wb_in", 0)
        prep_hi = count("prep_hi", 0)
        prep = count("prep", 0)
        pprep = count("pprep", 0)
        prep_mm = count("prep_mm", 0)
        x_in = count("x_in", 16)
        bn0, ag0, ve0, rs0, nm0 = (count(n, k) for n, k in (("bn0", T), ("ag0", T), ("ve0", 1), ("rs0", 1), ("nm0", 1)))
        xn_rdy = count("xn_rdy", T)
        xT_ps, xT_h, xT_l = count("xT_ps", 4), count("xT_h", 4), count("xT_l", 4)
        qk_ps, qk_hi, qk_lo = count("qk_ps", 8), count("qk_hi", 8), count("qk_lo", 8)
        v_ps, v_ev = count("v_ps", T), count("v_ev", 2 * T)
        onehot = count("onehot", 6)
        res_p = count("res_p", 3)
        ex_ps, ex_ev = count("ex_ps", T * E // 2), count("ex_ev", T * E)
        NSTACK = 2 * 2 * 3 + 2
        stack = count("stack", 16 * NSTACK)
        pair_st = count("pair_st", 16 * 4)
        res_st, res_in, out_st = count("res_st", 16), count("res_in", 16), count("out_st", 16, credit=1)
        S_ps, mx = count("S_ps", 2 * STEPS), count("mx", 2 * STEPS)
        mT_ps, mT_ev, mrow = count("mT_ps", G), count("mT_ev", G), count("mrow", 32 * G)
        mx_st = count("mx_st", 16 * G)
        ST_ps, ex_done, masked, pv = (count(n, k) for n, k in (("ST_ps", 2 * STEPS), ("exp_done", 2 * STEPS), ("masked", 2 * STEPS), ("pv", STEPS)))
        oT_ev = count("oT_ev", 2 * G)
        t1_ps, rc, att, t2_ps, aT_ev, wo_ps = (count(n, T) for n in ("t1_ps", "rc", "att", "t2_ps", "aT_ev", "wo_ps"))
        r1, bn1, ag1, ve1, rs1, nm1, n1_rdy = (count(n, k) for n, k in (("r1", T), ("bn1", T), ("ag1", T), ("ve1", 1), ("rs1", 1), ("nm1", 1), ("n1_rdy", T)))
        nT_ps, nT_h, nT_l = count("nT_ps", 4), count("nT_h", 4), count("nT_l", 4)
        u_ps, gel, g_hi, g_lo = (count(n, 2 * FC) for n in ("u_ps", "gel", "g_hi", "g_lo"))
        f_ps, bn2, ag2, ve2, rs2, f1 = (count(n, T) for n in ("f_ps", "bn2", "ag2", "ve2", "rs2", "f1"))
        f2 = count("f2", T, credit=1)
        passed = ctx.enter_context(nc.semaphore("passed"))

        block = ctx.enter_context(nc.Block())

        def wcols(k, w):
            return stage[:, k:k + w]

        SQK = wcols(0, 2 * DC * D).rearrange("p (w c d) -> p w c d", w=2, c=DC)
        SVG = wcols(1024, DC * (D + E)).rearrange("p (c d) -> p c d", c=DC)
        SW = pool0[:, :, :, :].rearrange("p a c t -> p (a c t)").bitcast(F32)
        SW1 = SW[:, 0:DC * F].rearrange("p (c f) -> p c f", c=DC)
        SW2 = SW[:, DC * F:DC * F + FC * D].rearrange("p (c d) -> p c d", c=FC)
        SEX = [t[:, :, :].rearrange("p t d -> p (t d)").rearrange("p (e d) -> p e d", e=E) for t in (res_r, xnbo)]

        @block.sync
        def _(sp):
            def c_in(src, p=P):
                return src.rearrange("(c p) d -> p c d", p=p)

            def load_weights_a():
                for dst, src in (
                    (SQK[:, 0], c_in(Wq)), (SQK[:, 1], c_in(Wk)), (SVG[:, :, 0:D], c_in(Wv)),
                    (SVG[:, :, D:D + E], c_in(gateT)), (bqk[:, 0:2], bq_c), (bqk[:, 2:4], bk_c),
                    (bc[:, 1], bv.partition_broadcast(P)), (bc[:, 3], b2.partition_broadcast(P)),
                ):
                    sp.dma_start(dst, src).then_inc(wa_in.sem, 16)

            def load_weights_b():
                for dst, src in (
                    (SEX[0], expT[:, 0:P, :].rearrange("e p f -> p e f")),
                    (SEX[1], expT[:, P:D, :].rearrange("e p f -> p e f")),
                    (SW1, c_in(W1)), (SW2, c_in(W2)), (wo[:, :, :], c_in(Wo)),
                    (cols[:, 0], g1_c), (cols[:, 1], b1_c), (c1c[:, :], c1_c),
                    (bc[:, 0], bo.partition_broadcast(P)), (bc[:, 2], g2.partition_broadcast(P)),
                    (rows[:, 0], c2.partition_broadcast(P)), (rows[:, 1], b1.partition_broadcast(P)),
                ):
                    sp.dma_start(dst, src).then_inc(wb_in.sem, 16)

            def load_x(b, first=False):
                if not first:
                    sp.wait_ge(res_st.sem, res_st.at(b, 0))
                sp.dma_start(x_sb[:, :, :], x_v[b]).then_inc(x_in.sem, 16)

            def stacks(b):
                for qk in range(2):
                    for half, (src, done) in enumerate(((qk_h, qk_hi), (qk_l, qk_lo))):
                        sp.wait_ge(done.sem, done.at(b, 4 * qk + 4))
                        sp.dma_start(pair_dram[half, 2 * qk:2 * qk + 2].rearrange("o p s -> p o s"),
                                     src[:, 2 * qk:2 * qk + 2, :]).then_inc(pair_st.sem, 16)
                    sp.wait_ge(pair_st.sem, pair_st.at(b, 32 * (qk + 1)))
                    for a in range(2):
                        for slot in range(3):
                            low = slot == (1 if qk else 2)
                            src = pair_dram[int(low), 2 * qk:2 * qk + 2].rearrange("c (j a d) s -> a d (c j) s", a=2, d=HD)[a]
                            r = W * a + HD * slot
                            dst = k_s[r:r + HD, :, W:W + S] if qk else q_s[r:r + HD, a:H:2, W:W + S]
                            sp.dma_start(dst, src).then_inc(stack.sem, 16)
                for a in range(2):
                    r = W * a + 3 * HD
                    sp.dma_start(q_s[r:r + 1, a:H:2, W:W + S], q_s[r:r + 1, 1 - a:H:2, W:W + S]).then_inc(stack.sem, 16)

            def store_res(b):
                sp.wait_ge(ex_ev.sem, ex_ev.at(b, T * E))
                sp.dma_start(res_dram[b], x_sb[:, :, :]).then_inc(res_st.sem, 16)

            def load_res(b):
                sp.wait_ge(res_st.sem, res_st.at(b, 16))
                sp.sem_inc(passed, 1)
                sp.wait_ge(out_st.sem, out_st.at(b, 0))
                sp.dma_start(res_r[:, :, :], res_dram[b]).then_inc(res_in.sem, 16)

            def max_rows(b, g):
                sp.wait_ge(mT_ev.sem, mT_ev.at(b, g + 1))
                sp.dma_start(max_dram[g].rearrange("h (t c) -> (h t) c", t=T), mT[:, g, :]).then_inc(mx_st.sem, 16)
                sp.wait_ge(mx_st.sem, mx_st.at(b, 16 * (g + 1)))
                for a in range(2):
                    r = W * a + 3 * HD
                    sp.dma_start(q_s[r:r + 1, 4 * g + a:4 * g + 4:2, W:W + S],
                                 max_dram[g:g + 1, a::2, :]).then_inc(mrow.sem, 16)

            def store_out(b):
                sp.wait_ge(f2.sem, f2.at(b, T))
                sp.dma_start(out_v[b], res_r[:, :, :]).then_inc(out_st.sem, 16)

            def turn(b, last):
                max_rows(b, 1)
                if not last:
                    load_x(b + 1)
                load_res(b)
                for g in range(2, G):
                    max_rows(b, g)
                if not last:
                    stacks(b + 1)
                    store_res(b + 1)
                    max_rows(b + 1, 0)
                store_out(b)

            sp.sem_inc(out_st.sem, out_st.credit)
            load_x(0, first=True)
            load_weights_a()
            load_weights_b()
            sp.wait_ge(pprep.sem, N_PPREP)
            stacks(0)
            store_res(0)
            max_rows(0, 0)
            with sp.Fori(0, NB - 1) as b:
                turn(b, False)
            turn(NB - 1, True)
            sp.wait_ge(out_st.sem, out_st.at(NB - 1, 16))

        @block.gpsimd
        def _(pool):
            done = 0

            def step(ins):
                nonlocal done
                ins.then_inc(pprep.sem, 1)
                done += 1
                pool.wait_ge(pprep.sem, done)

            def rstd(b, i, veps, rsd, t=None):
                if t is None:
                    pool.wait_ge(veps.sem, veps.at(b, 1))
                    nc.gpsimd.tensor_tensor(rs[:, i, :], ve[:, i, :], neghalf[:, :], ALU.pow).then_inc(rsd.sem, 1)
                else:
                    pool.wait_ge(veps.sem, veps.at(b, t + 1))
                    nc.gpsimd.tensor_tensor(rs[:, i, t:t + 1], ve[:, i, t:t + 1], neghalf[:, 0:1],
                                            ALU.pow).then_inc(rsd.sem, 1)

            step(nc.gpsimd.memset(ident[:, :], 0.0))
            step(nc.gpsimd.memset(neghalf[:, :], -0.5))
            step(nc.gpsimd.affine_select(out=ident[:, :], in_=ident[:, :], compare_op=ALU.not_equal, fill=1.0,
                                         base=0, pattern=[[-1, P]], channel_multiplier=1))
            rstd(0, 0, ve0, rs0)
            step(nc.gpsimd.iota(iota8[:, :], pattern=[[1, E]], base=-E, channel_multiplier=0, allow_small_or_imprecise_dtypes=True))
            step(nc.gpsimd.memset(v_a[:, :, :, :], 0.0))
            step(nc.gpsimd.memset(v_a[:, :, :, HD:HD + 1], 1.0))
            assert done == N_PPREP_V
            step(nc.gpsimd.memset(q_s[:, :, :].rearrange("p h s -> p (h s)").bitcast(F32), 0.0))
            step(nc.gpsimd.memset(k_s[:, :, :].rearrange("p h s -> p (h s)").bitcast(F32), 0.0))
            step(nc.gpsimd.memset(mask[:, :, :], 0.0))
            step(nc.gpsimd.memset(ones16[:, :], 1.0))
            step(nc.gpsimd.memset(rowb[:, :], 0.0))
            for r in (3 * HD, W + 3 * HD):
                q = r - HD
                step(nc.gpsimd.affine_select(out=k_s[q:q + 32, :, :], in_=k_s[q:q + 32, :, :], compare_op=ALU.not_equal,
                                             fill=KONE, base=-HD, pattern=[[0, H // 2], [0, S + 2 * W]],
                                             channel_multiplier=1))
            for a in range(2):
                part = mask[W * a:W * a + W, :, :]
                step(nc.gpsimd.affine_select(out=part, in_=part, compare_op=ALU.is_ge, fill=NEG, base=0,
                                             pattern=[[0, 3], [1, WIN]], channel_multiplier=-1))
                step(nc.gpsimd.affine_select(out=part, in_=part, compare_op=ALU.is_ge, fill=NEG, base=2 * W,
                                             pattern=[[0, 3], [-1, WIN]], channel_multiplier=1))
            step(nc.gpsimd.memset(mask[0:W, 0, 0:W], NEG))
            step(nc.gpsimd.memset(mask[W:P, 2, 2 * W:WIN], NEG))
            assert done == N_PPREP

            def band(b, k):
                pool.wait_ge(ex_done.sem, ex_done.at(b, 2 * k + 2))
                pool.sem_inc(passed, 1)
                p = prob[:, k % 3, :, 0:2 * W]
                nc.gpsimd.affine_select(out=p, in_=p, compare_op=ALU.is_ge, fill=0.0, base=0,
                                        pattern=[[0, 4], [1, 2 * W]], channel_multiplier=-1).then_inc(masked.sem, 1)
                p = prob[:, k % 3, :, 2 * W:QW]
                nc.gpsimd.affine_select(out=p, in_=p, compare_op=ALU.is_ge, fill=0.0, base=0,
                                        pattern=[[0, 4], [-1, 2 * W]], channel_multiplier=1).then_inc(masked.sem, 1)

            def residual(b):
                pool.wait_ge(xn_rdy.sem, xn_rdy.at(b, T))
                nc.gpsimd.tensor_tensor(x_sb[:, :, :], x_sb[:, :, :], xn[:, :, :], ALU.add).then_inc(res_p.sem, 1)
                pool.wait_ge(res_p.sem, res_p.at(b, 1))
                nc.gpsimd.tensor_tensor(x_sb[:, :, :], x_sb[:, :, :], bc[:, 3:4, :].broadcast_to([P, T, D]),
                                        ALU.add).then_inc(res_p.sem, 1)

            def residual_attn(b, first=False):
                if not first:
                    pool.wait_ge(r1.sem, r1.at(b, 0))
                nc.gpsimd.tensor_tensor(xnbo[:, :, :], xn[:, :, :], bc[:, 0:1, :].broadcast_to([P, T, D]),
                                        ALU.add).then_inc(res_p.sem, 1)

            def turn(b, last):
                for k in range(STEPS):
                    band(b, k)
                    if k == 19 and not last:
                        rstd(b + 1, 0, ve0, rs0)
                if not last:
                    residual(b + 1)
                rstd(b, 1, ve1, rs1)
                if not last:
                    residual_attn(b + 1)
                for t in range(T):
                    rstd(b, 2, ve2, rs2, t)

            pool.wait_ge(wa_in.sem, 16 * N_WA)
            residual(0)
            pool.wait_ge(wb_in.sem, 16 * N_WB)
            pool.wait_ge(prep.sem, N_PREP_EX)
            residual_attn(0, first=True)
            with pool.Fori(0, NB - 1) as b:
                turn(b, False)
            turn(NB - 1, True)

        @block.vector
        def _(dve):
            done = 0

            def step(ins, wait=False):
                nonlocal done
                ins.then_inc(prep.sem, 1)
                done += 1
                if wait:
                    dve.wait_ge(prep.sem, done)

            def low(hi, lo, src, n):
                dve.wait_ge(prep_hi.sem, n)
                step(nc.vector.scalar_tensor_tensor(out=lo, in0=src, scalar=WS, in1=hi, op0=ALU.mult, op1=ALU.subtract))

            def weights_a():
                dve.wait_ge(wa_in.sem, 16 * N_WA)
                step(nc.vector.tensor_scalar(bqk[:, :], bqk[:, :], WS, None, ALU.mult))
                for c in range(DC):
                    for o in range(2):
                        low(wqk_h[:, c, o * D:o * D + D], wqk_l[:, c, o * D:o * D + D], SQK[:, o, c], 2 * c + o + 1)
                for c in range(DC):
                    low(wvg_h[:, c], wvg_l[:, c], SVG[:, c], 2 * DC + c + 1)
                assert done == N_PREP_A

            def weights_b():
                dve.wait_ge(wb_in.sem, 16 * N_WB)
                dve.wait_ge(prep_mm.sem, 1)
                step(nc.vector.tensor_tensor(c1c[:, :], c1c[:, :], MB[0][:, 0:FC], ALU.add))
                for c in range(DC):
                    step(nc.vector.tensor_scalar(SW1[:, c], SW1[:, c], cols[:, 0, c:c + 1], None, ALU.mult))
                assert done == N_PREP_W1
                for c in range(DC):
                    low(ex_h[:, c], ex_l[:, c], SEX[c], 3 * DC + c + 1)
                assert done == N_PREP_EX

            def weights_c(t):
                low(w2_h[:, t], w2_l[:, t], SW2[:, t], 4 * DC + 1)
                c, w = t // TH, F // TH
                f = slice(t % TH * w, t % TH * w + w)
                low(w1_h[:, c, f], w1_l[:, c, f], SW1[:, c, f], 4 * DC + 2 + c)

            def weights_d():
                dve.wait_ge(pprep.sem, N_PPREP)
                step(nc.vector.tensor_tensor(rows[:, 0], rows[:, 0], rows[:, 1], ALU.add), wait=True)
                step(nc.vector.tensor_scalar(rowb[0:1, :], rows[0:1, 0], WS, None, ALU.mult))
                step(nc.vector.tensor_scalar(rows[32:33, 1], rows[32:33, 0], WS, None, ALU.mult), wait=True)
                step(nc.vector.tensor_copy(rowb[32:33, :], rows[32:33, 1]), wait=True)
                step(nc.vector.tensor_tensor(rowb[32:33, :], rows[32:33, 1], rowb[32:33, :], ALU.subtract))
                for c in range(DC):
                    step(nc.vector.tensor_scalar(ftmp[:, c, 0:P], ident[:, :], cols[:, 0, c:c + 1], None, ALU.mult), wait=True)
                    step(nc.vector.tensor_scalar(dg_h[:, c], ftmp[:, c, 0:P], WS, None, ALU.mult), wait=True)
                    step(nc.vector.scalar_tensor_tensor(out=dg_l[:, c], in0=ftmp[:, c, 0:P], scalar=WS, in1=dg_h[:, c],
                                                        op0=ALU.mult, op1=ALU.subtract))
                assert done == N_PREP, done
                dve.wait_ge(prep.sem, done)

            def bn(b, i, t, src, bnc, k):
                nc.vector.bn_stats(st[:, i, t, :], src).then_inc(bnc.sem, 1)

            def c1_stage(b):
                dve.wait_ge(x_in.sem, x_in.at(b, 16))
                for t in range(T):
                    bn(b, 0, t, x_sb[:, t, :], bn0, t)
                dve.wait_ge(bn0.sem, bn0.at(b, T))
                dve.sem_inc(passed, 1)
                for t in range(T):
                    nc.vector.bn_aggr(mv[:, 0, t, :], st[:, 0, t, :]).then_inc(ag0.sem, 1)
                dve.wait_ge(ag0.sem, ag0.at(b, T))
                nc.vector.tensor_scalar(ve[:, 0, :], mv[:, 0, :, 1], EPS, None, ALU.add).then_inc(ve0.sem, 1)
                dve.wait_ge(rs0.sem, rs0.at(b, 1))
                nc.vector.scalar_tensor_tensor(out=nm[:, 0, :], in0=mv[:, 0, :, 0], scalar=-1.0, in1=rs[:, 0, :],
                                               op0=ALU.mult, op1=ALU.mult).then_inc(nm0.sem, 1)

            def xn_low(b):
                for u in range(4):
                    hf, c = divmod(u, DC)
                    dve.wait_ge(xT_h.sem, xT_h.at(b, u + 1))
                    s = slice(hf * HALF, hf * HALF + HALF)
                    nc.vector.tensor_tensor(tr_l[:, c, s], MB[u % 2][:, :], tr_h[:, c, s], ALU.subtract).then_inc(xT_l.sem, 1)

            def c2_stage(b, first=False):
                if not first:
                    nm1_stage(b - 1)
                for u in range(8):
                    o, hf = divmod(u, 2)
                    dve.wait_ge(qk_hi.sem, qk_hi.at(b, u + 1))
                    s = slice(hf * HALF, hf * HALF + HALF)
                    nc.vector.scalar_tensor_tensor(out=qk_l[:, o, s], in0=QB[u % 4][:, :], scalar=bqk[:, o:o + 1],
                                                   in1=qk_h[:, o, s], op0=ALU.add, op1=ALU.subtract).then_inc(qk_lo.sem, 1)
                for t in range(T):
                    dve.wait_ge(v_ps.sem, v_ps.at(b, t + 1))
                    nc.vector.scalar_tensor_tensor(
                        out=v_a[:, t, :, 0:HD], in0=OB[t % 2][:, 0:D].rearrange("p (h d) -> p h d", h=H),
                        scalar=1.0 / WS, in1=bc[:, 1, :].rearrange("p (h d) -> p h d", h=H),
                        op0=ALU.mult, op1=ALU.add).then_inc(v_ev.sem, 1)
                    nc.vector.tensor_copy(sc[:, t, :], OB[t % 2][:, D:D + E]).then_inc(v_ev.sem, 1)
                dve.wait_ge(v_ev.sem, v_ev.at(b, 2 * T))
                nc.vector.tensor_reduce(mx8[:, 0, :], sc[:, :, :], AX.X, ALU.max).then_inc(onehot.sem, 1)
                dve.wait_ge(onehot.sem, onehot.at(b, 1))
                nc.vector.tensor_tensor(oh[:, :, :], sc[:, :, :], mx8[:, 0, :].unsqueeze(2).broadcast_to([P, T, E]),
                                        ALU.is_ge).then_inc(onehot.sem, 1)
                dve.wait_ge(onehot.sem, onehot.at(b, 2))
                iota_b = iota8[:, :].unsqueeze(1).broadcast_to([P, T, E])
                nc.vector.tensor_tensor(oh2[:, :, :], oh[:, :, :], iota_b, ALU.mult).then_inc(onehot.sem, 1)
                dve.wait_ge(onehot.sem, onehot.at(b, 3))
                nc.vector.tensor_reduce(mx8[:, 1, :], oh2[:, :, :], AX.X, ALU.min).then_inc(onehot.sem, 1)
                dve.wait_ge(onehot.sem, onehot.at(b, 4))
                nc.vector.tensor_tensor(oh[:, :, :], iota_b, mx8[:, 1, :].unsqueeze(2).broadcast_to([P, T, E]),
                                        ALU.is_equal).then_inc(onehot.sem, 1)
                dve.wait_ge(onehot.sem, onehot.at(b, 5))
                nc.vector.tensor_scalar(oh[:, :, :], oh[:, :, :], 1.0 / WS, None, ALU.mult).then_inc(onehot.sem, 1)
                dve.wait_ge(onehot.sem, onehot.at(b, 6))

            def experts(b, first=False):
                dve.wait_ge(res_p.sem, res_p.at(b, 2))
                for u in range(T * E // 2):
                    t, pr = divmod(u, E // 2)
                    dve.wait_ge(ex_ps.sem, ex_ps.at(b, u + 1))
                    for j in range(2):
                        e = 2 * pr + j
                        if e:
                            dve.wait_ge(ex_ev.sem, ex_ev.at(b, 2 * u + j))
                        nc.vector.scalar_tensor_tensor(
                            out=x_sb[:, t, :], in0=TB[u % 2][:, j * D:j * D + D], scalar=oh[:, t, e:e + 1],
                            in1=x_sb[:, t, :], op0=ALU.mult, op1=ALU.add).then_inc(ex_ev.sem, 1)
                    if first and pr == E // 2 - 1:
                        weights_c(t)

            def maxima(b, j):
                g, t = divmod(j, T)
                v = 0 if t == 0 else 2 if t == T - 1 else 1
                for pu in range(2):
                    u = 2 * j + pu
                    dve.wait_ge(S_ps.sem, S_ps.at(b, u + 1))
                    dve.sem_inc(passed, 1)
                    for i in range(2):
                        h = 4 * g + 2 * pu + i
                        ins = nc.vector.tensor_tensor_reduce(
                            out=SB[u % 2][:, i * WIN:i * WIN + WIN], in0=SB[u % 2][:, i * WIN:i * WIN + WIN], in1=mask[:, v, :], scale=1.0,
                            scalar=-3.0e38, op0=ALU.add, op1=ALU.max, accum_out=m_sb[:, h, t:t + 1])
                    ins.then_inc(mx.sem, 1)

            def max_cols(b, g):
                dve.wait_ge(mT_ps.sem, mT_ps.at(b, g + 1))
                nc.vector.tensor_scalar(mT[:, g, :], MB[g % 2][0:4 * T, 0:P], -1.0 / KONE, None,
                                        ALU.mult).then_inc(mT_ev.sem, 1)

            def normalize(b, t):
                dve.wait_ge(t1_ps.sem, t1_ps.at(b, t + 1))
                o = MB[t % 2][:, :].rearrange("p (h w) -> p h w", h=H)
                nc.vector.reciprocal(rec[:, t, :], o[:, :, HD]).then_inc(rc.sem, 1)
                dve.wait_ge(rc.sem, rc.at(b, t + 1))
                if t >= 2:
                    dve.wait_ge(t2_ps.sem, t2_ps.at(b, t - 1))
                nc.vector.tensor_tensor(attn[:, t % 2, :].rearrange("p (h d) -> p h d", h=H), o[:, :, 0:HD],
                                        rec[:, t, :].unsqueeze(2).broadcast_to([P, H, HD]), ALU.mult).then_inc(att.sem, 1)

            def b_sum(b, t):
                dve.wait_ge(wo_ps.sem, wo_ps.at(b, t + 1))
                nc.vector.tensor_tensor(n1[:, t, :], OB[t % 2][:, 0:D], xnbo[:, t, :], ALU.add).then_inc(r1.sem, 1)
                dve.wait_ge(r1.sem, r1.at(b, t + 1))
                bn(b, 1, t, n1[:, t, :], bn1, t)

            def b_stage(b):
                dve.wait_ge(res_p.sem, res_p.at(b, 3))
                dve.sem_inc(passed, 1)
                for s in range(T + 4):
                    if s < T:
                        normalize(b, s)
                    if s >= 4:
                        b_sum(b, s - 4)
                dve.wait_ge(bn1.sem, bn1.at(b, T))
                dve.sem_inc(passed, 1)
                for t in range(T):
                    nc.vector.bn_aggr(mv[:, 1, t, :], st[:, 1, t, :]).then_inc(ag1.sem, 1)
                dve.wait_ge(ag1.sem, ag1.at(b, T))
                nc.vector.tensor_scalar(ve[:, 1, :], mv[:, 1, :, 1], EPS, None, ALU.add).then_inc(ve1.sem, 1)

            def nm1_stage(b):
                dve.wait_ge(rs1.sem, rs1.at(b, 1))
                nc.vector.scalar_tensor_tensor(out=nm[:, 1, :], in0=mv[:, 1, :, 0], scalar=-1.0, in1=rs[:, 1, :],
                                               op0=ALU.mult, op1=ALU.mult).then_inc(nm1.sem, 1)

            def f_stats(b, t):
                dve.wait_ge(f_ps.sem, f_ps.at(b, t + 1))
                bn(b, 2, t, OB[t % 2][:, 0:D], bn2, t)
                dve.wait_ge(bn2.sem, bn2.at(b, t + 1))
                dve.sem_inc(passed, 1)
                nc.vector.bn_aggr(mv[:, 2, t, :], st[:, 2, t, :]).then_inc(ag2.sem, 1)
                dve.wait_ge(ag2.sem, ag2.at(b, t + 1))
                nc.vector.tensor_scalar(ve[:, 2, t:t + 1], mv[:, 2, t, 1:2], EPS * WS * WS, None, ALU.add).then_inc(ve2.sem, 1)

            def f_out(b, t):
                nc.vector.scalar_tensor_tensor(out=ftmp[:, t % 2, :], in0=OB[t % 2][:, 0:D], scalar=mv[:, 2, t, 0:1],
                                               in1=bc[:, 2, :], op0=ALU.subtract, op1=ALU.mult).then_inc(f1.sem, 1)
                dve.wait_ge(f1.sem, f1.at(b, t + 1))
                dve.wait_ge(rs2.sem, rs2.at(b, t + 1))
                nc.vector.scalar_tensor_tensor(out=res_r[:, t, :], in0=ftmp[:, t % 2, :], scalar=rs[:, 2, t:t + 1],
                                               in1=res_r[:, t, :], op0=ALU.mult, op1=ALU.add).then_inc(f2.sem, 1)

            def gelu_low(b, u):
                hf, c = divmod(u, FC)
                dve.wait_ge(g_hi.sem, g_hi.at(b, u + 1))
                nc.vector.tensor_tensor(gL[hf][:, c, :], g32[:, u % 2, :], gH[hf][:, c, :], ALU.subtract).then_inc(g_lo.sem, 1)

            def d_stage(b, last):
                for u in range(4):
                    hf, c = divmod(u, DC)
                    dve.wait_ge(nT_h.sem, nT_h.at(b, u + 1))
                    s = slice(hf * HALF, hf * HALF + HALF)
                    nc.vector.tensor_tensor(tr_l[:, c, s], MB[u % 2][:, :], tr_h[:, c, s], ALU.subtract).then_inc(nT_l.sem, 1)
                for u in range(2 * FC):
                    gelu_low(b, u)
                    if u % 2 and not last:
                        maxima(b + 1, u // 2)
                dve.wait_ge(res_in.sem, res_in.at(b, 16))
                for t in range(T):
                    f_stats(b, t)
                    if not last:
                        if t == 1:
                            max_cols(b + 1, 0)
                        maxima(b + 1, T + t)
                    f_out(b, t)

            def turn(b, last):
                for k in range(STEPS + LAG):
                    if k % T == MAX_AT and k < 3 * T:
                        max_cols(b, k // T + 1)
                    if k + LEAD < STEPS:
                        maxima(b, k + LEAD)
                    if k == 17 and not last:
                        c1_stage(b + 1)
                if not last:
                    xn_low(b + 1)
                b_stage(b)
                if last:
                    nm1_stage(b)
                else:
                    c2_stage(b + 1)
                    experts(b + 1)
                d_stage(b, last)

            c1_stage(0)
            weights_a()
            xn_low(0)
            dve.wait_ge(pprep.sem, N_PPREP_V)
            c2_stage(0, first=True)
            weights_b()
            experts(0, first=True)
            weights_d()
            for j in range(LEAD):
                if j == 10:
                    max_cols(0, 0)
                maxima(0, j)
            with dve.Fori(0, NB - 1) as b:
                turn(b, False)
            turn(NB - 1, True)

        @block.scalar
        def _(act):
            def high(hi, src):
                nc.scalar.activation(hi, src, ACT.Copy, scale=WS).then_inc(prep_hi.sem, 1)

            def weights_a():
                act.wait_ge(wa_in.sem, 16 * N_WA)
                for c in range(DC):
                    for o in range(2):
                        high(wqk_h[:, c, o * D:o * D + D], SQK[:, o, c])
                for c in range(DC):
                    high(wvg_h[:, c], SVG[:, c])

            def weights_b():
                act.wait_ge(wb_in.sem, 16 * N_WB)
                for c in range(DC):
                    high(ex_h[:, c], SEX[c])
                high(w2_h[:, :, :], SW2)
                act.wait_ge(prep.sem, N_PREP_W1)
                for c in range(DC):
                    high(w1_h[:, c], SW1[:, c])

            def norm(b, i, src, dst, rdy, tiles=range(T)):
                for t in tiles:
                    nc.scalar.activation(dst[:, t, :], src[:, t, :], ACT.Identity, bias=nm[:, i, t:t + 1],
                                         scale=rs[:, i, t:t + 1]).then_inc(rdy.sem, 1)

            def xn_tile(b, t, first=False):
                if t == 0:
                    act.wait_ge(nm0.sem, nm0.at(b, 1))
                    act.sem_inc(passed, 1)
                    if not first:
                        act.wait_ge(res_p.sem, res_p.at(b, 0))
                norm(b, 0, x_sb, xn, xn_rdy, (t,))

            def xn_high(b, u):
                hf, c = divmod(u, DC)
                act.wait_ge(xT_ps.sem, xT_ps.at(b, u + 1))
                nc.scalar.activation(tr_h[:, c, hf * HALF:hf * HALF + HALF], MB[u % 2][:, :], ACT.Copy).then_inc(xT_h.sem, 1)

            def c2_stage(b):
                for u in range(8):
                    o, hf = divmod(u, 2)
                    act.wait_ge(qk_ps.sem, qk_ps.at(b, u + 1))
                    nc.scalar.activation(qk_h[:, o, hf * HALF:hf * HALF + HALF], QB[u % 4][:, :], ACT.Identity,
                                         bias=bqk[:, o:o + 1]).then_inc(qk_hi.sem, 1)

            def exps(b, k):
                if k >= 3:
                    act.wait_ge(pv.sem, pv.at(b, k - 2))
                for pu in range(2):
                    u = 2 * k + pu
                    act.wait_ge(ST_ps.sem, ST_ps.at(b, u + 1))
                    nc.scalar.activation(prob[:, k % 3, 2 * pu:2 * pu + 2, :], TB[u % 2][:, :].rearrange("p (h q) -> p h q", h=2),
                                         ACT.Exp, scale=EXP_SCALE).then_inc(ex_done.sem, 1)

            def heads_out(b, g, hf):
                act.wait_ge(pv.sem, pv.at(b, T * g + (5 if hf == 0 else T)))
                nc.scalar.activation(oT[:, g, hf * HALF:hf * HALF + HALF], OB[hf][:, :], ACT.Copy).then_inc(oT_ev.sem, 1)

            def gelu_high(b, u):
                hf, c = divmod(u, FC)
                if u == FC and not isinstance(b, int):
                    act.wait_ge(pair_st.sem, pair_st.at(b + 1, 64))
                act.wait_ge(gel.sem, gel.at(b, u + 1))
                nc.scalar.activation(gH[hf][:, c, :], g32[:, u % 2, :], ACT.Copy).then_inc(g_hi.sem, 1)

            def turn(b, last):
                for k in range(STEPS + LAG):
                    if k < STEPS:
                        exps(b, k)
                    if k >= LAG + 5 and (k - LAG) % T == 5:
                        heads_out(b, (k - LAG) // T, 0)
                    if k > LAG and (k - LAG) % T == 0:
                        heads_out(b, (k - LAG) // T - 1, 1)
                    if STEPS - T <= k < STEPS and not last:
                        xn_tile(b + 1, k - (STEPS - T))
                    if k >= STEPS and not last:
                        for u in (0, 1):
                            xn_high(b + 1, 2 * (k - STEPS) + u)
                heads_out(b, G - 1, 1)
                for t in range(T):
                    act.wait_ge(t2_ps.sem, t2_ps.at(b, t + 1))
                    if t >= 2:
                        act.wait_ge(wo_ps.sem, wo_ps.at(b, t - 1))
                    nc.scalar.activation(aT[:, t % 2, :, :], TB[t % 2][:, 0:DC * P].rearrange("p (c q) -> p c q", c=DC),
                                         ACT.Copy).then_inc(aT_ev.sem, 1)
                if not last:
                    c2_stage(b + 1)
                act.wait_ge(nm1.sem, nm1.at(b, 1))
                norm(b, 1, n1, n1, n1_rdy)
                for u in range(4):
                    hf, c = divmod(u, DC)
                    act.wait_ge(nT_ps.sem, nT_ps.at(b, u + 1))
                    nc.scalar.activation(tr_h[:, c, hf * HALF:hf * HALF + HALF], MB[u % 2][:, :], ACT.Copy).then_inc(nT_h.sem, 1)
                for u in range(2 * FC):
                    c = u % FC
                    if u:
                        gelu_high(b, u - 1)
                    act.wait_ge(u_ps.sem, u_ps.at(b, u + 1))
                    if u >= 2:
                        act.wait_ge(g_lo.sem, g_lo.at(b, u - 1))
                    nc.scalar.activation(g32[:, u % 2, :], TB[u % 2][:, :], ACT.Gelu_apprx_tanh, bias=c1c[:, c:c + 1],
                                         scale=1.0 / WS).then_inc(gel.sem, 1)
                gelu_high(b, 2 * FC - 1)

            weights_a()
            for t in range(T):
                xn_tile(0, t, first=True)
            for u in range(4):
                xn_high(0, u)
            c2_stage(0)
            weights_b()
            act.wait_ge(prep.sem, N_PREP)
            with act.Fori(0, NB - 1) as b:
                turn(b, False)
            turn(NB - 1, True)

        @block.tensor
        def _(pe):
            pe.sem_inc(f2.sem, f2.credit)
            def b1_w1():
                pe.wait_ge(wb_in.sem, 16 * N_WB)
                for f in range(FC):
                    for c in range(DC):
                        mm = nc.tensor.matmul(MB[0][:, f:f + 1], SW1[:, c, f * P:f * P + P], cols[:, 1, c:c + 1],
                                              start=(c == 0), stop=(c == DC - 1))
                mm.then_inc(prep_mm.sem, 1)

            def triple(dst, lh, ll, rh, rl, start, stop):
                n = len(lh)
                for c in range(n):
                    nc.tensor.matmul(dst, lh[c], rh[c], start=start and c == 0, stop=False)
                    nc.tensor.matmul(dst, lh[c], rl[c], start=False, stop=False)
                for c in range(n):
                    mm = nc.tensor.matmul(dst, ll[c], rh[c], start=False, stop=stop and c == n - 1)
                return mm

            def transposes(src, u, ps):
                hf, c = divmod(u, DC)
                for tt in range(TH):
                    mm = nc.tensor.transpose(MB[u % 2][:, tt * P:tt * P + P], src[:, hf * TH + tt, c * P:c * P + P], ident[:, :])
                mm.then_inc(ps.sem, 1)

            def xn_transposes(b, u, first=False):
                pe.wait_ge(xn_rdy.sem, xn_rdy.at(b, TH * (u // DC) + TH))
                if u == 0 and not first:
                    pe.wait_ge(mT_ev.sem, mT_ev.at(b - 1, G))
                if u >= 2:
                    pe.wait_ge(xT_l.sem, xT_l.at(b, u - 1))
                transposes(xn, u, xT_ps)

            def c2_stage(b, first):
                for u in range(8):
                    o, hf = divmod(u, 2)
                    if u == 0:
                        pe.wait_ge(xT_l.sem, xT_l.at(b, 4))
                    if u >= 4:
                        pe.wait_ge(qk_lo.sem, qk_lo.at(b, u - 3))
                    s = slice(hf * HALF, hf * HALF + HALF)
                    f = slice(o * P, o * P + P)
                    mm = triple(QB[u % 4][:, :], [wqk_h[:, c, f] for c in range(DC)], [wqk_l[:, c, f] for c in range(DC)],
                                [tr_h[:, c, s] for c in range(DC)], [tr_l[:, c, s] for c in range(DC)], True, True)
                    mm.then_inc(qk_ps.sem, 1)
                for t in range(T):
                    if t >= 2:
                        pe.wait_ge(v_ev.sem, v_ev.at(b, 2 * (t - 1)))
                    elif not first:
                        pe.wait_ge(r1.sem, r1.at(b - 1, T))
                    s = slice(t * P, t * P + P)
                    mm = triple(OB[t % 2][:, 0:D + E], [tr_h[:, c, s] for c in range(DC)], [tr_l[:, c, s] for c in range(DC)],
                                [wvg_h[:, c] for c in range(DC)], [wvg_l[:, c] for c in range(DC)], True, True)
                    mm.then_inc(v_ps.sem, 1)

            def experts(b, first=False):
                for u in range(T * E // 2):
                    t, pr = divmod(u, E // 2)
                    if u < 2:
                        pe.wait_ge(qk_lo.sem, qk_lo.at(b, 8))
                    else:
                        pe.wait_ge(ex_ev.sem, ex_ev.at(b, 2 * (u - 1)))
                    s = slice(t * P, t * P + P)
                    e = slice(2 * pr, 2 * pr + 2)
                    mm = triple(TB[u % 2][:, :], [tr_h[:, c, s] for c in range(DC)], [tr_l[:, c, s] for c in range(DC)],
                                [ex_h[:, c, e] for c in range(DC)], [ex_l[:, c, e] for c in range(DC)], True, True)
                    mm.then_inc(ex_ps.sem, 1)

            def scores(b, j, first=False, half=None):
                g, t = divmod(j, T)
                if j == 0 and not half:
                    pe.wait_ge(stack.sem, stack.at(b, 16 * NSTACK))
                for pu in range(2) if half is None else (half,):
                    u = 2 * j + pu
                    if not first or u >= 2:
                        pe.wait_ge(mx.sem, mx.at(b, u - 1))
                    for i in range(2):
                        h = 4 * g + 2 * pu + i
                        for bl in range(2):
                            w0 = (2 * t + bl) * W
                            mm = nc.tensor.matmul(SB[u % 2][W * bl:W * bl + W, i * WIN:i * WIN + WIN],
                                                  q_s[:, h, W + w0:2 * W + w0], k_s[:, h // 2, w0:w0 + WIN],
                                                  start=True, stop=True)
                    mm.then_inc(S_ps.sem, 1)

            def max_cols(b, g):
                pe.wait_ge(mx.sem, mx.at(b, 2 * T * (g + 1)))
                nc.tensor.transpose(MB[g % 2][0:4 * T, 0:P], m_sb[:, 4 * g:4 * g + 4, :].rearrange("p h t -> p (h t)"),
                                    ident[:, :]).then_inc(mT_ps.sem, 1)

            def scores_t(b, k, pu):
                g, t = divmod(k, T)
                if t == 0 and pu == 0:
                    pe.wait_ge(mrow.sem, mrow.at(b, 32 * (g + 1)))
                u = 2 * k + pu
                if u >= 2:
                    pe.wait_ge(ex_done.sem, ex_done.at(b, u - 1))
                for i in range(2):
                    h = 4 * g + 2 * pu + i
                    mm = nc.tensor.matmul(TB[u % 2][:, i * QW:i * QW + QW], k_s[:, h // 2, W + t * P:W + t * P + P],
                                          q_s[:, h, t * P:t * P + QW], start=True, stop=True)
                mm.then_inc(ST_ps.sem, 1)

            def values(b, k):
                g, t = divmod(k, T)
                pe.wait_ge(masked.sem, masked.at(b, 2 * k + 2))
                if k == 0:
                    pe.wait_ge(v_ev.sem, v_ev.at(b, 2 * T))
                    pe.wait_ge(f2.sem, f2.at(b, 0))
                if t == 0 and g:
                    pe.wait_ge(oT_ev.sem, oT_ev.at(b, 2 * g - 1))
                if t == TH - 1 and g:
                    pe.wait_ge(oT_ev.sem, oT_ev.at(b, 2 * g))
                lo, hi = max(0, t * P - W), min(S, t * P + P + W)
                for hf in range(2):
                    a, z = max(lo, hf * HALF), min(hi, hf * HALF + HALF)
                    if a >= z:
                        continue
                    first = t == 0 if hf == 0 else t == TH - 1
                    last = t == TH if hf == 0 else t == T - 1
                    for hl in range(4):
                        q0 = a - (t * P - W)
                        mm = nc.tensor.matmul(OB[hf][32 * hl:32 * hl + 32, a - hf * HALF:z - hf * HALF],
                                              v_a[:, t, 4 * g + hl, :], prob[:, k % 3, hl, q0:q0 + z - a],
                                              start=first, stop=last, skip_group_check=True)
                mm.then_inc(pv.sem, 1)

            def b_stage(b, last):
                for s in range(T + 4):
                    if s < T:
                        t = s
                        if t == 0:
                            pe.wait_ge(oT_ev.sem, oT_ev.at(b, 2 * G))
                            if last:
                                pe.wait_ge(mT_ev.sem, mT_ev.at(b, G))
                            else:
                                pe.wait_ge(xT_l.sem, xT_l.at(b + 1, 4))
                        if t >= 2:
                            pe.wait_ge(att.sem, att.at(b, t - 1))
                        for g in range(G):
                            mm = nc.tensor.transpose(MB[t % 2][:, g * P:g * P + P], oT[:, g, t * P:t * P + P], ident[:, :])
                        mm.then_inc(t1_ps.sem, 1)
                    if 2 <= s < T + 2:
                        t = s - 2
                        pe.wait_ge(att.sem, att.at(b, t + 1))
                        if t >= 2:
                            pe.wait_ge(aT_ev.sem, aT_ev.at(b, t - 1))
                        for c in range(DC):
                            mm = nc.tensor.transpose(TB[t % 2][:, c * P:c * P + P], attn[:, t % 2, c * P:c * P + P], ident[:, :])
                        mm.then_inc(t2_ps.sem, 1)
                    if s >= 4:
                        t = s - 4
                        pe.wait_ge(aT_ev.sem, aT_ev.at(b, t + 1))
                        if t >= 2:
                            pe.wait_ge(r1.sem, r1.at(b, t - 1))
                        for c in range(DC):
                            mm = nc.tensor.matmul(OB[t % 2][:, 0:D], aT[:, t % 2, c, :], wo[:, c, :], start=(c == 0), stop=(c == DC - 1))
                        mm.then_inc(wo_ps.sem, 1)

            def w1_unit(b, u, last):
                hf, f = divmod(u, FC)
                pe.wait_ge(nT_l.sem, nT_l.at(b, DC * hf + DC))
                if u >= 2:
                    pe.wait_ge(gel.sem, gel.at(b, u - 1))
                elif not last:
                    pe.wait_ge(ex_ev.sem, ex_ev.at(b + 1, T * E))
                s = slice(hf * HALF, hf * HALF + HALF)
                fs = slice(f * P, f * P + P)
                mm = triple(TB[u % 2][:, :], [w1_h[:, c, fs] for c in range(DC)], [w1_l[:, c, fs] for c in range(DC)],
                            [tr_h[:, c, s] for c in range(DC)], [tr_l[:, c, s] for c in range(DC)], True, True)
                mm.then_inc(u_ps.sem, 1)

            def w2_tile(b, t, last):
                hf = t // TH
                pe.wait_ge(g_lo.sem, g_lo.at(b, FC * (hf + 1)))
                if t >= 2:
                    pe.wait_ge(f1.sem, f1.at(b, t - 1))
                elif not last:
                    pe.wait_ge(v_ev.sem, v_ev.at(b + 1, 2 * T))
                dst = OB[t % 2][:, 0:D]
                nc.tensor.matmul(dst, ones16[:, :], rowb[:, :], start=True, stop=False)
                s = slice(t * P, t * P + P)
                for c in range(DC):
                    triple(OB[t % 2][:, c * P:c * P + P], [tr_h[:, c, s]], [tr_l[:, c, s]], [dg_h[:, c]], [dg_l[:, c]], False, False)
                s = slice(t % TH * P, t % TH * P + P)
                mm = triple(dst, [gH[hf][:, f, s] for f in range(FC)], [gL[hf][:, f, s] for f in range(FC)],
                            [w2_h[:, f] for f in range(FC)], [w2_l[:, f] for f in range(FC)], False, True)
                mm.then_inc(f_ps.sem, 1)

            def d_stage(b, last):
                for u in range(4):
                    pe.wait_ge(n1_rdy.sem, n1_rdy.at(b, TH * (u // DC) + TH))
                    if u >= 2:
                        pe.wait_ge(nT_l.sem, nT_l.at(b, u - 1))
                    elif not last:
                        pe.wait_ge(xT_l.sem, xT_l.at(b + 1, 4))
                    transposes(n1, u, nT_ps)
                for u in range(2 * FC):
                    w1_unit(b, u, last)
                    if u % 2 and not last:
                        scores(b + 1, u // 2)
                for t in range(T):
                    w2_tile(b, t, last)
                    if not last:
                        if t == 1:
                            max_cols(b + 1, 0)
                        scores(b + 1, T + t)

            def turn(b, last):
                for k in range(STEPS + LAG):
                    if k % T == MAX_AT and k < 3 * T:
                        max_cols(b, k // T + 1)
                    for pu in range(2):
                        if k + LEAD < STEPS:
                            scores(b, k + LEAD, half=pu)
                        if k < STEPS:
                            scores_t(b, k, pu)
                    if k >= STEPS and not last:
                        for u in (0, 1):
                            xn_transposes(b + 1, 2 * (k - STEPS) + u)
                    if k >= LAG:
                        values(b, k - LAG)
                b_stage(b, last)
                if not last:
                    c2_stage(b + 1, False)
                    experts(b + 1)
                d_stage(b, last)

            pe.wait_ge(pprep.sem, 3)
            for u in range(4):
                xn_transposes(0, u, first=True)
            pe.wait_ge(prep.sem, N_PREP_A)
            c2_stage(0, True)
            pe.wait_ge(qk_lo.sem, qk_lo.at(0, 8))
            b1_w1()
            pe.wait_ge(prep.sem, N_PREP_EX)
            experts(0)
            pe.wait_ge(prep.sem, N_PREP)
            for j in range(LEAD):
                if j == 10:
                    max_cols(0, 0)
                scores(0, j, first=True)
            with pe.Fori(0, NB - 1) as b:
                turn(b, False)
            turn(NB - 1, True)


N_WA, N_WB = 8, 12
N_PPREP_V, N_PPREP = 6, 19
N_PREP_A, N_PREP_W1, N_PREP_EX, N_PREP = 7, 10, 12, 39

_INS = ["L0_attn_x", "L0_attn_Wq", "L0_attn_bq", "L0_attn_Wk", "L0_attn_bk", "L0_attn_Wv", "L0_attn_bv", "L0_attn_Wo",
        "L0_attn_bo", "L0_attn_g1", "L0_attn_b1", "L0_attn_W1", "L0_attn_c1", "L0_attn_W2", "L0_attn_c2",
        "L0_attn_g2", "L0_attn_b2", "L0_ffn_gate_w", "L0_ffn_expert_w"]


def kernel(**inputs):
    import numpy as _np
    import concourse.bacc as _bacc
    from concourse import mybir as _mybir
    from concourse.bass_utils import run_bass_kernel_spmd as _run

    nc = _bacc.Bacc("TRN2", target_bir_lowering=False, num_devices=1)
    arrays, args = {}, []

    def add(name, a):
        a = _np.ascontiguousarray(a)
        arrays[f"in_{name}"] = a
        args.append(nc.dram_tensor(f"in_{name}", a.shape, _mybir.dt.from_np(a.dtype), kind="ExternalInput").ap())

    for name in _INS:
        a = _np.asarray(inputs[name])
        if name == "L0_ffn_gate_w":
            a = a.T
        if name == "L0_ffn_expert_w":
            a = a.transpose(0, 2, 1)
        if name[8:] in ("bq", "bk", "g1", "c1"):
            a = a.reshape(-1, P).T
        add(name, a)
    add("b1_by_partition", _np.asarray(inputs["L0_attn_b1"]).reshape(-1, P).T)
    shape = inputs["L0_attn_x"].shape
    args.append(nc.dram_tensor("out_0", shape, _mybir.dt.float32, kind="ExternalOutput").ap())
    build(nc, *args)
    r = _run(nc, [arrays], core_ids=[0])
    return r.results[0]["out_0"]
```

```python
from contextlib import ExitStack

import concourse.bass as bass
from concourse import mybir
from concourse.alu_op_type import AluOpType as ALU

ACT = mybir.ActivationFunctionType
F32 = mybir.dt.float32
F16 = mybir.dt.float16
BF16 = mybir.dt.bfloat16
AX = mybir.AxisListType

P = 128
W = 64
HD = 16
WS = 16.0
KONE = 256.0
NEG = -1.0e30
EPS = 1e-5
LEAD = 16
MAX_AT = 1
ROUTE_POS = 9
LAG = 2


class Count:

    def __init__(self, sem, per, credit=0):
        self.sem, self.per, self.credit = sem, per, credit

    def at(self, b, k):
        return b * self.per + (k + self.credit)


def build(nc, x, Wq, bq_c, Wk, bk_c, Wv, bv, Wo, bo, g1_c, b1, W1, c1_c, W2, c2, g2, b2, gateT, expT, b1_c, out):
    NB, S, D = x.shape
    F = W1.shape[1]
    E = gateT.shape[1]
    H = D // HD
    T = S // P
    DC = D // P
    FC = F // P
    HALF = S // 2
    TH = T // 2
    G = H // 4
    STEPS = G * T
    WIN = 3 * W
    QW = 4 * W
    NT = T + E - 1
    RUN = 3
    EXP_SCALE = HD ** -0.5 / (WS * WS)
    VW = 32

    x_v = x.rearrange("b (t p) d -> b p t d", p=P)
    out_v = out.rearrange("b (t p) d -> b p t d", p=P)
    res_dram = nc.dram_tensor("res_dram", (NB, P, T, D), F32, kind="Internal").ap()

    pair_dram = nc.dram_tensor("pair_dram", (2, 4, P, S), F16, kind="Internal").ap()
    xs_dram = nc.dram_tensor("xs_dram", (NT * P, D), F32, kind="Internal").ap()
    ys_dram = nc.dram_tensor("ys_dram", (NT * P, D), F32, kind="Internal").ap()
    max_dram = nc.dram_tensor("max_dram", (G, 4, S), F16, kind="Internal").ap()

    with ExitStack() as ctx:
        def sb(name, shape, dt):
            return ctx.enter_context(nc.sbuf_tensor(name, shape, dt))

        def count(name, per, credit=0):
            return Count(ctx.enter_context(nc.semaphore(name)), per, credit)

        ident = sb("ident", [P, P], F32)
        mask = sb("mask", [P, 3, WIN], BF16)
        ones16 = sb("ones16", [P, P], F16)
        wqk_h, wqk_l = sb("wqk_h", [P, DC, 2 * D], F16), sb("wqk_l", [P, DC, 2 * D], F16)
        wvg_h, wvg_l = sb("wvg_h", [P, DC, D + E], F16), sb("wvg_l", [P, DC, D + E], F16)
        wo = sb("wo", [P, DC, D], F32)
        w1_h, w1_l = sb("w1_h", [P, DC, F], F16), sb("w1_l", [P, DC, F], F16)
        w2_h, w2_l = sb("w2_h", [P, FC, D], F16), sb("w2_l", [P, FC, D], F16)
        ex_h, ex_l = sb("ex_h", [P, DC, E, D], F16), sb("ex_l", [P, DC, E, D], F16)
        dg_h, dg_l = sb("dg_h", [P, DC, P], F16), sb("dg_l", [P, DC, P], F16)
        rowb = sb("rowb", [P, D], F16)
        bqk = sb("bqk", [P, 4], F32)
        cols = sb("cols", [P, 2, DC], F32)
        c1c = sb("c1c", [P, FC], F32)
        bc = sb("bc", [P, 4, D], F32)
        iota8 = sb("iota8", [P, E], F32)
        before = sb("before", [P, P], F16)
        upto = sb("upto", [P, E, E], F32)
        full = sb("full", [P, E], F32)
        tile_no = sb("tile_no", [P, NT], F32)
        neghalf = sb("neghalf", [P, T], F32)
        x_sb = sb("x_sb", [P, T, D], F32)
        xn = sb("xn", [P, T, D], F32)
        xnbo = sb("xnbo", [P, T, D], F32)
        res_r = sb("res_r", [P, T, D], F32)
        tr_h, tr_l = sb("tr_h", [P, DC, S], F16), sb("tr_l", [P, DC, S], F16)
        pool1 = sb("pool1", [P, 2, 4, S], F16)
        pool0 = sb("pool0", [P, 2, 8, HALF], F16)
        pool2 = sb("pool2", [P, 3 * 4 * QW], F32)
        q_s = sb("q_s", [P, H, S + 2 * W], F16)
        k_s = sb("k_s", [P, H // 2, S + 2 * W], F16)
        v_a = sb("v_a", [P, T, H, VW], F32)
        m_sb = sb("m_sb", [P, H, T], F32)
        mT = sb("mT", [4 * T, G, P], F16)
        sc = sb("sc", [P, T, E], F32)
        oh = sb("oh", [P, T, E], F32)
        oh2 = sb("oh2", [P, T, E], F32)
        oh16 = sb("oh16", [P, T + 1, E], F16)
        cnt = sb("cnt", [P, E, E], F32)
        tiles = sb("tiles", [P, 3, E], F32)
        own = sb("own", [P, NT, E - 1], F32)
        posf, pos = sb("posf", [P, T], F32), sb("pos", [P, T], mybir.dt.uint32)
        tef, te = sb("tef", [P, NT], F32), sb("te", [P, NT], mybir.dt.uint32)
        mx8 = sb("mx8", [P, 2, T], F32)
        rec = sb("rec", [P, T, H], F32)
        st = sb("st", [P, 3, T, 6], F32)
        mv = sb("mv", [P, 3, T, 2], F32)
        ve = sb("ve", [P, 3, T], F32)
        rs = sb("rs", [P, 3, T], F32)
        nm = sb("nm", [P, 2, T], F32)

        qk_h, qk_l = pool1[:, 0], pool1[:, 1]
        gH = [pool0[:, 0], pool1[:, 0].rearrange("p a (c t) -> p (a c) t", c=2)]
        gL = [pool0[:, 1], pool1[:, 1].rearrange("p a (c t) -> p (a c) t", c=2)]
        oT = pool0[:, :, :, :].rearrange("p a c t -> p (a c t)").bitcast(F32).rearrange("p (g t) -> p g t", g=G)
        prob = pool2[:, :].rearrange("p (s h q) -> p s h q", s=3, h=4)
        n1 = pool2[:, 0:T * D].rearrange("p (t d) -> p t d", t=T)
        g32 = pool2[:, T * D:T * D + 2 * HALF].rearrange("p (s t) -> p s t", s=2)
        stage = pool2[:, :]
        ftmp = pool2[:, T * D:T * D + 2 * D].rearrange("p (a d) -> p a d", a=2)
        rows = pool2[:, (T + 2) * D:(T + 4) * D].rearrange("p (a d) -> p a d", a=2)
        xs_h, xs_l = (pool2[:, (T + 2 + i) * D:(T + 3 + i) * D].bitcast(F16).rearrange("p (s c q) -> p s c q", s=2, c=DC) for i in range(2))
        xs = xn[:, 0:2 * RUN, :]
        ys = xn[:, 2 * RUN:T, :]
        attn = g32[:, 0, :].rearrange("p (s d) -> p s d", s=2)
        aT = g32[:, 1, :].rearrange("p (s c q) -> p s c q", s=2, c=DC)

        bank = [ctx.enter_context(nc.psum_tensor(f"bank{i}", [P, 512], F32)) for i in range(8)]
        SB, TB, OB, MB = bank[0:2], bank[2:4], bank[4:6], bank[6:8]

        QB = TB + MB

        wa_in, wb_in = count("wa_in", 0), count("wb_in", 0)
        prep_hi = count("prep_hi", 0)
        prep = count("prep", 0)
        pprep = count("pprep", 0)
        prep_mm = count("prep_mm", 0)
        x_in = count("x_in", 16)
        bn0, ag0, ve0, rs0, nm0 = (count(n, k) for n, k in (("bn0", T), ("ag0", T), ("ve0", 1), ("rs0", 1), ("nm0", 1)))
        xn_rdy = count("xn_rdy", T)
        xT_ps, xT_h, xT_l = count("xT_ps", 4), count("xT_h", 4), count("xT_l", 4)
        qk_ps, qk_hi, qk_lo = count("qk_ps", 8), count("qk_hi", 8), count("qk_lo", 8)
        v_ps, v_ev = count("v_ps", T), count("v_ev", 2 * T)
        onehot = count("onehot", 6)
        rank_ps, route = count("rank_ps", 1), count("route", 12)
        scat = count("scat", 16 * T)
        xs_in = [count(f"xs_in{i}", 16 * ((NT // RUN + 1 - i) // 2)) for i in range(2)]
        y_st = [count(f"y_st{i}", 16 * ((NT + 1 - i) // 2)) for i in range(2)]
        xs_ps, xs_hi, xs_lo = count("xs_ps", NT), count("xs_hi", NT), count("xs_lo", NT)
        y_ps, y_ev = count("y_ps", NT), count("y_ev", NT)
        y_in, res_y = count("y_in", 16 * T), count("res_y", 1, credit=1)
        res_p = count("res_p", 3)
        xs_fill = count("xs_fill", 0)
        NSTACK = 2 * 2 * 3 + 2
        stack = count("stack", 16 * NSTACK)
        pair_st = count("pair_st", 16 * 4)
        res_st, res_in, out_st = count("res_st", 16), count("res_in", 16), count("out_st", 16, credit=1)
        S_ps, mx = count("S_ps", 2 * STEPS), count("mx", 2 * STEPS)
        mT_ps, mT_ev, mrow = count("mT_ps", G), count("mT_ev", G), count("mrow", 32 * G)
        mx_st = count("mx_st", 16 * G)
        ST_ps, ex_done, masked, pv = (count(n, k) for n, k in (("ST_ps", 2 * STEPS), ("exp_done", 2 * STEPS), ("masked", 2 * STEPS), ("pv", STEPS)))
        oT_ev = count("oT_ev", 2 * G)
        t1_ps, rc, att, t2_ps, aT_ev, wo_ps = (count(n, T) for n in ("t1_ps", "rc", "att", "t2_ps", "aT_ev", "wo_ps"))
        r1, bn1, ag1, ve1, rs1, nm1, n1_rdy = (count(n, k) for n, k in (("r1", T), ("bn1", T), ("ag1", T), ("ve1", 1), ("rs1", 1), ("nm1", 1), ("n1_rdy", T)))
        nT_ps, nT_h, nT_l = count("nT_ps", 4), count("nT_h", 4), count("nT_l", 4)
        u_ps, gel, g_hi, g_lo = (count(n, 2 * FC) for n in ("u_ps", "gel", "g_hi", "g_lo"))
        f_ps, bn2, ag2, ve2, rs2, f1 = (count(n, T) for n in ("f_ps", "bn2", "ag2", "ve2", "rs2", "f1"))
        f2 = count("f2", T, credit=1)
        passed = ctx.enter_context(nc.semaphore("passed"))

        block = ctx.enter_context(nc.Block())

        def wcols(k, w):
            return stage[:, k:k + w]

        SQK = wcols(0, 2 * DC * D).rearrange("p (w c d) -> p w c d", w=2, c=DC)
        SVG = wcols(1024, DC * (D + E)).rearrange("p (c d) -> p c d", c=DC)
        SW = pool0[:, :, :, :].rearrange("p a c t -> p (a c t)").bitcast(F32)
        SW1 = SW[:, 0:DC * F].rearrange("p (c f) -> p c f", c=DC)
        SW2 = SW[:, DC * F:DC * F + FC * D].rearrange("p (c d) -> p c d", c=FC)
        SEX = [t[:, :, :].rearrange("p t d -> p (t d)").rearrange("p (e d) -> p e d", e=E) for t in (res_r, xnbo)]

        @block.sync
        def _(sp):
            def c_in(src, p=P):
                return src.rearrange("(c p) d -> p c d", p=p)

            def load_weights_a():
                for dst, src in (
                    (SQK[:, 0], c_in(Wq)), (SQK[:, 1], c_in(Wk)), (SVG[:, :, 0:D], c_in(Wv)),
                    (SVG[:, :, D:D + E], c_in(gateT)), (bqk[:, 0:2], bq_c), (bqk[:, 2:4], bk_c),
                    (bc[:, 1], bv.partition_broadcast(P)), (bc[:, 3], b2.partition_broadcast(P)),
                ):
                    sp.dma_start(dst, src).then_inc(wa_in.sem, 16)

            def load_weights_b():
                for dst, src in (
                    (SEX[0], expT[:, 0:P, :].rearrange("e p f -> p e f")),
                    (SEX[1], expT[:, P:D, :].rearrange("e p f -> p e f")),
                    (SW1, c_in(W1)), (SW2, c_in(W2)), (wo[:, :, :], c_in(Wo)),
                    (cols[:, 0], g1_c), (cols[:, 1], b1_c), (c1c[:, :], c1_c),
                    (bc[:, 0], bo.partition_broadcast(P)), (bc[:, 2], g2.partition_broadcast(P)),
                    (rows[:, 0], c2.partition_broadcast(P)), (rows[:, 1], b1.partition_broadcast(P)),
                ):
                    sp.dma_start(dst, src).then_inc(wb_in.sem, 16)

            def load_x(b, first=False):
                if not first:
                    sp.wait_ge(res_st.sem, res_st.at(b, 0))
                    sp.sem_inc(passed, 1)
                    sp.wait_ge(res_y.sem, res_y.at(b - 1, 0))
                sp.dma_start(x_sb[:, :, :], x_v[b]).then_inc(x_in.sem, 16)

            def stacks(b):
                for qk in range(2):
                    for half, (src, done) in enumerate(((qk_h, qk_hi), (qk_l, qk_lo))):
                        sp.wait_ge(done.sem, done.at(b, 4 * qk + 4))
                        sp.dma_start(pair_dram[half, 2 * qk:2 * qk + 2].rearrange("o p s -> p o s"),
                                     src[:, 2 * qk:2 * qk + 2, :]).then_inc(pair_st.sem, 16)
                    sp.wait_ge(pair_st.sem, pair_st.at(b, 32 * (qk + 1)))
                    for a in range(2):
                        for slot in range(3):
                            low = slot == (1 if qk else 2)
                            src = pair_dram[int(low), 2 * qk:2 * qk + 2].rearrange("c (j a d) s -> a d (c j) s", a=2, d=HD)[a]
                            r = W * a + HD * slot
                            dst = k_s[r:r + HD, :, W:W + S] if qk else q_s[r:r + HD, a:H:2, W:W + S]
                            sp.dma_start(dst, src).then_inc(stack.sem, 16)
                for a in range(2):
                    r = W * a + 3 * HD
                    sp.dma_start(q_s[r:r + 1, a:H:2, W:W + S], q_s[r:r + 1, 1 - a:H:2, W:W + S]).then_inc(stack.sem, 16)

            def store_res(b):
                sp.wait_ge(res_p.sem, res_p.at(b, 2))
                sp.dma_start(res_dram[b], x_sb[:, :, :]).then_inc(res_st.sem, 16)

            def load_sorted(b, g):
                if g == 0:
                    sp.wait_ge(scat.sem, scat.at(b, 16 * T))
                    sp.sem_inc(passed, 1)
                    sp.wait_ge(res_p.sem, res_p.at(b, 3))
                if g >= 2:
                    sp.wait_ge(xs_ps.sem, xs_ps.at(b, RUN * (g - 1)))
                sp.dma_start(xs[:, g % 2 * RUN:g % 2 * RUN + RUN, :],
                             xs_dram[g * RUN * P:(g + 1) * RUN * P, :].rearrange("(t p) d -> p t d", p=P)).then_inc(xs_in[g % 2].sem, 16)

            def sorted_tiles(b, rows_too):
                load_sorted(b, 0)
                load_sorted(b, 1)
                for i in range(NT):
                    sp.wait_ge(y_ev.sem, y_ev.at(b, i + 1))
                    sp.dma_start(ys_dram[i * P:i * P + P, :], ys[:, i % 2, :]).then_inc(y_st[i % 2].sem, 16)
                    if i % RUN == RUN - 1 and i // RUN + 2 < NT // RUN:
                        load_sorted(b, i // RUN + 2)
                    if i == 5 and rows_too:
                        max_rows(b, 0)

            def load_res(b):
                sp.wait_ge(res_st.sem, res_st.at(b, 16))
                sp.sem_inc(passed, 1)
                sp.wait_ge(out_st.sem, out_st.at(b, 0))
                sp.dma_start(res_r[:, :, :], res_dram[b]).then_inc(res_in.sem, 16)

            def max_rows(b, g):
                sp.wait_ge(mT_ev.sem, mT_ev.at(b, g + 1))
                sp.dma_start(max_dram[g].rearrange("h (t c) -> (h t) c", t=T), mT[:, g, :]).then_inc(mx_st.sem, 16)
                sp.wait_ge(mx_st.sem, mx_st.at(b, 16 * (g + 1)))
                for a in range(2):
                    r = W * a + 3 * HD
                    sp.dma_start(q_s[r:r + 1, 4 * g + a:4 * g + 4:2, W:W + S],
                                 max_dram[g:g + 1, a::2, :]).then_inc(mrow.sem, 16)

            def store_out(b):
                sp.wait_ge(f2.sem, f2.at(b, T))
                sp.dma_start(out_v[b], res_r[:, :, :]).then_inc(out_st.sem, 16)

            def turn(b, last):
                max_rows(b, 1)
                if not last:
                    load_x(b + 1)
                load_res(b)
                for g in range(2, G):
                    max_rows(b, g)
                if not last:
                    store_res(b + 1)
                    stacks(b + 1)
                    sorted_tiles(b + 1, True)
                store_out(b)

            sp.sem_inc(out_st.sem, out_st.credit)
            sp.sem_inc(res_y.sem, res_y.credit)
            load_x(0, first=True)
            load_weights_a()
            load_weights_b()
            sp.dma_start(xs_dram, x.rearrange("b s d -> (b s) d")[0:NT * P, :]).then_inc(xs_fill.sem, 16)
            sp.wait_ge(pprep.sem, N_PPREP)
            store_res(0)
            stacks(0)
            sorted_tiles(0, False)
            max_rows(0, 0)
            with sp.Fori(0, NB - 1) as b:
                turn(b, False)
            turn(NB - 1, True)
            sp.wait_ge(out_st.sem, out_st.at(NB - 1, 16))

        @block.gpsimd
        def _(pool):
            done = 0

            def step(ins):
                nonlocal done
                ins.then_inc(pprep.sem, 1)
                done += 1
                pool.wait_ge(pprep.sem, done)

            def rstd(b, i, veps, rsd, t=None):
                if t is None:
                    pool.wait_ge(veps.sem, veps.at(b, 1))
                    nc.gpsimd.tensor_tensor(rs[:, i, :], ve[:, i, :], neghalf[:, :], ALU.pow).then_inc(rsd.sem, 1)
                else:
                    pool.wait_ge(veps.sem, veps.at(b, t + 1))
                    nc.gpsimd.tensor_tensor(rs[:, i, t:t + 1], ve[:, i, t:t + 1], neghalf[:, 0:1],
                                            ALU.pow).then_inc(rsd.sem, 1)

            step(nc.gpsimd.memset(ident[:, :], 0.0))
            step(nc.gpsimd.memset(neghalf[:, :], -0.5))
            step(nc.gpsimd.affine_select(out=ident[:, :], in_=ident[:, :], compare_op=ALU.not_equal, fill=1.0,
                                         base=0, pattern=[[-1, P]], channel_multiplier=1))
            rstd(0, 0, ve0, rs0)
            step(nc.gpsimd.iota(iota8[:, :], pattern=[[1, E]], base=-E, channel_multiplier=0, allow_small_or_imprecise_dtypes=True))
            step(nc.gpsimd.memset(v_a[:, :, :, :], 0.0))
            step(nc.gpsimd.memset(v_a[:, :, :, HD:HD + 1], 1.0))
            step(nc.gpsimd.memset(oh16[:, :, :], 0.0))
            assert done == N_PPREP_V
            step(nc.gpsimd.memset(q_s[:, :, :].rearrange("p h s -> p (h s)").bitcast(F32), 0.0))
            step(nc.gpsimd.memset(k_s[:, :, :].rearrange("p h s -> p (h s)").bitcast(F32), 0.0))
            step(nc.gpsimd.memset(mask[:, :, :], 0.0))
            step(nc.gpsimd.memset(ones16[:, :], 1.0))
            step(nc.gpsimd.memset(rowb[:, :], 0.0))
            for r in (3 * HD, W + 3 * HD):
                q = r - HD
                step(nc.gpsimd.affine_select(out=k_s[q:q + 32, :, :], in_=k_s[q:q + 32, :, :], compare_op=ALU.not_equal,
                                             fill=KONE, base=-HD, pattern=[[0, H // 2], [0, S + 2 * W]],
                                             channel_multiplier=1))
            for a in range(2):
                part = mask[W * a:W * a + W, :, :]
                step(nc.gpsimd.affine_select(out=part, in_=part, compare_op=ALU.is_ge, fill=NEG, base=0,
                                             pattern=[[0, 3], [1, WIN]], channel_multiplier=-1))
                step(nc.gpsimd.affine_select(out=part, in_=part, compare_op=ALU.is_ge, fill=NEG, base=2 * W,
                                             pattern=[[0, 3], [-1, WIN]], channel_multiplier=1))
            step(nc.gpsimd.memset(before[:, :], 1.0))
            step(nc.gpsimd.affine_select(out=before[:, :], in_=before[:, :], compare_op=ALU.is_gt, fill=0.0,
                                         base=0, pattern=[[1, P]], channel_multiplier=-1))
            step(nc.gpsimd.memset(upto[:, :, :], 1.0))
            step(nc.gpsimd.affine_select(out=upto[:, :, :], in_=upto[:, :, :], compare_op=ALU.is_ge, fill=0.0,
                                         base=0, pattern=[[1, E], [-1, E]], channel_multiplier=0))
            step(nc.gpsimd.iota(full[:, :], pattern=[[P, E]], base=0, channel_multiplier=0, allow_small_or_imprecise_dtypes=True))
            step(nc.gpsimd.iota(tile_no[:, :], pattern=[[1, NT]], base=0, channel_multiplier=0, allow_small_or_imprecise_dtypes=True))
            step(nc.gpsimd.memset(mask[0:W, 0, 0:W], NEG))
            step(nc.gpsimd.memset(mask[W:P, 2, 2 * W:WIN], NEG))
            assert done == N_PPREP

            def band(b, k):
                pool.wait_ge(ex_done.sem, ex_done.at(b, 2 * k + 2))
                pool.sem_inc(passed, 1)
                p = prob[:, k % 3, :, 0:2 * W]
                nc.gpsimd.affine_select(out=p, in_=p, compare_op=ALU.is_ge, fill=0.0, base=0,
                                        pattern=[[0, 4], [1, 2 * W]], channel_multiplier=-1).then_inc(masked.sem, 1)
                p = prob[:, k % 3, :, 2 * W:QW]
                nc.gpsimd.affine_select(out=p, in_=p, compare_op=ALU.is_ge, fill=0.0, base=0,
                                        pattern=[[0, 4], [-1, 2 * W]], channel_multiplier=1).then_inc(masked.sem, 1)

            def residual(b):
                pool.wait_ge(xn_rdy.sem, xn_rdy.at(b, T))
                nc.gpsimd.tensor_tensor(x_sb[:, :, :], x_sb[:, :, :], xn[:, :, :], ALU.add).then_inc(res_p.sem, 1)
                pool.wait_ge(res_p.sem, res_p.at(b, 1))
                nc.gpsimd.tensor_tensor(x_sb[:, :, :], x_sb[:, :, :], bc[:, 3:4, :].broadcast_to([P, T, D]),
                                        ALU.add).then_inc(res_p.sem, 1)

            def residual_attn(b, first=False):
                if not first:
                    pool.wait_ge(r1.sem, r1.at(b, 0))
                nc.gpsimd.tensor_tensor(xnbo[:, :, :], xn[:, :, :], bc[:, 0:1, :].broadcast_to([P, T, D]),
                                        ALU.add).then_inc(res_p.sem, 1)

            def send(b):
                for t in range(T):
                    if t == 0:
                        pool.wait_ge(route.sem, route.at(b, ROUTE_POS))
                        pool.sem_inc(passed, 1)
                    nc.gpsimd.indirect_dma_start(out=xs_dram[:, :], out_offset=bass.IndirectOffsetOnAxis(ap=pos[:, t:t + 1], axis=0),
                                                 in_=xn[:, t, :], in_offset=None).then_inc(scat.sem, 16)

            def fetch(b, last):
                for sent in y_st:
                    pool.wait_ge(sent.sem, sent.at(b + 1, 0))
                    pool.sem_inc(passed, 1)
                if not last:
                    pool.wait_ge(res_st.sem, res_st.at(b + 1, 16))
                    pool.sem_inc(passed, 1)
                for t in range(T):
                    nc.gpsimd.indirect_dma_start(out=x_sb[:, t, :], out_offset=None, in_=ys_dram[:, :],
                                                 in_offset=bass.IndirectOffsetOnAxis(ap=pos[:, t:t + 1], axis=0)).then_inc(y_in.sem, 16)
                pool.wait_ge(res_in.sem, res_in.at(b, 16))
                pool.sem_inc(passed, 1)
                pool.wait_ge(y_in.sem, y_in.at(b, 16 * T))
                nc.gpsimd.tensor_tensor(res_r[:, :, :], res_r[:, :, :], x_sb[:, :, :], ALU.add).then_inc(res_y.sem, 1)

            def turn(b, last):
                for k in range(STEPS):
                    band(b, k)
                    if k == 19 and not last:
                        rstd(b + 1, 0, ve0, rs0)
                if not last:
                    residual(b + 1)
                rstd(b, 1, ve1, rs1)
                if not last:
                    residual_attn(b + 1)
                fetch(b, last)
                if not last:
                    send(b + 1)
                for t in range(T):
                    rstd(b, 2, ve2, rs2, t)

            pool.wait_ge(wa_in.sem, 16 * N_WA)
            residual(0)
            pool.wait_ge(wb_in.sem, 16 * N_WB)
            pool.wait_ge(prep.sem, N_PREP_EX)
            residual_attn(0, first=True)
            pool.wait_ge(xs_fill.sem, 16)
            send(0)
            with pool.Fori(0, NB - 1) as b:
                turn(b, False)
            turn(NB - 1, True)

        @block.vector
        def _(dve):
            done = 0

            def step(ins, wait=False):
                nonlocal done
                ins.then_inc(prep.sem, 1)
                done += 1
                if wait:
                    dve.wait_ge(prep.sem, done)

            def low(hi, lo, src, n):
                dve.wait_ge(prep_hi.sem, n)
                step(nc.vector.scalar_tensor_tensor(out=lo, in0=src, scalar=WS, in1=hi, op0=ALU.mult, op1=ALU.subtract))

            def weights_a():
                dve.wait_ge(wa_in.sem, 16 * N_WA)
                step(nc.vector.tensor_scalar(bqk[:, :], bqk[:, :], WS, None, ALU.mult))
                for c in range(DC):
                    for o in range(2):
                        low(wqk_h[:, c, o * D:o * D + D], wqk_l[:, c, o * D:o * D + D], SQK[:, o, c], 2 * c + o + 1)
                for c in range(DC):
                    low(wvg_h[:, c], wvg_l[:, c], SVG[:, c], 2 * DC + c + 1)
                assert done == N_PREP_A

            def weights_b():
                dve.wait_ge(wb_in.sem, 16 * N_WB)
                dve.wait_ge(prep_mm.sem, 1)
                step(nc.vector.tensor_tensor(c1c[:, :], c1c[:, :], MB[0][:, 0:FC], ALU.add))
                for c in range(DC):
                    step(nc.vector.tensor_scalar(SW1[:, c], SW1[:, c], cols[:, 0, c:c + 1], None, ALU.mult))
                assert done == N_PREP_W1
                for c in range(DC):
                    low(ex_h[:, c], ex_l[:, c], SEX[c], 3 * DC + c + 1)
                assert done == N_PREP_EX

            def weights_c(t):
                low(w2_h[:, t], w2_l[:, t], SW2[:, t], 4 * DC + 1)
                c, w = t // TH, F // TH
                f = slice(t % TH * w, t % TH * w + w)
                low(w1_h[:, c, f], w1_l[:, c, f], SW1[:, c, f], 4 * DC + 2 + c)

            def weights_d():
                dve.wait_ge(pprep.sem, N_PPREP)
                step(nc.vector.tensor_tensor(rows[:, 0], rows[:, 0], rows[:, 1], ALU.add), wait=True)
                step(nc.vector.tensor_scalar(rowb[0:1, :], rows[0:1, 0], WS, None, ALU.mult))
                step(nc.vector.tensor_scalar(rows[32:33, 1], rows[32:33, 0], WS, None, ALU.mult), wait=True)
                step(nc.vector.tensor_copy(rowb[32:33, :], rows[32:33, 1]), wait=True)
                step(nc.vector.tensor_tensor(rowb[32:33, :], rows[32:33, 1], rowb[32:33, :], ALU.subtract))
                for c in range(DC):
                    step(nc.vector.tensor_scalar(ftmp[:, c, 0:P], ident[:, :], cols[:, 0, c:c + 1], None, ALU.mult), wait=True)
                    step(nc.vector.tensor_scalar(dg_h[:, c], ftmp[:, c, 0:P], WS, None, ALU.mult), wait=True)
                    step(nc.vector.scalar_tensor_tensor(out=dg_l[:, c], in0=ftmp[:, c, 0:P], scalar=WS, in1=dg_h[:, c],
                                                        op0=ALU.mult, op1=ALU.subtract))
                assert done == N_PREP_D, done

            def bn(b, i, t, src, bnc, k):
                nc.vector.bn_stats(st[:, i, t, :], src).then_inc(bnc.sem, 1)

            def c1_stage(b):
                dve.wait_ge(x_in.sem, x_in.at(b, 16))
                for t in range(T):
                    bn(b, 0, t, x_sb[:, t, :], bn0, t)
                dve.wait_ge(bn0.sem, bn0.at(b, T))
                dve.sem_inc(passed, 1)
                for t in range(T):
                    nc.vector.bn_aggr(mv[:, 0, t, :], st[:, 0, t, :]).then_inc(ag0.sem, 1)
                dve.wait_ge(ag0.sem, ag0.at(b, T))
                nc.vector.tensor_scalar(ve[:, 0, :], mv[:, 0, :, 1], EPS, None, ALU.add).then_inc(ve0.sem, 1)
                dve.wait_ge(rs0.sem, rs0.at(b, 1))
                nc.vector.scalar_tensor_tensor(out=nm[:, 0, :], in0=mv[:, 0, :, 0], scalar=-1.0, in1=rs[:, 0, :],
                                               op0=ALU.mult, op1=ALU.mult).then_inc(nm0.sem, 1)

            def xn_low(b):
                for u in range(4):
                    hf, c = divmod(u, DC)
                    dve.wait_ge(xT_h.sem, xT_h.at(b, u + 1))
                    s = slice(hf * HALF, hf * HALF + HALF)
                    nc.vector.tensor_tensor(tr_l[:, c, s], MB[u % 2][:, :], tr_h[:, c, s], ALU.subtract).then_inc(xT_l.sem, 1)

            def c2_stage(b, first=False):
                if not first:
                    nm1_stage(b - 1)
                for u in range(8):
                    o, hf = divmod(u, 2)
                    dve.wait_ge(qk_hi.sem, qk_hi.at(b, u + 1))
                    s = slice(hf * HALF, hf * HALF + HALF)
                    nc.vector.scalar_tensor_tensor(out=qk_l[:, o, s], in0=QB[u % 4][:, :], scalar=bqk[:, o:o + 1],
                                                   in1=qk_h[:, o, s], op0=ALU.add, op1=ALU.subtract).then_inc(qk_lo.sem, 1)
                for t in range(T):
                    dve.wait_ge(v_ps.sem, v_ps.at(b, t + 1))
                    nc.vector.scalar_tensor_tensor(
                        out=v_a[:, t, :, 0:HD], in0=OB[t % 2][:, 0:D].rearrange("p (h d) -> p h d", h=H),
                        scalar=1.0 / WS, in1=bc[:, 1, :].rearrange("p (h d) -> p h d", h=H),
                        op0=ALU.mult, op1=ALU.add).then_inc(v_ev.sem, 1)
                    nc.vector.tensor_copy(sc[:, t, :], OB[t % 2][:, D:D + E]).then_inc(v_ev.sem, 1)
                dve.wait_ge(v_ev.sem, v_ev.at(b, 2 * T))
                nc.vector.tensor_reduce(mx8[:, 0, :], sc[:, :, :], AX.X, ALU.max).then_inc(onehot.sem, 1)
                dve.wait_ge(onehot.sem, onehot.at(b, 1))
                nc.vector.tensor_tensor(oh[:, :, :], sc[:, :, :], mx8[:, 0, :].unsqueeze(2).broadcast_to([P, T, E]),
                                        ALU.is_ge).then_inc(onehot.sem, 1)
                dve.wait_ge(onehot.sem, onehot.at(b, 2))
                iota_b = iota8[:, :].unsqueeze(1).broadcast_to([P, T, E])
                nc.vector.tensor_tensor(oh2[:, :, :], oh[:, :, :], iota_b, ALU.mult).then_inc(onehot.sem, 1)
                dve.wait_ge(onehot.sem, onehot.at(b, 3))
                nc.vector.tensor_reduce(mx8[:, 1, :], oh2[:, :, :], AX.X, ALU.min).then_inc(onehot.sem, 1)
                dve.wait_ge(onehot.sem, onehot.at(b, 4))
                nc.vector.tensor_tensor(oh[:, :, :], iota_b, mx8[:, 1, :].unsqueeze(2).broadcast_to([P, T, E]),
                                        ALU.is_equal).then_inc(onehot.sem, 1)
                dve.wait_ge(onehot.sem, onehot.at(b, 5))
                nc.vector.tensor_copy(oh16[:, 0:T, :], oh[:, :, :]).then_inc(onehot.sem, 1)

            def routing(b, first=False):
                ps = SB[0][:, 0:(T + 1) * E].rearrange("p (t e) -> p t e", e=E)
                n = 0

                def then(ins):
                    nonlocal n
                    ins.then_inc(route.sem, 1)
                    n += 1

                dve.wait_ge(rank_ps.sem, rank_ps.at(b, 1))
                then(nc.vector.tensor_tensor(cnt[:, :, :], ps[:, T, :].unsqueeze(2).broadcast_to([P, E, E]),
                                             full[:, :].unsqueeze(1).broadcast_to([P, E, E]), ALU.is_gt))
                dve.wait_ge(route.sem, route.at(b, n))
                then(nc.vector.tensor_reduce(tiles[:, 0, :], cnt[:, :, :], AX.X, ALU.add))
                dve.wait_ge(route.sem, route.at(b, n))
                then(nc.vector.tensor_tensor(cnt[:, :, :], tiles[:, 0:1, :].broadcast_to([P, E, E]), upto[:, :, :], ALU.mult))
                dve.wait_ge(route.sem, route.at(b, n))
                then(nc.vector.tensor_reduce(tiles[:, 1, :], cnt[:, :, :], AX.X, ALU.add))
                dve.wait_ge(route.sem, route.at(b, n))
                then(nc.vector.tensor_tensor(tiles[:, 2, :], tiles[:, 1, :], tiles[:, 0, :], ALU.subtract))
                dve.wait_ge(route.sem, route.at(b, n))
                then(nc.vector.scalar_tensor_tensor(out=oh2[:, :, :], in0=tiles[:, 2:3, :].broadcast_to([P, T, E]), scalar=float(P),
                                                    in1=ps[:, 0:T, :], op0=ALU.mult, op1=ALU.add))
                dve.wait_ge(route.sem, route.at(b, n))
                then(nc.vector.tensor_tensor(oh2[:, :, :], oh2[:, :, :], oh[:, :, :], ALU.mult))
                dve.wait_ge(route.sem, route.at(b, n))
                then(nc.vector.tensor_reduce(posf[:, :], oh2[:, :, :], AX.X, ALU.add))
                dve.wait_ge(route.sem, route.at(b, n))
                if not first:
                    dve.sem_inc(passed, 1)
                    dve.wait_ge(y_in.sem, y_in.at(b - 1, 16 * T))
                then(nc.vector.tensor_copy(pos[:, :], posf[:, :]))
                assert n == ROUTE_POS
                then(nc.vector.tensor_tensor(own[:, :, :], tiles[:, 1:2, 0:E - 1].broadcast_to([P, NT, E - 1]),
                                             tile_no[:, :].unsqueeze(2).broadcast_to([P, NT, E - 1]), ALU.is_le))
                dve.wait_ge(route.sem, route.at(b, n))
                then(nc.vector.tensor_reduce(tef[:, :], own[:, :, :], AX.X, ALU.add))
                dve.wait_ge(route.sem, route.at(b, n))
                then(nc.vector.tensor_copy(te[:, :], tef[:, :]))

            def xs_low(b, i):
                dve.wait_ge(xs_hi.sem, xs_hi.at(b, i + 1))
                nc.vector.tensor_tensor(xs_l[:, i % 2, :, :], TB[i % 2][:, 0:D].rearrange("p (c q) -> p c q", c=DC),
                                        xs_h[:, i % 2, :, :], ALU.subtract).then_inc(xs_lo.sem, 1)

            def maxima(b, j):
                g, t = divmod(j, T)
                v = 0 if t == 0 else 2 if t == T - 1 else 1
                for pu in range(2):
                    u = 2 * j + pu
                    dve.wait_ge(S_ps.sem, S_ps.at(b, u + 1))
                    dve.sem_inc(passed, 1)
                    for i in range(2):
                        h = 4 * g + 2 * pu + i
                        ins = nc.vector.tensor_tensor_reduce(
                            out=SB[u % 2][:, i * WIN:i * WIN + WIN], in0=SB[u % 2][:, i * WIN:i * WIN + WIN], in1=mask[:, v, :], scale=1.0,
                            scalar=-3.0e38, op0=ALU.add, op1=ALU.max, accum_out=m_sb[:, h, t:t + 1])
                    ins.then_inc(mx.sem, 1)

            def max_cols(b, g):
                dve.wait_ge(mT_ps.sem, mT_ps.at(b, g + 1))
                nc.vector.tensor_scalar(mT[:, g, :], MB[g % 2][0:4 * T, 0:P], -1.0 / KONE, None,
                                        ALU.mult).then_inc(mT_ev.sem, 1)

            def normalize(b, t):
                dve.wait_ge(t1_ps.sem, t1_ps.at(b, t + 1))
                o = MB[t % 2][:, :].rearrange("p (h w) -> p h w", h=H)
                nc.vector.reciprocal(rec[:, t, :], o[:, :, HD]).then_inc(rc.sem, 1)
                dve.wait_ge(rc.sem, rc.at(b, t + 1))
                if t >= 2:
                    dve.wait_ge(t2_ps.sem, t2_ps.at(b, t - 1))
                nc.vector.tensor_tensor(attn[:, t % 2, :].rearrange("p (h d) -> p h d", h=H), o[:, :, 0:HD],
                                        rec[:, t, :].unsqueeze(2).broadcast_to([P, H, HD]), ALU.mult).then_inc(att.sem, 1)

            def b_sum(b, t):
                dve.wait_ge(wo_ps.sem, wo_ps.at(b, t + 1))
                nc.vector.tensor_tensor(n1[:, t, :], OB[t % 2][:, 0:D], xnbo[:, t, :], ALU.add).then_inc(r1.sem, 1)
                dve.wait_ge(r1.sem, r1.at(b, t + 1))
                bn(b, 1, t, n1[:, t, :], bn1, t)

            def b_stage(b):
                dve.wait_ge(res_p.sem, res_p.at(b, 3))
                dve.sem_inc(passed, 1)
                for s in range(T + 4):
                    if s < T:
                        normalize(b, s)
                    if s >= 4:
                        b_sum(b, s - 4)
                dve.wait_ge(bn1.sem, bn1.at(b, T))
                dve.sem_inc(passed, 1)
                for t in range(T):
                    nc.vector.bn_aggr(mv[:, 1, t, :], st[:, 1, t, :]).then_inc(ag1.sem, 1)
                dve.wait_ge(ag1.sem, ag1.at(b, T))
                nc.vector.tensor_scalar(ve[:, 1, :], mv[:, 1, :, 1], EPS, None, ALU.add).then_inc(ve1.sem, 1)

            def nm1_stage(b):
                dve.wait_ge(rs1.sem, rs1.at(b, 1))
                nc.vector.scalar_tensor_tensor(out=nm[:, 1, :], in0=mv[:, 1, :, 0], scalar=-1.0, in1=rs[:, 1, :],
                                               op0=ALU.mult, op1=ALU.mult).then_inc(nm1.sem, 1)

            def f_stats(b, t):
                dve.wait_ge(f_ps.sem, f_ps.at(b, t + 1))
                bn(b, 2, t, OB[t % 2][:, 0:D], bn2, t)
                dve.wait_ge(bn2.sem, bn2.at(b, t + 1))
                dve.sem_inc(passed, 1)
                nc.vector.bn_aggr(mv[:, 2, t, :], st[:, 2, t, :]).then_inc(ag2.sem, 1)
                dve.wait_ge(ag2.sem, ag2.at(b, t + 1))
                nc.vector.tensor_scalar(ve[:, 2, t:t + 1], mv[:, 2, t, 1:2], EPS * WS * WS, None, ALU.add).then_inc(ve2.sem, 1)

            def f_out(b, t):
                nc.vector.scalar_tensor_tensor(out=ftmp[:, t % 2, :], in0=OB[t % 2][:, 0:D], scalar=mv[:, 2, t, 0:1],
                                               in1=bc[:, 2, :], op0=ALU.subtract, op1=ALU.mult).then_inc(f1.sem, 1)
                dve.wait_ge(f1.sem, f1.at(b, t + 1))
                dve.wait_ge(rs2.sem, rs2.at(b, t + 1))
                nc.vector.scalar_tensor_tensor(out=res_r[:, t, :], in0=ftmp[:, t % 2, :], scalar=rs[:, 2, t:t + 1],
                                               in1=res_r[:, t, :], op0=ALU.mult, op1=ALU.add).then_inc(f2.sem, 1)

            def gelu_low(b, u):
                hf, c = divmod(u, FC)
                dve.wait_ge(g_hi.sem, g_hi.at(b, u + 1))
                nc.vector.tensor_tensor(gL[hf][:, c, :], g32[:, u % 2, :], gH[hf][:, c, :], ALU.subtract).then_inc(g_lo.sem, 1)

            def d_stage(b, last):
                for u in range(4):
                    hf, c = divmod(u, DC)
                    dve.wait_ge(nT_h.sem, nT_h.at(b, u + 1))
                    s = slice(hf * HALF, hf * HALF + HALF)
                    nc.vector.tensor_tensor(tr_l[:, c, s], MB[u % 2][:, :], tr_h[:, c, s], ALU.subtract).then_inc(nT_l.sem, 1)
                if not last:
                    routing(b + 1)
                for u in range(2 * FC):
                    gelu_low(b, u)
                    if u % 2 and not last:
                        maxima(b + 1, u // 2)
                dve.wait_ge(res_y.sem, res_y.at(b, 1))
                dve.sem_inc(passed, 1)
                for t in range(T):
                    for i in range(2 * t, min(2 * t + 2, NT)):
                        if not last:
                            xs_low(b + 1, i)
                    f_stats(b, t)
                    if not last:
                        if t == 1:
                            max_cols(b + 1, 0)
                        maxima(b + 1, T + t)
                    f_out(b, t)

            def turn(b, last):
                for k in range(STEPS + LAG):
                    if k % T == MAX_AT and k < 3 * T:
                        max_cols(b, k // T + 1)
                    if k + LEAD < STEPS:
                        maxima(b, k + LEAD)
                    if k == 17 and not last:
                        c1_stage(b + 1)
                if not last:
                    xn_low(b + 1)
                b_stage(b)
                if last:
                    nm1_stage(b)
                else:
                    c2_stage(b + 1)
                d_stage(b, last)

            c1_stage(0)
            weights_a()
            xn_low(0)
            dve.wait_ge(pprep.sem, N_PPREP_V)
            c2_stage(0, first=True)
            weights_b()
            dve.wait_ge(pprep.sem, N_PPREP)
            routing(0, first=True)
            weights_d()
            for i in range(NT):
                xs_low(0, i)
                if i < T:
                    weights_c(i)
            assert done == N_PREP, done
            dve.wait_ge(prep.sem, done)
            for j in range(LEAD):
                if j == 10:
                    max_cols(0, 0)
                maxima(0, j)
            with dve.Fori(0, NB - 1) as b:
                turn(b, False)
            turn(NB - 1, True)

        @block.scalar
        def _(act):
            def high(hi, src):
                nc.scalar.activation(hi, src, ACT.Copy, scale=WS).then_inc(prep_hi.sem, 1)

            def weights_a():
                act.wait_ge(wa_in.sem, 16 * N_WA)
                for c in range(DC):
                    for o in range(2):
                        high(wqk_h[:, c, o * D:o * D + D], SQK[:, o, c])
                for c in range(DC):
                    high(wvg_h[:, c], SVG[:, c])

            def weights_b():
                act.wait_ge(wb_in.sem, 16 * N_WB)
                for c in range(DC):
                    high(ex_h[:, c], SEX[c])
                high(w2_h[:, :, :], SW2)
                act.wait_ge(prep.sem, N_PREP_W1)
                for c in range(DC):
                    high(w1_h[:, c], SW1[:, c])

            def norm(b, i, src, dst, rdy, tiles=range(T)):
                for t in tiles:
                    nc.scalar.activation(dst[:, t, :], src[:, t, :], ACT.Identity, bias=nm[:, i, t:t + 1],
                                         scale=rs[:, i, t:t + 1]).then_inc(rdy.sem, 1)

            def xn_tile(b, t, first=False):
                if t == 0:
                    act.wait_ge(nm0.sem, nm0.at(b, 1))
                    act.sem_inc(passed, 1)
                    if not first:
                        for sent in y_st:
                            act.wait_ge(sent.sem, sent.at(b, 0))
                            act.sem_inc(passed, 1)
                norm(b, 0, x_sb, xn, xn_rdy, (t,))

            def xn_high(b, u):
                hf, c = divmod(u, DC)
                act.wait_ge(xT_ps.sem, xT_ps.at(b, u + 1))
                nc.scalar.activation(tr_h[:, c, hf * HALF:hf * HALF + HALF], MB[u % 2][:, :], ACT.Copy).then_inc(xT_h.sem, 1)

            def c2_stage(b):
                for u in range(8):
                    o, hf = divmod(u, 2)
                    act.wait_ge(qk_ps.sem, qk_ps.at(b, u + 1))
                    nc.scalar.activation(qk_h[:, o, hf * HALF:hf * HALF + HALF], QB[u % 4][:, :], ACT.Identity,
                                         bias=bqk[:, o:o + 1]).then_inc(qk_hi.sem, 1)

            def xs_high(b, i):
                act.wait_ge(xs_ps.sem, xs_ps.at(b, i + 1))
                nc.scalar.activation(xs_h[:, i % 2, :, :], TB[i % 2][:, 0:D].rearrange("p (c q) -> p c q", c=DC),
                                     ACT.Copy).then_inc(xs_hi.sem, 1)

            def y_out(b, i):
                act.wait_ge(y_ps.sem, y_ps.at(b, i + 1))
                act.sem_inc(passed, 1)
                if i >= 2:
                    act.wait_ge(y_st[i % 2].sem, y_st[i % 2].at(b, 16 * (i // 2)))
                nc.scalar.activation(ys[:, i % 2, :], TB[i % 2][:, 0:D], ACT.Copy, scale=1.0 / WS).then_inc(y_ev.sem, 1)

            def exps(b, k):
                if k == 2:
                    act.wait_ge(f2.sem, f2.at(b, 0))
                    act.sem_inc(passed, 1)
                if k >= 3:
                    act.wait_ge(pv.sem, pv.at(b, k - 2))
                for pu in range(2):
                    u = 2 * k + pu
                    act.wait_ge(ST_ps.sem, ST_ps.at(b, u + 1))
                    nc.scalar.activation(prob[:, k % 3, 2 * pu:2 * pu + 2, :], TB[u % 2][:, :].rearrange("p (h q) -> p h q", h=2),
                                         ACT.Exp, scale=EXP_SCALE).then_inc(ex_done.sem, 1)

            def heads_out(b, g, hf):
                act.wait_ge(pv.sem, pv.at(b, T * g + (5 if hf == 0 else T)))
                nc.scalar.activation(oT[:, g, hf * HALF:hf * HALF + HALF], OB[hf][:, :], ACT.Copy).then_inc(oT_ev.sem, 1)

            def gelu_high(b, u):
                hf, c = divmod(u, FC)
                if u == FC and not isinstance(b, int):
                    act.wait_ge(pair_st.sem, pair_st.at(b + 1, 64))
                act.wait_ge(gel.sem, gel.at(b, u + 1))
                nc.scalar.activation(gH[hf][:, c, :], g32[:, u % 2, :], ACT.Copy).then_inc(g_hi.sem, 1)

            def turn(b, last):
                for k in range(STEPS + LAG):
                    if k < STEPS:
                        exps(b, k)
                    if k >= LAG + 5 and (k - LAG) % T == 5:
                        heads_out(b, (k - LAG) // T, 0)
                    if k > LAG and (k - LAG) % T == 0:
                        heads_out(b, (k - LAG) // T - 1, 1)
                    if STEPS - T <= k < STEPS and not last:
                        xn_tile(b + 1, k - (STEPS - T))
                    if k >= STEPS and not last:
                        for u in (0, 1):
                            xn_high(b + 1, 2 * (k - STEPS) + u)
                heads_out(b, G - 1, 1)
                for t in range(T):
                    act.wait_ge(t2_ps.sem, t2_ps.at(b, t + 1))
                    if t >= 2:
                        act.wait_ge(wo_ps.sem, wo_ps.at(b, t - 1))
                    nc.scalar.activation(aT[:, t % 2, :, :], TB[t % 2][:, 0:DC * P].rearrange("p (c q) -> p c q", c=DC),
                                         ACT.Copy).then_inc(aT_ev.sem, 1)
                if not last:
                    c2_stage(b + 1)
                act.wait_ge(nm1.sem, nm1.at(b, 1))
                norm(b, 1, n1, n1, n1_rdy)
                for u in range(4):
                    hf, c = divmod(u, DC)
                    act.wait_ge(nT_ps.sem, nT_ps.at(b, u + 1))
                    nc.scalar.activation(tr_h[:, c, hf * HALF:hf * HALF + HALF], MB[u % 2][:, :], ACT.Copy).then_inc(nT_h.sem, 1)
                for u in range(2 * FC):
                    c = u % FC
                    if u:
                        gelu_high(b, u - 1)
                    act.wait_ge(u_ps.sem, u_ps.at(b, u + 1))
                    if u >= 2:
                        act.wait_ge(g_lo.sem, g_lo.at(b, u - 1))
                    nc.scalar.activation(g32[:, u % 2, :], TB[u % 2][:, :], ACT.Gelu_apprx_tanh, bias=c1c[:, c:c + 1],
                                         scale=1.0 / WS).then_inc(gel.sem, 1)
                gelu_high(b, 2 * FC - 1)
                if not last:
                    act.wait_ge(g_lo.sem, g_lo.at(b, 2 * FC))
                    act.sem_inc(passed, 1)
                    for t in range(T):
                        for i in range(2 * t, min(2 * t + 2, NT)):
                            xs_high(b + 1, i)
                        for i in range(2 * t, min(2 * t + 2, NT)):
                            y_out(b + 1, i)

            weights_a()
            for t in range(T):
                xn_tile(0, t, first=True)
            for u in range(4):
                xn_high(0, u)
            c2_stage(0)
            weights_b()
            act.wait_ge(prep.sem, N_PREP_D)
            for t in range(T):
                for i in range(2 * t, min(2 * t + 2, NT)):
                    xs_high(0, i)
                for i in range(2 * t, min(2 * t + 2, NT)):
                    y_out(0, i)
            act.wait_ge(prep.sem, N_PREP)
            with act.Fori(0, NB - 1) as b:
                turn(b, False)
            turn(NB - 1, True)

        @block.tensor
        def _(pe):
            pe.sem_inc(f2.sem, f2.credit)
            def b1_w1():
                pe.wait_ge(wb_in.sem, 16 * N_WB)
                for f in range(FC):
                    for c in range(DC):
                        mm = nc.tensor.matmul(MB[0][:, f:f + 1], SW1[:, c, f * P:f * P + P], cols[:, 1, c:c + 1],
                                              start=(c == 0), stop=(c == DC - 1))
                mm.then_inc(prep_mm.sem, 1)

            def triple(dst, lh, ll, rh, rl, start, stop):
                n = len(lh)
                for c in range(n):
                    nc.tensor.matmul(dst, lh[c], rh[c], start=start and c == 0, stop=False)
                    nc.tensor.matmul(dst, lh[c], rl[c], start=False, stop=False)
                for c in range(n):
                    mm = nc.tensor.matmul(dst, ll[c], rh[c], start=False, stop=stop and c == n - 1)
                return mm

            def transposes(src, u, ps):
                hf, c = divmod(u, DC)
                for tt in range(TH):
                    mm = nc.tensor.transpose(MB[u % 2][:, tt * P:tt * P + P], src[:, hf * TH + tt, c * P:c * P + P], ident[:, :])
                mm.then_inc(ps.sem, 1)

            def xn_transposes(b, u, first=False):
                pe.wait_ge(xn_rdy.sem, xn_rdy.at(b, TH * (u // DC) + TH))
                if u == 0 and not first:
                    pe.wait_ge(mT_ev.sem, mT_ev.at(b - 1, G))
                if u >= 2:
                    pe.wait_ge(xT_l.sem, xT_l.at(b, u - 1))
                transposes(xn, u, xT_ps)

            def c2_stage(b, first):
                for u in range(8):
                    o, hf = divmod(u, 2)
                    if u == 0:
                        pe.wait_ge(xT_l.sem, xT_l.at(b, 4))
                    if u >= 4:
                        pe.wait_ge(qk_lo.sem, qk_lo.at(b, u - 3))
                    s = slice(hf * HALF, hf * HALF + HALF)
                    f = slice(o * P, o * P + P)
                    mm = triple(QB[u % 4][:, :], [wqk_h[:, c, f] for c in range(DC)], [wqk_l[:, c, f] for c in range(DC)],
                                [tr_h[:, c, s] for c in range(DC)], [tr_l[:, c, s] for c in range(DC)], True, True)
                    mm.then_inc(qk_ps.sem, 1)
                for t in range(T):
                    if t >= 2:
                        pe.wait_ge(v_ev.sem, v_ev.at(b, 2 * (t - 1)))
                    elif not first:
                        pe.wait_ge(r1.sem, r1.at(b - 1, T))
                    s = slice(t * P, t * P + P)
                    mm = triple(OB[t % 2][:, 0:D + E], [tr_h[:, c, s] for c in range(DC)], [tr_l[:, c, s] for c in range(DC)],
                                [wvg_h[:, c] for c in range(DC)], [wvg_l[:, c] for c in range(DC)], True, True)
                    mm.then_inc(v_ps.sem, 1)

            def ranks(b, first=False):
                pe.wait_ge(onehot.sem, onehot.at(b, 6))
                if not first:
                    pe.wait_ge(mx.sem, mx.at(b, 0))
                nc.tensor.matmul(SB[0][:, 0:(T + 1) * E], before[:, :], oh16[:, :, :].rearrange("p t e -> p (t e)"),
                                 start=True, stop=True)
                for t in range(T):
                    mm = nc.tensor.matmul(SB[0][:, (t + 1) * E:(T + 1) * E], ones16[:, :],
                                          oh16[:, t:t + 1, :].broadcast_to([P, T - t, E]), start=False, stop=True,
                                          skip_group_check=True)
                mm.then_inc(rank_ps.sem, 1)

            def sorted_transposes(b, i):
                if i % RUN == 0:
                    g = i // RUN
                    pe.wait_ge(xs_in[g % 2].sem, xs_in[g % 2].at(b, 16 * (g // 2 + 1)))
                if i >= 2:
                    pe.wait_ge(y_ev.sem, y_ev.at(b, i - 1))
                for c in range(DC):
                    mm = nc.tensor.transpose(TB[i % 2][:, c * P:c * P + P], xs[:, i % (2 * RUN), c * P:c * P + P], ident[:, :])
                mm.then_inc(xs_ps.sem, 1)

            def sorted_expert(b, i):
                if i == 0:
                    pe.wait_ge(route.sem, route.at(b, 12))
                    pe.sem_inc(passed, 1)
                e = nc.values_load(te[0:1, i:i + 1], engines=[mybir.EngineType.PE], min_val=0, max_val=E - 1,
                                   skip_runtime_bounds_check_because="it counts how many of E - 1 experts end before the tile")
                pe.wait_ge(xs_lo.sem, xs_lo.at(b, i + 1))
                we = [[w[:, c, bass.ds(e, 1), :] for c in range(DC)] for w in (ex_h, ex_l)]
                mm = triple(TB[i % 2][:, 0:D], [xs_h[:, i % 2, c, :] for c in range(DC)], [xs_l[:, i % 2, c, :] for c in range(DC)],
                            we[0], we[1], True, True)
                mm.then_inc(y_ps.sem, 1)

            def scores(b, j, first=False, half=None):
                g, t = divmod(j, T)
                if j == 0 and not half:
                    pe.wait_ge(route.sem, route.at(b, 6))
                    pe.wait_ge(stack.sem, stack.at(b, 16 * NSTACK))
                for pu in range(2) if half is None else (half,):
                    u = 2 * j + pu
                    if not first or u >= 2:
                        pe.wait_ge(mx.sem, mx.at(b, u - 1))
                    for i in range(2):
                        h = 4 * g + 2 * pu + i
                        for bl in range(2):
                            w0 = (2 * t + bl) * W
                            mm = nc.tensor.matmul(SB[u % 2][W * bl:W * bl + W, i * WIN:i * WIN + WIN],
                                                  q_s[:, h, W + w0:2 * W + w0], k_s[:, h // 2, w0:w0 + WIN],
                                                  start=True, stop=True)
                    mm.then_inc(S_ps.sem, 1)

            def max_cols(b, g):
                pe.wait_ge(mx.sem, mx.at(b, 2 * T * (g + 1)))
                nc.tensor.transpose(MB[g % 2][0:4 * T, 0:P], m_sb[:, 4 * g:4 * g + 4, :].rearrange("p h t -> p (h t)"),
                                    ident[:, :]).then_inc(mT_ps.sem, 1)

            def scores_t(b, k, pu):
                g, t = divmod(k, T)
                if k == 0 and pu == 0:
                    pe.wait_ge(y_ev.sem, y_ev.at(b, NT))
                if t == 0 and pu == 0:
                    pe.wait_ge(mrow.sem, mrow.at(b, 32 * (g + 1)))
                u = 2 * k + pu
                if u >= 2:
                    pe.wait_ge(ex_done.sem, ex_done.at(b, u - 1))
                for i in range(2):
                    h = 4 * g + 2 * pu + i
                    mm = nc.tensor.matmul(TB[u % 2][:, i * QW:i * QW + QW], k_s[:, h // 2, W + t * P:W + t * P + P],
                                          q_s[:, h, t * P:t * P + QW], start=True, stop=True)
                mm.then_inc(ST_ps.sem, 1)

            def values(b, k):
                g, t = divmod(k, T)
                pe.wait_ge(masked.sem, masked.at(b, 2 * k + 2))
                if k == 0:
                    pe.wait_ge(v_ev.sem, v_ev.at(b, 2 * T))
                    pe.wait_ge(f2.sem, f2.at(b, 0))
                if t == 0 and g:
                    pe.wait_ge(oT_ev.sem, oT_ev.at(b, 2 * g - 1))
                if t == TH - 1 and g:
                    pe.wait_ge(oT_ev.sem, oT_ev.at(b, 2 * g))
                lo, hi = max(0, t * P - W), min(S, t * P + P + W)
                for hf in range(2):
                    a, z = max(lo, hf * HALF), min(hi, hf * HALF + HALF)
                    if a >= z:
                        continue
                    first = t == 0 if hf == 0 else t == TH - 1
                    last = t == TH if hf == 0 else t == T - 1
                    for hl in range(4):
                        q0 = a - (t * P - W)
                        mm = nc.tensor.matmul(OB[hf][32 * hl:32 * hl + 32, a - hf * HALF:z - hf * HALF],
                                              v_a[:, t, 4 * g + hl, :], prob[:, k % 3, hl, q0:q0 + z - a],
                                              start=first, stop=last, skip_group_check=True)
                mm.then_inc(pv.sem, 1)

            def b_stage(b, last):
                for s in range(T + 4):
                    if s < T:
                        t = s
                        if t == 0:
                            pe.wait_ge(oT_ev.sem, oT_ev.at(b, 2 * G))
                            if last:
                                pe.wait_ge(mT_ev.sem, mT_ev.at(b, G))
                            else:
                                pe.wait_ge(xT_l.sem, xT_l.at(b + 1, 4))
                        if t >= 2:
                            pe.wait_ge(att.sem, att.at(b, t - 1))
                        for g in range(G):
                            mm = nc.tensor.transpose(MB[t % 2][:, g * P:g * P + P], oT[:, g, t * P:t * P + P], ident[:, :])
                        mm.then_inc(t1_ps.sem, 1)
                    if 2 <= s < T + 2:
                        t = s - 2
                        pe.wait_ge(att.sem, att.at(b, t + 1))
                        if t >= 2:
                            pe.wait_ge(aT_ev.sem, aT_ev.at(b, t - 1))
                        for c in range(DC):
                            mm = nc.tensor.transpose(TB[t % 2][:, c * P:c * P + P], attn[:, t % 2, c * P:c * P + P], ident[:, :])
                        mm.then_inc(t2_ps.sem, 1)
                    if s >= 4:
                        t = s - 4
                        pe.wait_ge(aT_ev.sem, aT_ev.at(b, t + 1))
                        if t >= 2:
                            pe.wait_ge(r1.sem, r1.at(b, t - 1))
                        for c in range(DC):
                            mm = nc.tensor.matmul(OB[t % 2][:, 0:D], aT[:, t % 2, c, :], wo[:, c, :], start=(c == 0), stop=(c == DC - 1))
                        mm.then_inc(wo_ps.sem, 1)

            def w1_unit(b, u, last):
                hf, f = divmod(u, FC)
                pe.wait_ge(nT_l.sem, nT_l.at(b, DC * hf + DC))
                if u >= 2:
                    pe.wait_ge(gel.sem, gel.at(b, u - 1))
                elif not last:
                    pe.wait_ge(qk_lo.sem, qk_lo.at(b + 1, 8))
                s = slice(hf * HALF, hf * HALF + HALF)
                fs = slice(f * P, f * P + P)
                mm = triple(TB[u % 2][:, :], [w1_h[:, c, fs] for c in range(DC)], [w1_l[:, c, fs] for c in range(DC)],
                            [tr_h[:, c, s] for c in range(DC)], [tr_l[:, c, s] for c in range(DC)], True, True)
                mm.then_inc(u_ps.sem, 1)

            def w2_tile(b, t, last):
                hf = t // TH
                pe.wait_ge(g_lo.sem, g_lo.at(b, FC * (hf + 1)))
                if t >= 2:
                    pe.wait_ge(f1.sem, f1.at(b, t - 1))
                elif not last:
                    pe.wait_ge(v_ev.sem, v_ev.at(b + 1, 2 * T))
                dst = OB[t % 2][:, 0:D]
                nc.tensor.matmul(dst, ones16[:, :], rowb[:, :], start=True, stop=False)
                s = slice(t * P, t * P + P)
                for c in range(DC):
                    triple(OB[t % 2][:, c * P:c * P + P], [tr_h[:, c, s]], [tr_l[:, c, s]], [dg_h[:, c]], [dg_l[:, c]], False, False)
                s = slice(t % TH * P, t % TH * P + P)
                mm = triple(dst, [gH[hf][:, f, s] for f in range(FC)], [gL[hf][:, f, s] for f in range(FC)],
                            [w2_h[:, f] for f in range(FC)], [w2_l[:, f] for f in range(FC)], False, True)
                mm.then_inc(f_ps.sem, 1)

            def d_stage(b, last):
                for u in range(4):
                    pe.wait_ge(n1_rdy.sem, n1_rdy.at(b, TH * (u // DC) + TH))
                    if u >= 2:
                        pe.wait_ge(nT_l.sem, nT_l.at(b, u - 1))
                    elif not last:
                        pe.wait_ge(qk_lo.sem, qk_lo.at(b + 1, 8))
                    transposes(n1, u, nT_ps)
                    if u == 1 and not last:
                        ranks(b + 1)
                for u in range(2 * FC):
                    w1_unit(b, u, last)
                    if u % 2 and not last:
                        scores(b + 1, u // 2)
                for t in range(T):
                    for i in range(2 * t, min(2 * t + 2, NT)):
                        if not last:
                            if i == 0:
                                pe.wait_ge(gel.sem, gel.at(b, 2 * FC))
                            sorted_transposes(b + 1, i)
                    w2_tile(b, t, last)
                    for i in range(2 * t, min(2 * t + 2, NT)):
                        if not last:
                            sorted_expert(b + 1, i)
                    if not last:
                        if t == 1:
                            max_cols(b + 1, 0)
                        scores(b + 1, T + t)

            def turn(b, last):
                for k in range(STEPS + LAG):
                    if k % T == MAX_AT and k < 3 * T:
                        max_cols(b, k // T + 1)
                    for pu in range(2):
                        if k + LEAD < STEPS:
                            scores(b, k + LEAD, half=pu)
                        if k < STEPS:
                            scores_t(b, k, pu)
                    if k >= STEPS and not last:
                        for u in (0, 1):
                            xn_transposes(b + 1, 2 * (k - STEPS) + u)
                    if k >= LAG:
                        values(b, k - LAG)
                b_stage(b, last)
                if not last:
                    c2_stage(b + 1, False)
                d_stage(b, last)

            pe.wait_ge(pprep.sem, 3)
            for u in range(4):
                xn_transposes(0, u, first=True)
            pe.wait_ge(prep.sem, N_PREP_A)
            c2_stage(0, True)
            pe.wait_ge(qk_lo.sem, qk_lo.at(0, 8))
            b1_w1()
            pe.wait_ge(prep.sem, N_PREP_EX)
            pe.wait_ge(pprep.sem, N_PPREP)
            ranks(0, first=True)
            for t in range(T):
                for i in range(2 * t, min(2 * t + 2, NT)):
                    sorted_transposes(0, i)
                for i in range(2 * t, min(2 * t + 2, NT)):
                    sorted_expert(0, i)
            pe.wait_ge(prep.sem, N_PREP)
            for j in range(LEAD):
                if j == 10:
                    max_cols(0, 0)
                scores(0, j, first=True)
            with pe.Fori(0, NB - 1) as b:
                turn(b, False)
            turn(NB - 1, True)


N_WA, N_WB = 8, 12
N_PPREP_V, N_PPREP = 7, 26
N_PREP_A, N_PREP_W1, N_PREP_EX, N_PREP_D, N_PREP = 7, 10, 12, 23, 39

_INS = ["L0_attn_x", "L0_attn_Wq", "L0_attn_bq", "L0_attn_Wk", "L0_attn_bk", "L0_attn_Wv", "L0_attn_bv", "L0_attn_Wo",
        "L0_attn_bo", "L0_attn_g1", "L0_attn_b1", "L0_attn_W1", "L0_attn_c1", "L0_attn_W2", "L0_attn_c2",
        "L0_attn_g2", "L0_attn_b2", "L0_ffn_gate_w", "L0_ffn_expert_w"]


def kernel(**inputs):
    import numpy as _np
    import concourse.bacc as _bacc
    from concourse import mybir as _mybir
    from concourse.bass_utils import run_bass_kernel_spmd as _run

    nc = _bacc.Bacc("TRN2", target_bir_lowering=False, num_devices=1)
    arrays, args = {}, []

    def add(name, a):
        a = _np.ascontiguousarray(a)
        arrays[f"in_{name}"] = a
        args.append(nc.dram_tensor(f"in_{name}", a.shape, _mybir.dt.from_np(a.dtype), kind="ExternalInput").ap())

    for name in _INS:
        a = _np.asarray(inputs[name])
        if name == "L0_ffn_gate_w":
            a = a.T
        if name == "L0_ffn_expert_w":
            a = a.transpose(0, 2, 1)
        if name[8:] in ("bq", "bk", "g1", "c1"):
            a = a.reshape(-1, P).T
        add(name, a)
    add("b1_by_partition", _np.asarray(inputs["L0_attn_b1"]).reshape(-1, P).T)
    shape = inputs["L0_attn_x"].shape
    args.append(nc.dram_tensor("out_0", shape, _mybir.dt.float32, kind="ExternalOutput").ap())
    build(nc, *args)
    r = _run(nc, [arrays], core_ids=[0])
    return r.results[0]["out_0"]
```

```python
from contextlib import ExitStack

import concourse.bass as bass
from concourse import mybir
from concourse.alu_op_type import AluOpType as ALU

ACT = mybir.ActivationFunctionType
F32 = mybir.dt.float32
F16 = mybir.dt.float16
BF16 = mybir.dt.bfloat16
AX = mybir.AxisListType

P = 128
W = 64
HD = 16
WS = 16.0
KONE = 256.0
NEG = -1.0e30
EPS = 1e-5
LEAD = 14
MAX_AT = 4
ROUTE_POS = 9
LAG = 2


class Count:

    def __init__(self, sem, per, credit=0):
        self.sem, self.per, self.credit = sem, per, credit

    def at(self, b, k):
        return b * self.per + (k + self.credit)


def build(nc, x, Wq, bq_c, Wk, bk_c, Wv, bv, Wo, bo, g1_c, b1, W1, c1_c, W2, c2, g2, b2, gateT, expT, b1_c, g1_row, out):
    NB, S, D = x.shape
    F = W1.shape[1]
    E = gateT.shape[1]
    H = D // HD
    T = S // P
    DC = D // P
    FC = F // P
    HALF = S // 2
    TH = T // 2
    G = H // 4
    STEPS = G * T
    SHARED = range(22, 28)
    XN_AT = 23
    WIN = 3 * W
    QW = 4 * W
    NT = T + E - 1
    RUN = 3
    EXP_SCALE = HD ** -0.5 / (WS * WS)
    VW = 32

    x_v = x.rearrange("b (t p) d -> b p t d", p=P)
    out_v = out.rearrange("b (t p) d -> b p t d", p=P)
    res_dram = nc.dram_tensor("res_dram", (NB, P, T, D), F32, kind="Internal").ap()

    pair_dram = nc.dram_tensor("pair_dram", (2, 4, P, S), F16, kind="Internal").ap()
    xs_dram = nc.dram_tensor("xs_dram", (NT * P, D), F32, kind="Internal").ap()
    ys_dram = nc.dram_tensor("ys_dram", (NT * P, D), F32, kind="Internal").ap()
    max_dram = nc.dram_tensor("max_dram", (G, 4, S), F16, kind="Internal").ap()

    W1_STEPS = range(5, 2 * FC, 2)
    assert len(W1_STEPS) + T == LEAD

    def tiles_at(t):
        return range(max(0, 2 * t - (2 * T - NT)), 2 * t + 2 - (2 * T - NT))

    with ExitStack() as ctx:
        def sb(name, shape, dt):
            return ctx.enter_context(nc.sbuf_tensor(name, shape, dt))

        def count(name, per, credit=0):
            return Count(ctx.enter_context(nc.semaphore(name)), per, credit)

        ident = sb("ident", [P, P], F32)
        mask = sb("mask", [P, 3, WIN], BF16)
        ones16 = sb("ones16", [P, P], F16)
        wqk_h, wqk_l = sb("wqk_h", [P, DC, 2 * D], F16), sb("wqk_l", [P, DC, 2 * D], F16)
        wvg_h, wvg_l = sb("wvg_h", [P, DC, D + E], F16), sb("wvg_l", [P, DC, D + E], F16)
        wo = sb("wo", [P, DC, D], F32)
        w1_h, w1_l = sb("w1_h", [P, DC, F], F16), sb("w1_l", [P, DC, F], F16)
        w2_h, w2_l = sb("w2_h", [P, FC, D], F16), sb("w2_l", [P, FC, D], F16)
        ex_h, ex_l = sb("ex_h", [P, DC, E, D], F16), sb("ex_l", [P, DC, E, D], F16)
        bqk = sb("bqk", [P, 4], F32)
        cols = sb("cols", [P, 2, DC], F32)
        c1c = sb("c1c", [P, FC], F32)
        bc = sb("bc", [P, 6, D], F32)
        iota8 = sb("iota8", [P, E], F32)
        before = sb("before", [P, P], F16)
        upto = sb("upto", [P, E, E], F32)
        full = sb("full", [P, E], F32)
        tile_no = sb("tile_no", [P, NT], F32)
        neghalf = sb("neghalf", [P, T], F32)
        x_sb = sb("x_sb", [P, T, D], F32)
        xn = sb("xn", [P, T, D], F32)
        xnbo = sb("xnbo", [P, T, D], F32)
        res_r = sb("res_r", [P, T, D], F32)
        tr_h, tr_l = sb("tr_h", [P, DC, S], F16), sb("tr_l", [P, DC, S], F16)
        pool1 = sb("pool1", [P, 2, 4, S], F16)
        pool0 = sb("pool0", [P, 2, 8, HALF], F16)
        pool2 = sb("pool2", [P, 3 * 4 * QW], F32)
        q_s = sb("q_s", [P, H, S + 2 * W], F16)
        k_s = sb("k_s", [P, H // 2, S + 2 * W], F16)
        v_a = sb("v_a", [P, T, H, VW], F32)
        m_sb = sb("m_sb", [P, H, T], F32)
        mT = sb("mT", [4 * T, G, P], F16)
        sc = sb("sc", [P, T, E], F32)
        oh = sb("oh", [P, T, E], F32)
        oh2 = sb("oh2", [P, max(T, E), E], F32)
        cnt = oh2[:, 0:E, :]
        oh16 = sb("oh16", [P, T + 1, E], F16)
        tiles = sb("tiles", [P, 3, E], F32)
        own = sb("own", [P, NT, E - 1], F32)
        posf, pos = sb("posf", [P, T], F32), sb("pos", [P, T], mybir.dt.uint32)
        pos_y = sb("pos_y", [P, T], mybir.dt.uint32)
        tef, te = sb("tef", [P, NT], F32), sb("te", [P, NT], mybir.dt.uint32)
        mx8 = sb("mx8", [P, 2, T], F32)
        keep = sb("keep", [P, 2 * W], BF16)
        rec = sb("rec", [P, T, H], F32)
        st = sb("st", [P, 3, T, 6], F32)
        mv = sb("mv", [P, 3, T, 2], F32)
        ve = sb("ve", [P, 3, T], F32)
        rs = sb("rs", [P, 3, T], F32)
        nm = sb("nm", [P, 2, T], F32)

        qk_h, qk_l = pool1[:, 0], pool1[:, 1]
        gH = [pool0[:, 0], pool1[:, 0].rearrange("p a (c t) -> p (a c) t", c=2)]
        gL = [pool0[:, 1], pool1[:, 1].rearrange("p a (c t) -> p (a c) t", c=2)]
        oT = pool0[:, :, :, :].rearrange("p a c t -> p (a c t)").bitcast(F32).rearrange("p (g t) -> p g t", g=G)
        prob = pool2[:, :].rearrange("p (s h q) -> p s h q", s=3, h=4)
        n1 = pool2[:, 0:T * D].rearrange("p (t d) -> p t d", t=T)
        g32 = pool2[:, T * D:T * D + 2 * HALF].rearrange("p (s t) -> p s t", s=2)
        stage = pool2[:, :]
        rows = pool2[:, (T + 2) * D:(T + 3) * D]
        xs_h, xs_l = (pool2[:, (T + 2 + i) * D:(T + 3 + i) * D].bitcast(F16).rearrange("p (s c q) -> p s c q", s=2, c=DC) for i in range(2))
        xs = xn[:, 0:2 * RUN, :]
        ys = xn[:, 2 * RUN:T, :]
        attn = g32[:, 0, :].rearrange("p (s d) -> p s d", s=2)
        aT = g32[:, 1, :].rearrange("p (s c q) -> p s c q", s=2, c=DC)

        bank = [ctx.enter_context(nc.psum_tensor(f"bank{i}", [P, 512], F32)) for i in range(8)]
        SB, TB, OB, MB = bank[0:2], bank[2:4], bank[4:6], bank[6:8]

        QB, VB = TB + MB, OB + TB

        wa_in, wb_in = count("wa_in", 0), count("wb_in", 0)
        prep_hi = count("prep_hi", 0)
        prep = count("prep", 0)
        pprep = count("pprep", 0)
        prep_mm = count("prep_mm", 0)
        x_in = count("x_in", 16)
        bn0, ag0, ve0, rs0, nm0 = (count(n, k) for n, k in (("bn0", T), ("ag0", T), ("ve0", 1), ("rs0", 1), ("nm0", 1)))
        xn_rdy = count("xn_rdy", T)
        xT_ps, xT_h, xT_l = count("xT_ps", 4), count("xT_h", 4), count("xT_l", 4)
        qk_ps, qk_hi, qk_lo = count("qk_ps", 8), count("qk_hi", 8), count("qk_lo", 8)
        v_ps, v_ev = count("v_ps", T), count("v_ev", 2 * T)
        onehot = count("onehot", 6)
        kept = count("kept", 1)
        rank_ps, route = count("rank_ps", 1), count("route", 12)
        scat = count("scat", 16 * T)
        xs_in = [count(f"xs_in{i}", 16 * ((NT // RUN + 1 - i) // 2)) for i in range(2)]
        y_st = [count(f"y_st{i}", 16 * ((NT + 1 - i) // 2)) for i in range(2)]
        xs_ps, xs_hi, xs_lo = count("xs_ps", NT), count("xs_hi", NT), count("xs_lo", NT)
        y_ps, y_ev = count("y_ps", NT), count("y_ev", NT)
        y_in, res_y = count("y_in", 16 * T), count("res_y", 1, credit=1)
        res_p = count("res_p", 3)
        xs_fill = count("xs_fill", 0)
        NSTACK = 2 * 2 * 3 + 2
        stack = count("stack", 16 * NSTACK)
        pair_st = count("pair_st", 16 * 4)
        res_st, res_in, out_st = count("res_st", 16), count("res_in", 16), count("out_st", 16, credit=1)
        S_ps, mx = count("S_ps", 2 * STEPS), count("mx", 2 * STEPS)
        mT_ps, mT_ev, mrow = count("mT_ps", G), count("mT_ev", G), count("mrow", 32 * G)
        mx_st = count("mx_st", 16 * G)
        ST_ps, ex_done, masked, pv = (count(n, k) for n, k in (("ST_ps", 2 * STEPS), ("exp_done", 2 * STEPS), ("masked", 2 * STEPS - len(SHARED)), ("pv", STEPS)))
        masked_v = count("masked_v", len(SHARED))
        oT_ev = count("oT_ev", 2 * G)
        t1_ps, rc, att, t2_ps, aT_ev, wo_ps = (count(n, T) for n in ("t1_ps", "rc", "att", "t2_ps", "aT_ev", "wo_ps"))
        r1, bn1, ag1, ve1, rs1, nm1, n1_rdy = (count(n, k) for n, k in (("r1", T), ("bn1", T), ("ag1", T), ("ve1", 1), ("rs1", 1), ("nm1", 1), ("n1_rdy", T)))
        nT_ps, nT_h, nT_l = count("nT_ps", 4), count("nT_h", 4), count("nT_l", 4)
        u_ps, gel, g_hi, g_lo = (count(n, 2 * FC) for n in ("u_ps", "gel", "g_hi", "g_lo"))
        h_rdy = count("h_rdy", 2)
        f_ps, bn2, ag2, ve2, rs2, f1 = (count(n, T) for n in ("f_ps", "bn2", "ag2", "ve2", "rs2", "f1"))
        r2 = count("r2", T, credit=1)
        f2 = count("f2", T, credit=TH + 1)
        passed = ctx.enter_context(nc.semaphore("passed"))

        block = ctx.enter_context(nc.Block())

        def wcols(k, w):
            return stage[:, k:k + w]

        SQK = wcols(0, 2 * DC * D).rearrange("p (w c d) -> p w c d", w=2, c=DC)
        SVG = wcols(1024, DC * (D + E)).rearrange("p (c d) -> p c d", c=DC)
        SW = pool0[:, :, :, :].rearrange("p a c t -> p (a c t)").bitcast(F32)
        SW1 = SW[:, 0:DC * F].rearrange("p (c f) -> p c f", c=DC)
        SW2 = SW[:, DC * F:DC * F + FC * D].rearrange("p (c d) -> p c d", c=FC)
        SEX = [t[:, :, :].rearrange("p t d -> p (t d)").rearrange("p (e d) -> p e d", e=E) for t in (res_r, xnbo)]

        @block.sync
        def _(sp):
            def c_in(src, p=P):
                return src.rearrange("(c p) d -> p c d", p=p)

            def load_weights_a():
                for dst, src in (
                    (SQK[:, 0], c_in(Wq)), (SQK[:, 1], c_in(Wk)), (SVG[:, :, 0:D], c_in(Wv)),
                    (SVG[:, :, D:D + E], c_in(gateT)), (bqk[:, 0:2], bq_c), (bqk[:, 2:4], bk_c),
                    (bc[:, 1], bv.partition_broadcast(P)), (bc[:, 3], b2.partition_broadcast(P)),
                ):
                    sp.dma_start(dst, src).then_inc(wa_in.sem, 16)

            def load_weights_b():
                for dst, src in (
                    (SEX[0], expT[:, 0:P, :].rearrange("e p f -> p e f")),
                    (SEX[1], expT[:, P:D, :].rearrange("e p f -> p e f")),
                    (SW1, c_in(W1)), (SW2, c_in(W2)), (wo[:, :, :], c_in(Wo)),
                    (cols[:, 0], g1_c), (cols[:, 1], b1_c), (c1c[:, :], c1_c),
                    (bc[:, 0], bo.partition_broadcast(P)), (bc[:, 2], g2.partition_broadcast(P)),
                    (bc[:, 4], g1_row.partition_broadcast(P)), (bc[:, 5], c2.partition_broadcast(P)),
                    (rows, b1.partition_broadcast(P)),
                ):
                    sp.dma_start(dst, src).then_inc(wb_in.sem, 16)

            def load_x(b, first=False):
                if not first:
                    sp.wait_ge(res_st.sem, res_st.at(b, 0))
                    sp.sem_inc(passed, 1)
                    sp.wait_ge(res_y.sem, res_y.at(b - 1, 0))
                sp.dma_start(x_sb[:, :, :], x_v[b]).then_inc(x_in.sem, 16)

            def stacks(b):
                for qk in range(2):
                    for half, (src, done) in enumerate(((qk_h, qk_hi), (qk_l, qk_lo))):
                        sp.wait_ge(done.sem, done.at(b, 4 * qk + 4))
                        sp.dma_start(pair_dram[half, 2 * qk:2 * qk + 2].rearrange("o p s -> p o s"),
                                     src[:, 2 * qk:2 * qk + 2, :]).then_inc(pair_st.sem, 16)
                    sp.wait_ge(pair_st.sem, pair_st.at(b, 32 * (qk + 1)))
                    for a in range(2):
                        for slot in range(3):
                            low = slot == (1 if qk else 2)
                            src = pair_dram[int(low), 2 * qk:2 * qk + 2].rearrange("c (j a d) s -> a d (c j) s", a=2, d=HD)[a]
                            r = W * a + HD * slot
                            dst = k_s[r:r + HD, :, W:W + S] if qk else q_s[r:r + HD, a:H:2, W:W + S]
                            sp.dma_start(dst, src).then_inc(stack.sem, 16)
                for a in range(2):
                    r = W * a + 3 * HD
                    sp.dma_start(q_s[r:r + 1, a:H:2, W:W + S], q_s[r:r + 1, 1 - a:H:2, W:W + S]).then_inc(stack.sem, 16)

            def store_res(b):
                sp.wait_ge(res_p.sem, res_p.at(b, 2))
                sp.dma_start(res_dram[b], x_sb[:, :, :]).then_inc(res_st.sem, 16)

            def load_sorted(b, g):
                if g == 0:
                    sp.wait_ge(scat.sem, scat.at(b, 16 * T))
                    sp.sem_inc(passed, 1)
                    sp.wait_ge(res_p.sem, res_p.at(b, 3))
                if g >= 2:
                    sp.wait_ge(xs_ps.sem, xs_ps.at(b, RUN * (g - 1)))
                sp.dma_start(xs[:, g % 2 * RUN:g % 2 * RUN + RUN, :],
                             xs_dram[g * RUN * P:(g + 1) * RUN * P, :].rearrange("(t p) d -> p t d", p=P)).then_inc(xs_in[g % 2].sem, 16)

            def sorted_tiles(b):
                load_sorted(b, 0)
                load_sorted(b, 1)
                for i in range(NT):
                    if i % RUN == RUN - 1 and i // RUN + 2 < NT // RUN:
                        load_sorted(b, i // RUN + 2)
                    sp.wait_ge(y_ev.sem, y_ev.at(b, i + 1))
                    sp.dma_start(ys_dram[i * P:i * P + P, :], ys[:, i % 2, :]).then_inc(y_st[i % 2].sem, 16)
                    if i == 6:
                        max_rows_out(b, 0)
                    if i == 8:
                        max_rows_in(b, 0)

            def load_res(b):
                sp.wait_ge(res_st.sem, res_st.at(b, 16))
                sp.sem_inc(passed, 1)
                sp.wait_ge(out_st.sem, out_st.at(b, 0))
                sp.dma_start(res_r[:, :, :], res_dram[b]).then_inc(res_in.sem, 16)

            def max_rows_out(b, g):
                sp.wait_ge(mT_ev.sem, mT_ev.at(b, g + 1))
                sp.dma_start(max_dram[g].rearrange("h (t c) -> (h t) c", t=T), mT[:, g, :]).then_inc(mx_st.sem, 16)

            def max_rows_in(b, g):
                sp.wait_ge(mx_st.sem, mx_st.at(b, 16 * (g + 1)))
                for a in range(2):
                    r = W * a + 3 * HD
                    sp.dma_start(q_s[r:r + 1, 4 * g + a:4 * g + 4:2, W:W + S],
                                 max_dram[g:g + 1, a::2, :]).then_inc(mrow.sem, 16)

            def max_rows(b, g):
                max_rows_out(b, g)
                max_rows_in(b, g)

            def store_out(b):
                sp.wait_ge(f2.sem, f2.at(b, T))
                sp.dma_start(out_v[b], res_r[:, :, :]).then_inc(out_st.sem, 16)

            def turn(b, last):
                max_rows(b, 1)
                if not last:
                    load_x(b + 1)
                load_res(b)
                for g in range(2, G):
                    max_rows(b, g)
                if not last:
                    store_res(b + 1)
                    stacks(b + 1)
                    sorted_tiles(b + 1)
                store_out(b)

            sp.sem_inc(out_st.sem, out_st.credit)
            sp.sem_inc(res_y.sem, res_y.credit)
            load_x(0, first=True)
            load_weights_a()
            load_weights_b()
            sp.dma_start(xs_dram, x.rearrange("b s d -> (b s) d")[0:NT * P, :]).then_inc(xs_fill.sem, 16)
            sp.wait_ge(pprep.sem, N_PPREP)
            stacks(0)
            store_res(0)
            sorted_tiles(0)
            with sp.Fori(0, NB - 1) as b:
                turn(b, False)
            turn(NB - 1, True)
            sp.wait_ge(out_st.sem, out_st.at(NB - 1, 16))

        @block.gpsimd
        def _(pool):
            done = 0

            def step(ins):
                nonlocal done
                ins.then_inc(pprep.sem, 1)
                done += 1
                pool.wait_ge(pprep.sem, done)

            def rstd(b, i, veps, rsd, t=None):
                if t is None:
                    pool.wait_ge(veps.sem, veps.at(b, 1))
                    nc.gpsimd.tensor_tensor(rs[:, i, :], ve[:, i, :], neghalf[:, :], ALU.pow).then_inc(rsd.sem, 1)
                else:
                    pool.wait_ge(veps.sem, veps.at(b, t + 1))
                    nc.gpsimd.tensor_tensor(rs[:, i, t:t + 1], ve[:, i, t:t + 1], neghalf[:, 0:1],
                                            ALU.pow).then_inc(rsd.sem, 1)

            step(nc.gpsimd.memset(ident[:, :], 0.0))
            step(nc.gpsimd.memset(neghalf[:, :], -0.5))
            step(nc.gpsimd.affine_select(out=ident[:, :], in_=ident[:, :], compare_op=ALU.not_equal, fill=1.0,
                                         base=0, pattern=[[-1, P]], channel_multiplier=1))
            rstd(0, 0, ve0, rs0)
            step(nc.gpsimd.iota(iota8[:, :], pattern=[[1, E]], base=-E, channel_multiplier=0, allow_small_or_imprecise_dtypes=True))
            pool.wait_ge(prep.sem, N_PREP_Z)
            step(nc.gpsimd.memset(v_a[:, :, :, HD:HD + 1], 1.0))
            step(nc.gpsimd.memset(oh16[:, :, :], 0.0))
            assert done == N_PPREP_V
            step(nc.gpsimd.memset(q_s[:, :, :].rearrange("p h s -> p (h s)").bitcast(F32), 0.0))
            step(nc.gpsimd.memset(mask[:, :, :], 0.0))
            step(nc.gpsimd.memset(ones16[:, :], 1.0))
            for r in (3 * HD, W + 3 * HD):
                q = r - HD
                step(nc.gpsimd.affine_select(out=k_s[q:q + 32, :, :], in_=k_s[q:q + 32, :, :], compare_op=ALU.not_equal,
                                             fill=KONE, base=-HD, pattern=[[0, H // 2], [0, S + 2 * W]],
                                             channel_multiplier=1))
            for a in range(2):
                part = mask[W * a:W * a + W, :, :]
                step(nc.gpsimd.affine_select(out=part, in_=part, compare_op=ALU.is_ge, fill=NEG, base=0,
                                             pattern=[[0, 3], [1, WIN]], channel_multiplier=-1))
                step(nc.gpsimd.affine_select(out=part, in_=part, compare_op=ALU.is_ge, fill=NEG, base=2 * W,
                                             pattern=[[0, 3], [-1, WIN]], channel_multiplier=1))
            step(nc.gpsimd.memset(keep[:, :], 1.0))
            step(nc.gpsimd.affine_select(out=keep[:, :], in_=keep[:, :], compare_op=ALU.is_ge, fill=0.0, base=0,
                                         pattern=[[-1, 2 * W]], channel_multiplier=1))
            step(nc.gpsimd.memset(before[:, :], 1.0))
            step(nc.gpsimd.affine_select(out=before[:, :], in_=before[:, :], compare_op=ALU.is_gt, fill=0.0,
                                         base=0, pattern=[[1, P]], channel_multiplier=-1))
            step(nc.gpsimd.memset(upto[:, :, :], 1.0))
            step(nc.gpsimd.affine_select(out=upto[:, :, :], in_=upto[:, :, :], compare_op=ALU.is_ge, fill=0.0,
                                         base=0, pattern=[[1, E], [-1, E]], channel_multiplier=0))
            step(nc.gpsimd.iota(full[:, :], pattern=[[P, E]], base=0, channel_multiplier=0, allow_small_or_imprecise_dtypes=True))
            step(nc.gpsimd.iota(tile_no[:, :], pattern=[[1, NT]], base=0, channel_multiplier=0, allow_small_or_imprecise_dtypes=True))
            step(nc.gpsimd.memset(mask[0:W, 0, 0:W], NEG))
            step(nc.gpsimd.memset(mask[W:P, 2, 2 * W:WIN], NEG))
            assert done == N_PPREP

            def band(b, k):
                pool.wait_ge(ex_done.sem, ex_done.at(b, 2 * k + 2))
                pool.sem_inc(passed, 1)
                p = prob[:, (k + 2) % 3, :, 0:2 * W]
                nc.gpsimd.affine_select(out=p, in_=p, compare_op=ALU.is_ge, fill=0.0, base=0,
                                        pattern=[[0, 4], [1, 2 * W]], channel_multiplier=-1).then_inc(masked.sem, 1)
                if k in SHARED:
                    return
                p = prob[:, (k + 2) % 3, :, 2 * W:QW]
                nc.gpsimd.affine_select(out=p, in_=p, compare_op=ALU.is_ge, fill=0.0, base=0,
                                        pattern=[[0, 4], [-1, 2 * W]], channel_multiplier=1).then_inc(masked.sem, 1)

            def residual(b):
                pool.wait_ge(xn_rdy.sem, xn_rdy.at(b, T))
                nc.gpsimd.tensor_tensor(x_sb[:, :, :], x_sb[:, :, :], xn[:, :, :], ALU.add).then_inc(res_p.sem, 1)
                pool.wait_ge(res_p.sem, res_p.at(b, 1))
                nc.gpsimd.tensor_tensor(x_sb[:, :, :], x_sb[:, :, :], bc[:, 3:4, :].broadcast_to([P, T, D]),
                                        ALU.add).then_inc(res_p.sem, 1)

            def residual_attn(b, first=False):
                if not first:
                    pool.wait_ge(r1.sem, r1.at(b, 0))
                nc.gpsimd.tensor_tensor(xnbo[:, :, :], xn[:, :, :], bc[:, 0:1, :].broadcast_to([P, T, D]),
                                        ALU.add).then_inc(res_p.sem, 1)

            def residual_mlp(b):
                pool.wait_ge(nT_ps.sem, nT_ps.at(b, 4))
                pool.sem_inc(passed, 1)
                nc.gpsimd.tensor_tensor(n1[:, :, :], n1[:, :, :], bc[:, 4:5, :].broadcast_to([P, T, D]), ALU.mult).then_inc(h_rdy.sem, 1)
                pool.wait_ge(h_rdy.sem, h_rdy.at(b, 1))
                nc.gpsimd.tensor_tensor(n1[:, :, :], n1[:, :, :], bc[:, 5:6, :].broadcast_to([P, T, D]), ALU.add).then_inc(h_rdy.sem, 1)

            def send(b):
                for t in range(T):
                    if t == 0:
                        pool.wait_ge(route.sem, route.at(b, ROUTE_POS))
                        pool.sem_inc(passed, 1)
                    nc.gpsimd.indirect_dma_start(out=xs_dram[:, :], out_offset=bass.IndirectOffsetOnAxis(ap=pos[:, t:t + 1], axis=0),
                                                 in_=xn[:, t, :], in_offset=None).then_inc(scat.sem, 16)

            def fetch(b, last):
                pool.wait_ge(kept.sem, kept.at(b, 1))
                pool.sem_inc(passed, 1)
                for sent in y_st:
                    pool.wait_ge(sent.sem, sent.at(b + 1, 0))
                    pool.sem_inc(passed, 1)
                if not last:
                    pool.wait_ge(res_st.sem, res_st.at(b + 1, 16))
                    pool.sem_inc(passed, 1)
                for t in range(T):
                    nc.gpsimd.indirect_dma_start(out=x_sb[:, t, :], out_offset=None, in_=ys_dram[:, :],
                                                 in_offset=bass.IndirectOffsetOnAxis(ap=pos_y[:, t:t + 1], axis=0)).then_inc(y_in.sem, 16)
                pool.wait_ge(res_in.sem, res_in.at(b, 16))
                pool.sem_inc(passed, 1)
                pool.wait_ge(y_in.sem, y_in.at(b, 16 * T))
                nc.gpsimd.tensor_tensor(res_r[:, :, :], res_r[:, :, :], x_sb[:, :, :], ALU.add).then_inc(res_y.sem, 1)

            def turn(b, last):
                for k in range(STEPS):
                    band(b, k)
                    if k == XN_AT - 1 and not last:
                        rstd(b + 1, 0, ve0, rs0)
                if not last:
                    residual(b + 1)
                rstd(b, 1, ve1, rs1)
                if not last:
                    residual_attn(b + 1)
                fetch(b, last)
                if not last:
                    send(b + 1)
                residual_mlp(b)
                for t in range(T):
                    rstd(b, 2, ve2, rs2, t)

            pool.wait_ge(wa_in.sem, 16 * N_WA)
            residual(0)
            pool.wait_ge(wb_in.sem, 16 * N_WB)
            pool.wait_ge(prep.sem, N_PREP_EX)
            residual_attn(0, first=True)
            pool.wait_ge(xs_fill.sem, 16)
            send(0)
            pool.wait_ge(prep.sem, N_PREP_D)
            with pool.Fori(0, NB - 1) as b:
                turn(b, False)
            turn(NB - 1, True)

        @block.vector
        def _(dve):
            done = 0

            def step(ins, wait=False):
                nonlocal done
                ins.then_inc(prep.sem, 1)
                done += 1
                if wait:
                    dve.wait_ge(prep.sem, done)

            def low(hi, lo, src, n):
                dve.wait_ge(prep_hi.sem, n)
                step(nc.vector.scalar_tensor_tensor(out=lo, in0=src, scalar=WS, in1=hi, op0=ALU.mult, op1=ALU.subtract))

            def weights_a():
                dve.wait_ge(wa_in.sem, 16 * N_WA)
                step(nc.vector.tensor_scalar(bqk[:, :], bqk[:, :], WS, None, ALU.mult))
                for c in range(DC):
                    for o in range(2):
                        low(wqk_h[:, c, o * D:o * D + D], wqk_l[:, c, o * D:o * D + D], SQK[:, o, c], 2 * c + o + 1)
                for c in range(DC):
                    low(wvg_h[:, c], wvg_l[:, c], SVG[:, c], 2 * DC + c + 1)
                assert done == N_PREP_A

            def weights_b():
                dve.wait_ge(wb_in.sem, 16 * N_WB)
                dve.wait_ge(prep_mm.sem, 1)
                step(nc.vector.tensor_tensor(c1c[:, :], c1c[:, :], MB[0][:, 0:FC], ALU.add))
                for c in range(DC):
                    step(nc.vector.tensor_scalar(SW1[:, c], SW1[:, c], cols[:, 0, c:c + 1], None, ALU.mult))
                assert done == N_PREP_W1
                for c in range(DC):
                    low(ex_h[:, c], ex_l[:, c], SEX[c], 3 * DC + c + 1)
                assert done == N_PREP_EX

            def weights_c(t):
                low(w2_h[:, t], w2_l[:, t], SW2[:, t], 4 * DC + 1)
                c, w = t // TH, F // TH
                f = slice(t % TH * w, t % TH * w + w)
                low(w1_h[:, c, f], w1_l[:, c, f], SW1[:, c, f], 4 * DC + 2 + c)

            def weights_d():
                step(nc.vector.tensor_tensor(bc[:, 5], bc[:, 5], rows, ALU.add))
                assert done == N_PREP_D, done

            def bn(b, i, t, src, bnc, k):
                nc.vector.bn_stats(st[:, i, t, :], src).then_inc(bnc.sem, 1)

            def c1_stage(b):
                dve.wait_ge(x_in.sem, x_in.at(b, 16))
                for t in range(T):
                    bn(b, 0, t, x_sb[:, t, :], bn0, t)
                dve.wait_ge(bn0.sem, bn0.at(b, T))
                dve.sem_inc(passed, 1)
                for t in range(T):
                    nc.vector.bn_aggr(mv[:, 0, t, :], st[:, 0, t, :]).then_inc(ag0.sem, 1)
                dve.wait_ge(ag0.sem, ag0.at(b, T))
                nc.vector.tensor_scalar(ve[:, 0, :], mv[:, 0, :, 1], EPS, None, ALU.add).then_inc(ve0.sem, 1)

            def xn_tile(b, t, first=False):
                if t == 0:
                    dve.wait_ge(rs0.sem, rs0.at(b, 1))
                    nc.vector.scalar_tensor_tensor(out=nm[:, 0, :], in0=mv[:, 0, :, 0], scalar=-1.0, in1=rs[:, 0, :],
                                                   op0=ALU.mult, op1=ALU.mult).then_inc(nm0.sem, 1)
                    dve.wait_ge(nm0.sem, nm0.at(b, 1))
                    if not first:
                        for sent in y_st:
                            dve.sem_inc(passed, 1)
                            dve.wait_ge(sent.sem, sent.at(b, 0))
                        dve.sem_inc(passed, 1)
                nc.vector.tensor_scalar(xn[:, t, :], x_sb[:, t, :], rs[:, 0, t:t + 1], nm[:, 0, t:t + 1],
                                        ALU.mult, ALU.add).then_inc(xn_rdy.sem, 1)

            def xn_low(b, u):
                hf, c = divmod(u, DC)
                dve.wait_ge(xT_h.sem, xT_h.at(b, u + 1))
                s = slice(hf * HALF, hf * HALF + HALF)
                nc.vector.tensor_tensor(tr_l[:, c, s], MB[u % 2][:, :], tr_h[:, c, s], ALU.subtract).then_inc(xT_l.sem, 1)

            def n1_low(b, u):
                hf, c = divmod(u, DC)
                dve.wait_ge(nT_h.sem, nT_h.at(b, u + 1))
                s = slice(hf * HALF, hf * HALF + HALF)
                nc.vector.tensor_tensor(tr_l[:, c, s], MB[u % 2][:, :], tr_h[:, c, s], ALU.subtract).then_inc(nT_l.sem, 1)

            def c2_stage(b, first=False):
                if not first:
                    nm1_stage(b - 1)
                for u in range(8):
                    o, hf = divmod(u, 2)
                    dve.wait_ge(qk_hi.sem, qk_hi.at(b, u + 1))
                    s = slice(hf * HALF, hf * HALF + HALF)
                    nc.vector.scalar_tensor_tensor(out=qk_l[:, o, s], in0=QB[u % 4][:, :], scalar=bqk[:, o:o + 1],
                                                   in1=qk_h[:, o, s], op0=ALU.add, op1=ALU.subtract).then_inc(qk_lo.sem, 1)
                for t in range(T):
                    dve.wait_ge(v_ps.sem, v_ps.at(b, t + 1))
                    nc.vector.scalar_tensor_tensor(
                        out=v_a[:, t, :, 0:HD], in0=VB[t % 4][:, 0:D].rearrange("p (h d) -> p h d", h=H),
                        scalar=1.0 / WS, in1=bc[:, 1, :].rearrange("p (h d) -> p h d", h=H),
                        op0=ALU.mult, op1=ALU.add).then_inc(v_ev.sem, 1)
                    nc.vector.tensor_copy(sc[:, t, :], VB[t % 4][:, D:D + E]).then_inc(v_ev.sem, 1)
                    if t == T - 2 and not first:
                        for u in range(2):
                            n1_low(b - 1, u)

            def one_hot(b):
                dve.wait_ge(v_ev.sem, v_ev.at(b, 2 * T))
                nc.vector.tensor_reduce(mx8[:, 0, :], sc[:, :, :], AX.X, ALU.max).then_inc(onehot.sem, 1)
                dve.wait_ge(onehot.sem, onehot.at(b, 1))
                nc.vector.tensor_tensor(oh[:, :, :], sc[:, :, :], mx8[:, 0, :].unsqueeze(2).broadcast_to([P, T, E]),
                                        ALU.is_ge).then_inc(onehot.sem, 1)
                dve.wait_ge(onehot.sem, onehot.at(b, 2))
                iota_b = iota8[:, :].unsqueeze(1).broadcast_to([P, T, E])
                nc.vector.tensor_tensor(oh2[:, 0:T, :], oh[:, :, :], iota_b, ALU.mult).then_inc(onehot.sem, 1)
                dve.wait_ge(onehot.sem, onehot.at(b, 3))
                nc.vector.tensor_reduce(mx8[:, 1, :], oh2[:, 0:T, :], AX.X, ALU.min).then_inc(onehot.sem, 1)
                dve.wait_ge(onehot.sem, onehot.at(b, 4))
                nc.vector.tensor_tensor(oh[:, :, :], iota_b, mx8[:, 1, :].unsqueeze(2).broadcast_to([P, T, E]),
                                        ALU.is_equal).then_inc(onehot.sem, 1)
                dve.wait_ge(onehot.sem, onehot.at(b, 5))
                nc.vector.tensor_copy(oh16[:, 0:T, :], oh[:, :, :]).then_inc(onehot.sem, 1)

            ranked = SB[0][:, 0:(T + 1) * E].rearrange("p (t e) -> p t e", e=E)

            def routing_tiles(b):
                dve.wait_ge(rank_ps.sem, rank_ps.at(b, 1))
                nc.vector.tensor_tensor(cnt, ranked[:, T, :].unsqueeze(2).broadcast_to([P, E, E]),
                                             full[:, :].unsqueeze(1).broadcast_to([P, E, E]), ALU.is_gt).then_inc(route.sem, 1)
                dve.wait_ge(route.sem, route.at(b, 1))
                nc.vector.tensor_reduce(tiles[:, 0, :], cnt, AX.X, ALU.add).then_inc(route.sem, 1)
                dve.wait_ge(route.sem, route.at(b, 2))
                nc.vector.tensor_tensor(cnt, tiles[:, 0:1, :].broadcast_to([P, E, E]), upto[:, :, :], ALU.mult).then_inc(route.sem, 1)
                dve.wait_ge(route.sem, route.at(b, 3))
                nc.vector.tensor_reduce(tiles[:, 1, :], cnt, AX.X, ALU.add).then_inc(route.sem, 1)
                dve.wait_ge(route.sem, route.at(b, 4))
                nc.vector.tensor_tensor(tiles[:, 2, :], tiles[:, 1, :], tiles[:, 0, :], ALU.subtract).then_inc(route.sem, 1)

            def routing_positions(b):
                dve.wait_ge(route.sem, route.at(b, 5))
                nc.vector.scalar_tensor_tensor(out=oh2[:, 0:T, :], in0=tiles[:, 2:3, :].broadcast_to([P, T, E]), scalar=float(P),
                                                    in1=ranked[:, 0:T, :], op0=ALU.mult, op1=ALU.add).then_inc(route.sem, 1)
                dve.wait_ge(route.sem, route.at(b, 6))
                nc.vector.tensor_tensor(oh2[:, 0:T, :], oh2[:, 0:T, :], oh[:, :, :], ALU.mult).then_inc(route.sem, 1)
                dve.wait_ge(route.sem, route.at(b, 7))
                nc.vector.tensor_reduce(posf[:, :], oh2[:, 0:T, :], AX.X, ALU.add).then_inc(route.sem, 1)
                dve.wait_ge(route.sem, route.at(b, 8))
                nc.vector.tensor_copy(pos[:, :], posf[:, :]).then_inc(route.sem, 1)

            def routing_experts(b):
                nc.vector.tensor_tensor(own[:, :, :], tiles[:, 1:2, 0:E - 1].broadcast_to([P, NT, E - 1]),
                                             tile_no[:, :].unsqueeze(2).broadcast_to([P, NT, E - 1]), ALU.is_le).then_inc(route.sem, 1)
                dve.wait_ge(route.sem, route.at(b, 10))
                nc.vector.tensor_reduce(tef[:, :], own[:, :, :], AX.X, ALU.add).then_inc(route.sem, 1)
                dve.wait_ge(route.sem, route.at(b, 11))
                nc.vector.tensor_copy(te[:, :], tef[:, :]).then_inc(route.sem, 1)

            def keep_positions(b):
                nc.vector.tensor_copy(pos_y[:, :], posf[:, :]).then_inc(kept.sem, 1)

            def xs_low(b, i):
                dve.wait_ge(xs_hi.sem, xs_hi.at(b, i + 1))
                nc.vector.tensor_tensor(xs_l[:, i % 2, :, :], TB[i % 2][:, 0:D].rearrange("p (c q) -> p c q", c=DC),
                                        xs_h[:, i % 2, :, :], ALU.subtract).then_inc(xs_lo.sem, 1)

            def maxima(b, j):
                g, t = divmod(j, T)
                v = 0 if t == 0 else 2 if t == T - 1 else 1
                for pu in range(2):
                    u = 2 * j + pu
                    dve.wait_ge(S_ps.sem, S_ps.at(b, u + 1))
                    dve.sem_inc(passed, 1)
                    for i in range(2):
                        h = 4 * g + 2 * pu + i
                        ins = nc.vector.tensor_tensor_reduce(
                            out=SB[u % 2][:, i * WIN:i * WIN + WIN], in0=SB[u % 2][:, i * WIN:i * WIN + WIN], in1=mask[:, v, :], scale=1.0,
                            scalar=-3.0e38, op0=ALU.add, op1=ALU.max, accum_out=m_sb[:, h, t:t + 1])
                    ins.then_inc(mx.sem, 1)

            def max_cols(b, g):
                dve.wait_ge(mT_ps.sem, mT_ps.at(b, g + 1))
                nc.vector.tensor_scalar(mT[:, g, :], MB[g % 2][0:4 * T, 0:P], -1.0 / KONE, None,
                                        ALU.mult).then_inc(mT_ev.sem, 1)

            def band(b, k):
                dve.wait_ge(ex_done.sem, ex_done.at(b, 2 * k + 2))
                p = prob[:, (k + 2) % 3, :, 2 * W:QW]
                nc.vector.tensor_tensor(p, p, keep[:, :].unsqueeze(1).broadcast_to([P, 4, 2 * W]), ALU.mult).then_inc(masked_v.sem, 1)

            def normalize(b, t):
                dve.wait_ge(t1_ps.sem, t1_ps.at(b, t + 1))
                o = MB[t % 2][:, :].rearrange("p (h w) -> p h w", h=H)
                nc.vector.reciprocal(rec[:, t, :], o[:, :, HD]).then_inc(rc.sem, 1)
                dve.wait_ge(rc.sem, rc.at(b, t + 1))
                if t >= 2:
                    dve.wait_ge(t2_ps.sem, t2_ps.at(b, t - 1))
                nc.vector.tensor_tensor(attn[:, t % 2, :].rearrange("p (h d) -> p h d", h=H), o[:, :, 0:HD],
                                        rec[:, t, :].unsqueeze(2).broadcast_to([P, H, HD]), ALU.mult).then_inc(att.sem, 1)

            def b_sum(b, t):
                dve.wait_ge(wo_ps.sem, wo_ps.at(b, t + 1))
                nc.vector.tensor_tensor(n1[:, t, :], OB[t % 2][:, 0:D], xnbo[:, t, :], ALU.add).then_inc(r1.sem, 1)
                dve.wait_ge(r1.sem, r1.at(b, t + 1))
                bn(b, 1, t, n1[:, t, :], bn1, t)

            def b_stage(b):
                dve.wait_ge(res_p.sem, res_p.at(b, 3))
                dve.sem_inc(passed, 1)
                for s in range(T + 4):
                    if s < T:
                        normalize(b, s)
                    if s >= 4:
                        b_sum(b, s - 4)
                dve.wait_ge(bn1.sem, bn1.at(b, T))
                dve.sem_inc(passed, 1)
                for t in range(T):
                    nc.vector.bn_aggr(mv[:, 1, t, :], st[:, 1, t, :]).then_inc(ag1.sem, 1)
                dve.wait_ge(ag1.sem, ag1.at(b, T))
                nc.vector.tensor_scalar(ve[:, 1, :], mv[:, 1, :, 1], EPS, None, ALU.add).then_inc(ve1.sem, 1)

            def nm1_stage(b):
                dve.wait_ge(rs1.sem, rs1.at(b, 1))
                nc.vector.scalar_tensor_tensor(out=nm[:, 1, :], in0=mv[:, 1, :, 0], scalar=-1.0, in1=rs[:, 1, :],
                                               op0=ALU.mult, op1=ALU.mult).then_inc(nm1.sem, 1)

            def f_stats(b, t):
                dve.wait_ge(f_ps.sem, f_ps.at(b, t + 1))
                nc.vector.scalar_tensor_tensor(out=n1[:, t, :], in0=OB[t % 2][:, 0:D], scalar=1.0 / WS, in1=n1[:, t, :],
                                               op0=ALU.mult, op1=ALU.add).then_inc(r2.sem, 1)
                dve.wait_ge(r2.sem, r2.at(b, t + 1))
                bn(b, 2, t, n1[:, t, :], bn2, t)
                dve.wait_ge(bn2.sem, bn2.at(b, t + 1))
                dve.sem_inc(passed, 1)
                nc.vector.bn_aggr(mv[:, 2, t, :], st[:, 2, t, :]).then_inc(ag2.sem, 1)
                dve.wait_ge(ag2.sem, ag2.at(b, t + 1))
                nc.vector.tensor_scalar(ve[:, 2, t:t + 1], mv[:, 2, t, 1:2], EPS, None, ALU.add).then_inc(ve2.sem, 1)

            def f_out(b, t):
                nc.vector.scalar_tensor_tensor(out=n1[:, t, :], in0=n1[:, t, :], scalar=mv[:, 2, t, 0:1],
                                               in1=bc[:, 2, :], op0=ALU.subtract, op1=ALU.mult).then_inc(f1.sem, 1)
                dve.wait_ge(f1.sem, f1.at(b, t + 1))
                dve.sem_inc(passed, 1)
                dve.wait_ge(rs2.sem, rs2.at(b, t + 1))
                nc.vector.scalar_tensor_tensor(out=res_r[:, t, :], in0=n1[:, t, :], scalar=rs[:, 2, t:t + 1],
                                               in1=res_r[:, t, :], op0=ALU.mult, op1=ALU.add).then_inc(f2.sem, 1)

            def gelu_low(b, u):
                hf, c = divmod(u, FC)
                dve.wait_ge(g_hi.sem, g_hi.at(b, u + 1))
                nc.vector.tensor_tensor(gL[hf][:, c, :], g32[:, u % 2, :], gH[hf][:, c, :], ALU.subtract).then_inc(g_lo.sem, 1)

            def d_stage(b, last):
                for u in range(0 if last else 2, 4):
                    n1_low(b, u)
                if not last:
                    one_hot(b + 1)
                for u in range(2 * FC):
                    gelu_low(b, u)
                    if u == 0 and not last:
                        routing_tiles(b + 1)
                    if u == 1 and not last:
                        routing_positions(b + 1)
                    if u == 2 and not last:
                        routing_experts(b + 1)
                    if u in W1_STEPS and not last:
                        maxima(b + 1, W1_STEPS.index(u))
                dve.wait_ge(res_y.sem, res_y.at(b, 1))
                dve.sem_inc(passed, 1)
                dve.wait_ge(h_rdy.sem, h_rdy.at(b, 2))
                dve.sem_inc(passed, 1)
                for t in range(T):
                    for i in tiles_at(t):
                        if not last:
                            xs_low(b + 1, i)
                    f_stats(b, t)
                    if not last:
                        if t == 3:
                            max_cols(b + 1, 0)
                        maxima(b + 1, LEAD - T + t)
                    f_out(b, t)
                if not last:
                    keep_positions(b + 1)

            def turn(b, last):
                for k in range(STEPS + LAG):
                    if k % T == MAX_AT and k < 3 * T:
                        max_cols(b, k // T + 1)
                    if 1 <= k and k - 1 + LEAD < STEPS:
                        maxima(b, k - 1 + LEAD)
                    if k == 2 * T + MAX_AT and not last:
                        c1_stage(b + 1)
                    if k in SHARED:
                        band(b, k)
                    if XN_AT <= k < XN_AT + T // 2 and not last:
                        for t in range(2):
                            xn_tile(b + 1, 2 * (k - XN_AT) + t)
                    if STEPS - 4 <= k < STEPS and not last:
                        xn_low(b + 1, k - (STEPS - 4))
                b_stage(b)
                if last:
                    nm1_stage(b)
                else:
                    c2_stage(b + 1)
                d_stage(b, last)

            step(nc.vector.memset(v_a[:, :, :, :], 0.0))
            step(nc.vector.memset(k_s[:, :, :].rearrange("p h s -> p (h s)").bitcast(F32), 0.0))
            assert done == N_PREP_Z
            c1_stage(0)
            for t in range(T):
                xn_tile(0, t, first=True)
            weights_a()
            for u in range(4):
                xn_low(0, u)
            dve.wait_ge(pprep.sem, N_PPREP_V)
            c2_stage(0, first=True)
            dve.wait_ge(pprep.sem, N_PPREP)
            one_hot(0)
            routing_tiles(0)
            routing_positions(0)
            routing_experts(0)
            keep_positions(0)
            weights_b()
            weights_d()
            for t in range(T):
                weights_c(t)
            for j in range(LEAD - T):
                maxima(0, j)
            for t in range(T):
                for i in tiles_at(t):
                    xs_low(0, i)
                if t == 3:
                    max_cols(0, 0)
                maxima(0, LEAD - T + t)
            assert done == N_PREP, done
            dve.wait_ge(prep.sem, done)
            with dve.Fori(0, NB - 1) as b:
                turn(b, False)
            turn(NB - 1, True)

        @block.scalar
        def _(act):
            def high(hi, src):
                nc.scalar.activation(hi, src, ACT.Copy, scale=WS).then_inc(prep_hi.sem, 1)

            def weights_a():
                act.wait_ge(wa_in.sem, 16 * N_WA)
                for c in range(DC):
                    for o in range(2):
                        high(wqk_h[:, c, o * D:o * D + D], SQK[:, o, c])
                for c in range(DC):
                    high(wvg_h[:, c], SVG[:, c])

            def weights_b():
                act.wait_ge(wb_in.sem, 16 * N_WB)
                for c in range(DC):
                    high(ex_h[:, c], SEX[c])
                high(w2_h[:, :, :], SW2)
                act.wait_ge(prep.sem, N_PREP_W1)
                for c in range(DC):
                    high(w1_h[:, c], SW1[:, c])

            def n1_tiles(b):
                for t in range(T):
                    nc.scalar.activation(n1[:, t, :], n1[:, t, :], ACT.Identity, bias=nm[:, 1, t:t + 1],
                                         scale=rs[:, 1, t:t + 1]).then_inc(n1_rdy.sem, 1)

            def xn_high(b, u):
                hf, c = divmod(u, DC)
                act.wait_ge(xT_ps.sem, xT_ps.at(b, u + 1))
                nc.scalar.activation(tr_h[:, c, hf * HALF:hf * HALF + HALF], MB[u % 2][:, :], ACT.Copy).then_inc(xT_h.sem, 1)

            def c2_stage(b):
                for u in range(8):
                    o, hf = divmod(u, 2)
                    act.wait_ge(qk_ps.sem, qk_ps.at(b, u + 1))
                    nc.scalar.activation(qk_h[:, o, hf * HALF:hf * HALF + HALF], QB[u % 4][:, :], ACT.Identity,
                                         bias=bqk[:, o:o + 1]).then_inc(qk_hi.sem, 1)

            def xs_high(b, i):
                act.wait_ge(xs_ps.sem, xs_ps.at(b, i + 1))
                nc.scalar.activation(xs_h[:, i % 2, :, :], TB[i % 2][:, 0:D].rearrange("p (c q) -> p c q", c=DC),
                                     ACT.Copy).then_inc(xs_hi.sem, 1)

            def y_out(b, i):
                act.wait_ge(y_ps.sem, y_ps.at(b, i + 1))
                act.sem_inc(passed, 1)
                if i >= 2:
                    act.wait_ge(y_st[i % 2].sem, y_st[i % 2].at(b, 16 * (i // 2)))
                nc.scalar.activation(ys[:, i % 2, :], TB[i % 2][:, 0:D], ACT.Copy, scale=1.0 / WS).then_inc(y_ev.sem, 1)

            def exps(b, k):
                if k in (1, 2):
                    act.wait_ge(f2.sem, f2.at(b, -TH if k == 1 else 0))
                    act.sem_inc(passed, 1)
                if k >= 3:
                    act.wait_ge(pv.sem, pv.at(b, k - 2))
                for pu in range(2):
                    u = 2 * k + pu
                    act.wait_ge(ST_ps.sem, ST_ps.at(b, u + 1))
                    nc.scalar.activation(prob[:, (k + 2) % 3, 2 * pu:2 * pu + 2, :], TB[u % 2][:, :].rearrange("p (h q) -> p h q", h=2),
                                         ACT.Exp, scale=EXP_SCALE).then_inc(ex_done.sem, 1)

            def heads_out(b, g, hf):
                act.wait_ge(pv.sem, pv.at(b, T * g + (5 if hf == 0 else T)))
                nc.scalar.activation(oT[:, g, hf * HALF:hf * HALF + HALF], OB[hf][:, :], ACT.Copy).then_inc(oT_ev.sem, 1)

            def gelu_high(b, u):
                hf, c = divmod(u, FC)
                if u == FC and not isinstance(b, int):
                    act.wait_ge(pair_st.sem, pair_st.at(b + 1, 64))
                act.wait_ge(gel.sem, gel.at(b, u + 1))
                nc.scalar.activation(gH[hf][:, c, :], g32[:, u % 2, :], ACT.Copy).then_inc(g_hi.sem, 1)

            def turn(b, last):
                for k in range(STEPS + LAG):
                    if k < STEPS:
                        exps(b, k)
                    if k >= LAG + 5 and (k - LAG) % T == 5:
                        heads_out(b, (k - LAG) // T, 0)
                    if k > LAG and (k - LAG) % T == 0:
                        heads_out(b, (k - LAG) // T - 1, 1)
                    if STEPS - 4 <= k < STEPS and not last:
                        xn_high(b + 1, k - (STEPS - 4))
                heads_out(b, G - 1, 1)
                for t in range(T):
                    act.wait_ge(t2_ps.sem, t2_ps.at(b, t + 1))
                    if t >= 2:
                        act.wait_ge(wo_ps.sem, wo_ps.at(b, t - 1))
                    nc.scalar.activation(aT[:, t % 2, :, :], TB[t % 2][:, 0:DC * P].rearrange("p (c q) -> p c q", c=DC),
                                         ACT.Copy).then_inc(aT_ev.sem, 1)
                if not last:
                    c2_stage(b + 1)
                act.wait_ge(nm1.sem, nm1.at(b, 1))
                n1_tiles(b)
                for u in range(4):
                    hf, c = divmod(u, DC)
                    act.wait_ge(nT_ps.sem, nT_ps.at(b, u + 1))
                    nc.scalar.activation(tr_h[:, c, hf * HALF:hf * HALF + HALF], MB[u % 2][:, :], ACT.Copy).then_inc(nT_h.sem, 1)
                for u in range(2 * FC):
                    c = u % FC
                    if u:
                        gelu_high(b, u - 1)
                    act.wait_ge(u_ps.sem, u_ps.at(b, u + 1))
                    if u >= 2:
                        act.wait_ge(g_lo.sem, g_lo.at(b, u - 1))
                    nc.scalar.activation(g32[:, u % 2, :], TB[u % 2][:, :], ACT.Gelu_apprx_tanh, bias=c1c[:, c:c + 1],
                                         scale=1.0 / WS).then_inc(gel.sem, 1)
                gelu_high(b, 2 * FC - 1)
                if not last:
                    act.wait_ge(g_lo.sem, g_lo.at(b, 2 * FC))
                    act.sem_inc(passed, 1)
                    for t in range(T):
                        for i in tiles_at(t):
                            xs_high(b + 1, i)
                        for i in tiles_at(t):
                            y_out(b + 1, i)

            weights_a()
            for u in range(4):
                xn_high(0, u)
            c2_stage(0)
            weights_b()
            act.wait_ge(prep.sem, N_PREP_D)
            for t in range(T):
                for i in tiles_at(t):
                    xs_high(0, i)
                for i in tiles_at(t):
                    y_out(0, i)
            act.wait_ge(prep.sem, N_PREP)
            with act.Fori(0, NB - 1) as b:
                turn(b, False)
            turn(NB - 1, True)

        @block.tensor
        def _(pe):
            pe.sem_inc(f2.sem, f2.credit)
            pe.sem_inc(r2.sem, r2.credit)
            def b1_w1():
                pe.wait_ge(wb_in.sem, 16 * N_WB)
                for f in range(FC):
                    for c in range(DC):
                        mm = nc.tensor.matmul(MB[0][:, f:f + 1], SW1[:, c, f * P:f * P + P], cols[:, 1, c:c + 1],
                                              start=(c == 0), stop=(c == DC - 1))
                mm.then_inc(prep_mm.sem, 1)

            def triple(dst, lh, ll, rh, rl, start, stop):
                n = len(lh)
                for c in range(n):
                    nc.tensor.matmul(dst, lh[c], rh[c], start=start and c == 0, stop=False)
                    nc.tensor.matmul(dst, lh[c], rl[c], start=False, stop=False)
                for c in range(n):
                    mm = nc.tensor.matmul(dst, ll[c], rh[c], start=False, stop=stop and c == n - 1)
                return mm

            def transposes(src, u, ps):
                hf, c = divmod(u, DC)
                for tt in range(TH):
                    mm = nc.tensor.transpose(MB[u % 2][:, tt * P:tt * P + P], src[:, hf * TH + tt, c * P:c * P + P], ident[:, :])
                mm.then_inc(ps.sem, 1)

            def xn_transposes(b, u, first=False):
                pe.wait_ge(xn_rdy.sem, xn_rdy.at(b, TH * (u // DC) + TH))
                if u == 0 and not first:
                    pe.wait_ge(mT_ev.sem, mT_ev.at(b - 1, G))
                if u >= 2:
                    pe.wait_ge(xT_l.sem, xT_l.at(b, u - 1))
                transposes(xn, u, xT_ps)

            def c2_stage(b, first):
                for u in range(8):
                    o, hf = divmod(u, 2)
                    if u == 0:
                        pe.wait_ge(xT_l.sem, xT_l.at(b, 4))
                    if u >= 4:
                        pe.wait_ge(qk_lo.sem, qk_lo.at(b, u - 3))
                    s = slice(hf * HALF, hf * HALF + HALF)
                    f = slice(o * P, o * P + P)
                    mm = triple(QB[u % 4][:, :], [wqk_h[:, c, f] for c in range(DC)], [wqk_l[:, c, f] for c in range(DC)],
                                [tr_h[:, c, s] for c in range(DC)], [tr_l[:, c, s] for c in range(DC)], True, True)
                    mm.then_inc(qk_ps.sem, 1)
                for t in range(T):
                    if t == T - 2 and not first:
                        for u in range(2):
                            n1_transposes(b - 1, u)
                    if t >= 4:
                        pe.wait_ge(v_ev.sem, v_ev.at(b, 2 * (t - 3)))
                    elif t >= 2:
                        pe.wait_ge(qk_lo.sem, qk_lo.at(b, 4 + t - 1))
                    elif not first:
                        pe.wait_ge(r1.sem, r1.at(b - 1, T))
                    s = slice(t * P, t * P + P)
                    mm = triple(VB[t % 4][:, 0:D + E], [tr_h[:, c, s] for c in range(DC)], [tr_l[:, c, s] for c in range(DC)],
                                [wvg_h[:, c] for c in range(DC)], [wvg_l[:, c] for c in range(DC)], True, True)
                    mm.then_inc(v_ps.sem, 1)

            def ranks(b, first=False):
                pe.wait_ge(onehot.sem, onehot.at(b, 6))
                if not first:
                    pe.wait_ge(mx.sem, mx.at(b, 0))
                nc.tensor.matmul(SB[0][:, 0:(T + 1) * E], before[:, :], oh16[:, :, :].rearrange("p t e -> p (t e)"),
                                 start=True, stop=True)
                for t in range(T):
                    mm = nc.tensor.matmul(SB[0][:, (t + 1) * E:(T + 1) * E], ones16[:, :],
                                          oh16[:, t:t + 1, :].broadcast_to([P, T - t, E]), start=False, stop=True,
                                          skip_group_check=True)
                mm.then_inc(rank_ps.sem, 1)

            def sorted_transposes(b, i):
                if i % RUN == 0:
                    g = i // RUN
                    pe.wait_ge(xs_in[g % 2].sem, xs_in[g % 2].at(b, 16 * (g // 2 + 1)))
                if i >= 2:
                    pe.wait_ge(y_ev.sem, y_ev.at(b, i - 1))
                for c in range(DC):
                    mm = nc.tensor.transpose(TB[i % 2][:, c * P:c * P + P], xs[:, i % (2 * RUN), c * P:c * P + P], ident[:, :])
                mm.then_inc(xs_ps.sem, 1)

            def sorted_expert(b, i):
                if i == 0:
                    pe.wait_ge(route.sem, route.at(b, 12))
                    pe.sem_inc(passed, 1)
                e = nc.values_load(te[0:1, i:i + 1], engines=[mybir.EngineType.PE], min_val=0, max_val=E - 1,
                                   skip_runtime_bounds_check_because="it counts how many of E - 1 experts end before the tile")
                pe.wait_ge(xs_lo.sem, xs_lo.at(b, i + 1))
                we = [[w[:, c, bass.ds(e, 1), :] for c in range(DC)] for w in (ex_h, ex_l)]
                mm = triple(TB[i % 2][:, 0:D], [xs_h[:, i % 2, c, :] for c in range(DC)], [xs_l[:, i % 2, c, :] for c in range(DC)],
                            we[0], we[1], True, True)
                mm.then_inc(y_ps.sem, 1)

            def scores(b, j, first=False, half=None):
                g, t = divmod(j, T)
                if j == 0 and not half:
                    pe.wait_ge(route.sem, route.at(b, 6))
                    pe.wait_ge(stack.sem, stack.at(b, 16 * NSTACK))
                for pu in range(2) if half is None else (half,):
                    u = 2 * j + pu
                    if not first or u >= 2:
                        pe.wait_ge(mx.sem, mx.at(b, u - 1))
                    for i in range(2):
                        h = 4 * g + 2 * pu + i
                        for bl in range(2):
                            w0 = (2 * t + bl) * W
                            mm = nc.tensor.matmul(SB[u % 2][W * bl:W * bl + W, i * WIN:i * WIN + WIN],
                                                  q_s[:, h, W + w0:2 * W + w0], k_s[:, h // 2, w0:w0 + WIN],
                                                  start=True, stop=True)
                    mm.then_inc(S_ps.sem, 1)

            def max_cols(b, g):
                pe.wait_ge(mx.sem, mx.at(b, 2 * T * (g + 1)))
                nc.tensor.transpose(MB[g % 2][0:4 * T, 0:P], m_sb[:, 4 * g:4 * g + 4, :].rearrange("p h t -> p (h t)"),
                                    ident[:, :]).then_inc(mT_ps.sem, 1)

            def scores_t(b, k, pu):
                g, t = divmod(k, T)
                if k == 0 and pu == 0:
                    pe.wait_ge(y_ev.sem, y_ev.at(b, NT))
                if t == 0 and pu == 0:
                    pe.wait_ge(mrow.sem, mrow.at(b, 32 * (g + 1)))
                u = 2 * k + pu
                if u >= 2:
                    pe.wait_ge(ex_done.sem, ex_done.at(b, u - 1))
                for i in range(2):
                    h = 4 * g + 2 * pu + i
                    mm = nc.tensor.matmul(TB[u % 2][:, i * QW:i * QW + QW], k_s[:, h // 2, W + t * P:W + t * P + P],
                                          q_s[:, h, t * P:t * P + QW], start=True, stop=True)
                mm.then_inc(ST_ps.sem, 1)

            def values(b, k):
                g, t = divmod(k, T)
                shared = len([i for i in SHARED if i <= k])
                pe.wait_ge(masked.sem, masked.at(b, 2 * k + 2 - shared))
                if k in SHARED:
                    pe.sem_inc(passed, 1)
                    pe.wait_ge(masked_v.sem, masked_v.at(b, shared))
                if k == 0:
                    pe.wait_ge(v_ev.sem, v_ev.at(b, 2 * T))
                    pe.wait_ge(r2.sem, r2.at(b, 0))
                if t == 0 and g:
                    pe.wait_ge(oT_ev.sem, oT_ev.at(b, 2 * g - 1))
                if t == TH - 1 and g:
                    pe.wait_ge(oT_ev.sem, oT_ev.at(b, 2 * g))
                lo, hi = max(0, t * P - W), min(S, t * P + P + W)
                for hf in range(2):
                    a, z = max(lo, hf * HALF), min(hi, hf * HALF + HALF)
                    if a >= z:
                        continue
                    first = t == 0 if hf == 0 else t == TH - 1
                    last = t == TH if hf == 0 else t == T - 1
                    for hl in range(4):
                        q0 = a - (t * P - W)
                        mm = nc.tensor.matmul(OB[hf][32 * hl:32 * hl + 32, a - hf * HALF:z - hf * HALF],
                                              v_a[:, t, 4 * g + hl, :], prob[:, (k + 2) % 3, hl, q0:q0 + z - a],
                                              start=first, stop=last, skip_group_check=True)
                mm.then_inc(pv.sem, 1)

            def b_stage(b, last):
                for s in range(T + 4):
                    if s < T:
                        t = s
                        if t % TH == 0:
                            pe.wait_ge(oT_ev.sem, oT_ev.at(b, 2 * G - 1 + t // TH))
                        if t == 0:
                            if last:
                                pe.wait_ge(mT_ev.sem, mT_ev.at(b, G))
                            else:
                                pe.wait_ge(xT_l.sem, xT_l.at(b + 1, 4))
                        if t >= 2:
                            pe.wait_ge(att.sem, att.at(b, t - 1))
                        for g in range(G):
                            mm = nc.tensor.transpose(MB[t % 2][:, g * P:g * P + P], oT[:, g, t * P:t * P + P], ident[:, :])
                        mm.then_inc(t1_ps.sem, 1)
                    if 2 <= s < T + 2:
                        t = s - 2
                        pe.wait_ge(att.sem, att.at(b, t + 1))
                        if t >= 2:
                            pe.wait_ge(aT_ev.sem, aT_ev.at(b, t - 1))
                        for c in range(DC):
                            mm = nc.tensor.transpose(TB[t % 2][:, c * P:c * P + P], attn[:, t % 2, c * P:c * P + P], ident[:, :])
                        mm.then_inc(t2_ps.sem, 1)
                    if s >= 4:
                        t = s - 4
                        pe.wait_ge(aT_ev.sem, aT_ev.at(b, t + 1))
                        if t >= 2:
                            pe.wait_ge(r1.sem, r1.at(b, t - 1))
                        for c in range(DC):
                            mm = nc.tensor.matmul(OB[t % 2][:, 0:D], aT[:, t % 2, c, :], wo[:, c, :], start=(c == 0), stop=(c == DC - 1))
                        mm.then_inc(wo_ps.sem, 1)

            def n1_transposes(b, u, last=False):
                if u % DC == 0:
                    pe.wait_ge(n1_rdy.sem, n1_rdy.at(b, TH * (u // DC) + TH))
                if u >= 2:
                    pe.wait_ge(nT_l.sem, nT_l.at(b, u - 1))
                elif not last:
                    pe.wait_ge(qk_lo.sem, qk_lo.at(b + 1, 8))
                transposes(n1, u, nT_ps)

            def w1_unit(b, u, last):
                hf, f = divmod(u, FC)
                pe.wait_ge(nT_l.sem, nT_l.at(b, DC * hf + DC))
                if u >= 2:
                    pe.wait_ge(gel.sem, gel.at(b, u - 1))
                elif not last:
                    pe.wait_ge(v_ev.sem, v_ev.at(b + 1, 2 * (T - 1 + u)))
                s = slice(hf * HALF, hf * HALF + HALF)
                fs = slice(f * P, f * P + P)
                mm = triple(TB[u % 2][:, :], [w1_h[:, c, fs] for c in range(DC)], [w1_l[:, c, fs] for c in range(DC)],
                            [tr_h[:, c, s] for c in range(DC)], [tr_l[:, c, s] for c in range(DC)], True, True)
                mm.then_inc(u_ps.sem, 1)

            def w2_tile(b, t, last):
                hf = t // TH
                pe.wait_ge(g_lo.sem, g_lo.at(b, FC * (hf + 1)))
                if t >= 2:
                    pe.wait_ge(r2.sem, r2.at(b, t - 1))
                elif not last:
                    pe.wait_ge(v_ev.sem, v_ev.at(b + 1, 2 * T))
                dst = OB[t % 2][:, 0:D]
                s = slice(t % TH * P, t % TH * P + P)
                mm = triple(dst, [gH[hf][:, f, s] for f in range(FC)], [gL[hf][:, f, s] for f in range(FC)],
                            [w2_h[:, f] for f in range(FC)], [w2_l[:, f] for f in range(FC)], True, True)
                mm.then_inc(f_ps.sem, 1)

            def d_stage(b, last):
                for u in range(0 if last else 2, 4):
                    n1_transposes(b, u, last)
                for u in range(2 * FC):
                    w1_unit(b, u, last)
                    if u == 1 and not last:
                        ranks(b + 1)
                    if u in W1_STEPS and not last:
                        scores(b + 1, W1_STEPS.index(u))
                for t in range(T):
                    for i in tiles_at(t):
                        if not last:
                            if i == 0:
                                pe.wait_ge(gel.sem, gel.at(b, 2 * FC))
                            sorted_transposes(b + 1, i)
                    w2_tile(b, t, last)
                    for i in tiles_at(t):
                        if not last:
                            sorted_expert(b + 1, i)
                    if not last:
                        if t == 3:
                            max_cols(b + 1, 0)
                        scores(b + 1, LEAD - T + t)

            def turn(b, last):
                for k in range(STEPS + LAG):
                    if k % T == MAX_AT and k < 3 * T:
                        max_cols(b, k // T + 1)
                    for pu in range(2):
                        if k < STEPS:
                            scores_t(b, k, pu)
                        if 1 <= k and k - 1 + LEAD < STEPS:
                            scores(b, k - 1 + LEAD, half=pu)
                    if STEPS - 4 <= k < STEPS and not last:
                        xn_transposes(b + 1, k - (STEPS - 4))
                    if k >= LAG:
                        values(b, k - LAG)
                b_stage(b, last)
                if not last:
                    c2_stage(b + 1, False)
                d_stage(b, last)

            pe.wait_ge(pprep.sem, 3)
            for u in range(4):
                xn_transposes(0, u, first=True)
            pe.wait_ge(prep.sem, N_PREP_A)
            c2_stage(0, True)
            pe.wait_ge(qk_lo.sem, qk_lo.at(0, 8))
            b1_w1()
            pe.wait_ge(pprep.sem, N_PPREP)
            ranks(0, first=True)
            pe.wait_ge(prep.sem, N_PREP_EX)
            for j in range(LEAD - T):
                scores(0, j, first=True)
            for t in range(T):
                for i in tiles_at(t):
                    sorted_transposes(0, i)
                if t == 3:
                    max_cols(0, 0)
                scores(0, LEAD - T + t, first=True)
                for i in tiles_at(t):
                    sorted_expert(0, i)
            pe.wait_ge(prep.sem, N_PREP)
            with pe.Fori(0, NB - 1) as b:
                turn(b, False)
            turn(NB - 1, True)


N_WA, N_WB = 8, 13
N_PPREP_V, N_PPREP = 6, 25
N_PREP_Z, N_PREP_A, N_PREP_W1, N_PREP_EX, N_PREP_D, N_PREP = 2, 9, 12, 14, 15, 31

_INS = ["L0_attn_x", "L0_attn_Wq", "L0_attn_bq", "L0_attn_Wk", "L0_attn_bk", "L0_attn_Wv", "L0_attn_bv", "L0_attn_Wo",
        "L0_attn_bo", "L0_attn_g1", "L0_attn_b1", "L0_attn_W1", "L0_attn_c1", "L0_attn_W2", "L0_attn_c2",
        "L0_attn_g2", "L0_attn_b2", "L0_ffn_gate_w", "L0_ffn_expert_w"]


def kernel(**inputs):
    import numpy as _np
    import concourse.bacc as _bacc
    from concourse import mybir as _mybir
    from concourse.bass_utils import run_bass_kernel_spmd as _run

    nc = _bacc.Bacc("TRN2", target_bir_lowering=False, num_devices=1)
    arrays, args = {}, []

    def add(name, a):
        a = _np.ascontiguousarray(a)
        arrays[f"in_{name}"] = a
        args.append(nc.dram_tensor(f"in_{name}", a.shape, _mybir.dt.from_np(a.dtype), kind="ExternalInput").ap())

    for name in _INS:
        a = _np.asarray(inputs[name])
        if name == "L0_ffn_gate_w":
            a = a.T
        if name == "L0_ffn_expert_w":
            a = a.transpose(0, 2, 1)
        if name[8:] in ("bq", "bk", "g1", "c1"):
            a = a.reshape(-1, P).T
        add(name, a)
    add("b1_by_partition", _np.asarray(inputs["L0_attn_b1"]).reshape(-1, P).T)
    add("g1_row", _np.asarray(inputs["L0_attn_g1"]))
    shape = inputs["L0_attn_x"].shape
    args.append(nc.dram_tensor("out_0", shape, _mybir.dt.float32, kind="ExternalOutput").ap())
    build(nc, *args)
    r = _run(nc, [arrays], core_ids=[0])
    return r.results[0]["out_0"]
```
